# Optimizing a Trainium2 kernel written in Bass

```python
import numpy as np
import jax
import jax.numpy as jnp

def _softmax(x, axis=-1):
    return jax.nn.softmax(x, axis=axis)

def _gelu(x):
    return jax.nn.gelu(x, approximate=True)

def _silu(x):
    return jax.nn.silu(x)

def _sigmoid(x):
    return jax.nn.sigmoid(x)

def _layernorm(x, axis=-1, eps=1e-05):
    m = jnp.mean(x, axis=axis, keepdims=True)
    v = jnp.var(x, axis=axis, keepdims=True)
    return (x - m) / jnp.sqrt(v + eps)

def _scatter_add(tgt, idx, src, axis=0):
    return tgt.at[idx].add(src)

def _segment_sum(src, seg, n):
    return jax.ops.segment_sum(src, seg, n)
kernel_name = 'mk_xattn_ffn_d2_seqx_r4_3d6e2e'

def setup_inputs(seed: int=0):
    np.random.seed(seed)
    _w = jnp.asarray

    def _rec_inputs():
        import jax
        import jax.numpy as jnp
        _rk = jax.random.key(seed)
        x = -0.0001231 + 1 * jax.random.normal(jax.random.fold_in(_rk, 1), (16, 256, 256), jnp.float32)
        _lenS = 256 - jax.random.randint(jax.random.fold_in(_rk, 7), (16,), 0, max(1, 256 // 4) + 1, jnp.int32)
        _lenS2 = 256 - jax.random.randint(jax.random.fold_in(_rk, 8), (16,), 0, max(1, 256 // 4) + 1, jnp.int32)
        _ctx_1024P = jax.random.normal(jax.random.fold_in(_rk, 11), (16, 16, 256), jnp.float32)
        _ctx_1024c = jax.random.dirichlet(jax.random.fold_in(_rk, 511), 0.3 * jnp.ones((16,), jnp.float32), (16, 256))
        _ctx_1024t = jnp.einsum('bsk,bkd->bsd', _ctx_1024c, _ctx_1024P)
        _ctx_1024t = _ctx_1024t * jax.lax.rsqrt(jnp.mean(jnp.square(_ctx_1024t)) + 1e-12) * 0.953939
        ctx_1024 = -0.000137203 + 0.999727 * (_ctx_1024t + 0.3 * jax.random.normal(jax.random.fold_in(_rk, 611), (16, 256, 256), jnp.float32))
        _validS = jnp.arange(256)[None, :] < _lenS[:, None]
        _validS2 = jnp.arange(256)[None, :] < _lenS2[:, None]
        _causal = jnp.tril(jnp.ones((256, 256), dtype=bool))
        mask_SxS2_ik1 = jnp.where(jnp.broadcast_to(_validS2[0:1, :], (256, 256)), 1, 0).astype(jnp.int32)
        return (x, ctx_1024, mask_SxS2_ik1)
    x, ctx_1024, mask_SxS2_ik1 = _rec_inputs()

    def _L0_xattn_setup():
        import jax, jax.numpy as jnp
        import numpy as np
        B, S, HID, NH, K = (4, 375, 256, 16, 64)
        DH = HID // NH

        def _rel_bias(pos_emb, length):
            kk = (pos_emb.shape[0] - 1) // 2
            idx = jnp.arange(length)
            dist = jnp.clip(idx[None, :] - idx[:, None], -kk, kk) + kk
            return pos_emb[dist]
        key = jax.random.key(seed)
        ks = jax.random.split(key, 12)
        sq = 1.0 / np.sqrt(HID)
        inp = {'query': jax.random.normal(ks[0], (B, S, HID), jnp.float32), 'key': jax.random.normal(ks[1], (B, S, HID), jnp.float32), 'value': jax.random.normal(ks[2], (B, S, HID), jnp.float32), 'Wq': jax.random.normal(ks[3], (NH, HID, DH), jnp.float32) * sq, 'bq': jnp.zeros((NH, DH), jnp.float32), 'Wk': jax.random.normal(ks[4], (NH, HID, DH), jnp.float32) * sq, 'bk': jnp.zeros((NH, DH), jnp.float32), 'Wv': jax.random.normal(ks[5], (NH, HID, DH), jnp.float32) * sq, 'bv': jnp.zeros((NH, DH), jnp.float32), 'pos_k': jax.random.normal(ks[6], (2 * K + 1, DH), jnp.float32) * 0.1, 'pos_v': jax.random.normal(ks[7], (2 * K + 1, DH), jnp.float32) * 0.1, 'W_fc': jax.random.normal(ks[8], (HID, HID), jnp.float32) * sq, 'b_fc': jnp.zeros((HID,), jnp.float32)}
        return inp
    _L0_xattn_all = _L0_xattn_setup()
    _L0_xattn_in = {k: v for k, v in _L0_xattn_all.items() if k in ('Wq', 'bq', 'Wk', 'bk', 'Wv', 'bv', 'pos_k', 'pos_v', 'W_fc', 'b_fc')}
    del _L0_xattn_all

    def _L0_ffn_setup():
        import jax, jax.numpy as jnp
        import numpy as np
        BLOCK = 32
        W_BITS = 4
        ACT_BITS = 16

        def act_qdq(x):
            qmax = 2.0 ** (ACT_BITS - 1) - 1.0
            scale = jnp.maximum(jnp.max(jnp.abs(x)) / qmax, 1e-12)
            return jnp.clip(jnp.round(x / scale), -qmax - 1.0, qmax) * scale

        def fixed_qdq_u16(x):
            scale = 1.0 / 65536.0
            return jnp.clip(jnp.round(x / scale), 0.0, 65535.0) * scale

        def lpbq_dequant(w):
            O, I = w.shape
            qmax = 2.0 ** (W_BITS - 1) - 1.0
            wb = w.reshape(O, I // BLOCK, BLOCK)
            s = jnp.maximum(jnp.max(jnp.abs(wb), axis=-1, keepdims=True) / qmax, 1e-12)
            wq = jnp.clip(jnp.round(wb / s), -qmax - 1.0, qmax) * s
            return wq.reshape(O, I)
        key = jax.random.key(seed)
        k1, k2, k3, k4 = jax.random.split(key, 4)
        B, S, H, I = (2, 1024, 256, 768)
        x = jax.random.normal(k1, (B, S, H), jnp.float32)
        w_gate = jax.random.normal(k2, (I, H), jnp.float32) * 0.02
        w_up = jax.random.normal(k3, (I, H), jnp.float32) * 0.02
        w_down = jax.random.normal(k4, (H, I), jnp.float32) * 0.02
        return {'x': x, 'w_gate': w_gate, 'w_up': w_up, 'w_down': w_down}
    _L0_ffn_all = _L0_ffn_setup()
    _L0_ffn_in = {k: v for k, v in _L0_ffn_all.items() if k in ('w_gate', 'w_up', 'w_down')}
    del _L0_ffn_all

    def _L1_xattn_setup():
        import jax, jax.numpy as jnp
        import numpy as np
        B, QS, KVS = (2, 512, 512)
        Q_DIM = KV_DIM = E = 256
        H = 16
        HD = E // H
        SCALE = 1.0 / np.sqrt(HD).astype(np.float32)
        key = jax.random.key(seed)
        ks = jax.random.split(key, 8)
        return {'v_in': jax.random.normal(ks[0], (B, KVS, KV_DIM), jnp.float32), 'k_in': jax.random.normal(ks[1], (B, KVS, KV_DIM), jnp.float32), 'q_in': jax.random.normal(ks[2], (B, QS, Q_DIM), jnp.float32), 'mask': jax.random.randint(ks[3], (QS, KVS), 0, 2, jnp.int32), 'Wv': jax.random.normal(ks[4], (E, KV_DIM), jnp.float32) / np.sqrt(KV_DIM), 'Wk': jax.random.normal(ks[5], (E, KV_DIM), jnp.float32) / np.sqrt(KV_DIM), 'Wq': jax.random.normal(ks[6], (E, Q_DIM), jnp.float32) / np.sqrt(Q_DIM), 'Wout': jax.random.normal(ks[7], (Q_DIM, E), jnp.float32) / np.sqrt(E)}
    _L1_xattn_all = _L1_xattn_setup()
    _L1_xattn_in = {k: v for k, v in _L1_xattn_all.items() if k in ('Wv', 'Wk', 'Wq', 'Wout')}
    del _L1_xattn_all

    def _L1_ffn_setup():
        import jax, jax.numpy as jnp
        import numpy as np
        HIDDEN_SIZE = 256
        NUM_EXPERTS = 8
        MOE_INTERMEDIATE_SIZE = 352
        NUM_EXPERTS_PER_TOK = 2
        SHARED_EXPERT_INTERMEDIATE_SIZE = 704
        B, T = (2, 256)
        W_SCALE = 0.02
        key = jax.random.key(seed)
        ks = jax.random.split(key, 8)
        H, E, I, SI = (HIDDEN_SIZE, NUM_EXPERTS, MOE_INTERMEDIATE_SIZE, SHARED_EXPERT_INTERMEDIATE_SIZE)
        return {'x': jax.random.normal(ks[0], (B, T, H), jnp.float32), 'gate_w': jax.random.normal(ks[1], (E, H), jnp.float32) * W_SCALE, 'experts_gate_up': jax.random.normal(ks[2], (E, 2 * I, H), jnp.float32) * W_SCALE, 'experts_down': jax.random.normal(ks[3], (E, H, I), jnp.float32) * W_SCALE, 'shared_gate_w': jax.random.normal(ks[4], (SI, H), jnp.float32) * W_SCALE, 'shared_up_w': jax.random.normal(ks[5], (SI, H), jnp.float32) * W_SCALE, 'shared_down_w': jax.random.normal(ks[6], (H, SI), jnp.float32) * W_SCALE, 'shared_expert_gate_w': jax.random.normal(ks[7], (1, H), jnp.float32) * W_SCALE}
    _L1_ffn_all = _L1_ffn_setup()
    _L1_ffn_in = {k: v for k, v in _L1_ffn_all.items() if k in ('gate_w', 'experts_gate_up', 'experts_down', 'shared_gate_w', 'shared_up_w', 'shared_down_w', 'shared_expert_gate_w')}
    del _L1_ffn_all
    return {'x': x, 'ctx_1024': ctx_1024, 'mask_SxS2_ik1': mask_SxS2_ik1, 'L0_xattn_Wq': _L0_xattn_in['Wq'], 'L0_xattn_bq': _L0_xattn_in['bq'], 'L0_xattn_Wk': _L0_xattn_in['Wk'], 'L0_xattn_bk': _L0_xattn_in['bk'], 'L0_xattn_Wv': _L0_xattn_in['Wv'], 'L0_xattn_bv': _L0_xattn_in['bv'], 'L0_xattn_pos_k': _L0_xattn_in['pos_k'], 'L0_xattn_pos_v': _L0_xattn_in['pos_v'], 'L0_xattn_W_fc': _L0_xattn_in['W_fc'], 'L0_xattn_b_fc': _L0_xattn_in['b_fc'], 'L0_ffn_w_gate': _L0_ffn_in['w_gate'], 'L0_ffn_w_up': _L0_ffn_in['w_up'], 'L0_ffn_w_down': _L0_ffn_in['w_down'], 'L1_xattn_Wv': _L1_xattn_in['Wv'], 'L1_xattn_Wk': _L1_xattn_in['Wk'], 'L1_xattn_Wq': _L1_xattn_in['Wq'], 'L1_xattn_Wout': _L1_xattn_in['Wout'], 'L1_ffn_gate_w': _L1_ffn_in['gate_w'], 'L1_ffn_experts_gate_up': _L1_ffn_in['experts_gate_up'], 'L1_ffn_experts_down': _L1_ffn_in['experts_down'], 'L1_ffn_shared_gate_w': _L1_ffn_in['shared_gate_w'], 'L1_ffn_shared_up_w': _L1_ffn_in['shared_up_w'], 'L1_ffn_shared_down_w': _L1_ffn_in['shared_down_w'], 'L1_ffn_shared_expert_gate_w': _L1_ffn_in['shared_expert_gate_w']}

def reference(x, ctx_1024, mask_SxS2_ik1, L0_xattn_Wq, L0_xattn_bq, L0_xattn_Wk, L0_xattn_bk, L0_xattn_Wv, L0_xattn_bv, L0_xattn_pos_k, L0_xattn_pos_v, L0_xattn_W_fc, L0_xattn_b_fc, L0_ffn_w_gate, L0_ffn_w_up, L0_ffn_w_down, L1_xattn_Wv, L1_xattn_Wk, L1_xattn_Wq, L1_xattn_Wout, L1_ffn_gate_w, L1_ffn_experts_gate_up, L1_ffn_experts_down, L1_ffn_shared_gate_w, L1_ffn_shared_up_w, L1_ffn_shared_down_w, L1_ffn_shared_expert_gate_w):
    import jax
    import jax.numpy as jnp

    def _L0_xattn_ref(query, key, value, Wq, bq, Wk, bk, Wv, bv, pos_k, pos_v, W_fc, b_fc):
        import jax, jax.numpy as jnp
        import numpy as np
        B, S, HID, NH, K = (4, 375, 256, 16, 64)
        DH = HID // NH

        def _rel_bias(pos_emb, length):
            kk = (pos_emb.shape[0] - 1) // 2
            idx = jnp.arange(length)
            dist = jnp.clip(idx[None, :] - idx[:, None], -kk, kk) + kk
            return pos_emb[dist]
        seq = query.shape[1]
        k_bias = _rel_bias(pos_k, seq)
        v_bias = _rel_bias(pos_v, seq)
        q = jnp.einsum('bsh,nhd->bnsd', query, Wq) + bq[None, :, None, :]
        k = jnp.einsum('bsh,nhd->bnsd', key, Wk) + bk[None, :, None, :]
        v = jnp.einsum('bsh,nhd->bnsd', value, Wv) + bv[None, :, None, :]
        attn_1 = jnp.einsum('bnqd,bnkd->bnqk', q, k)
        attn_2 = jnp.einsum('bnqd,qkd->bnqk', q, k_bias)
        scores = (attn_1 + attn_2) / jnp.sqrt(jnp.float32(DH))
        w = jax.nn.softmax(scores, axis=-1)
        values_1 = jnp.einsum('bnqk,bnkd->bnqd', w, v)
        values_2 = jnp.einsum('bnqk,qkd->bnqd', w, v_bias)
        heads = values_1 + values_2
        hidden = jnp.transpose(heads, (0, 2, 1, 3)).reshape(query.shape[0], seq, -1)
        return hidden @ W_fc + b_fc

    def _L0_ffn_ref(x, w_gate, w_up, w_down):
        import jax, jax.numpy as jnp
        import numpy as np
        BLOCK = 32
        W_BITS = 4
        ACT_BITS = 16

        def act_qdq(x):
            qmax = 2.0 ** (ACT_BITS - 1) - 1.0
            scale = jnp.maximum(jnp.max(jnp.abs(x)) / qmax, 1e-12)
            return jnp.clip(jnp.round(x / scale), -qmax - 1.0, qmax) * scale

        def fixed_qdq_u16(x):
            scale = 1.0 / 65536.0
            return jnp.clip(jnp.round(x / scale), 0.0, 65535.0) * scale

        def lpbq_dequant(w):
            O, I = w.shape
            qmax = 2.0 ** (W_BITS - 1) - 1.0
            wb = w.reshape(O, I // BLOCK, BLOCK)
            s = jnp.maximum(jnp.max(jnp.abs(wb), axis=-1, keepdims=True) / qmax, 1e-12)
            wq = jnp.clip(jnp.round(wb / s), -qmax - 1.0, qmax) * s
            return wq.reshape(O, I)
        x = act_qdq(x)
        up = act_qdq(x @ lpbq_dequant(w_up).T)
        gate = act_qdq(x @ lpbq_dequant(w_gate).T)
        sig = fixed_qdq_u16(jax.nn.sigmoid(gate))
        gate = act_qdq(gate * sig)
        o = act_qdq(gate * up)
        return o @ lpbq_dequant(w_down).T

    def _L1_xattn_ref(v_in, k_in, q_in, mask, Wv, Wk, Wq, Wout):
        import jax, jax.numpy as jnp
        import numpy as np
        B, QS, KVS = (2, 512, 512)
        Q_DIM = KV_DIM = E = 256
        H = 16
        HD = E // H
        SCALE = 1.0 / np.sqrt(HD).astype(np.float32)
        b, kv_s, _ = v_in.shape
        _, q_s, _ = q_in.shape
        V = v_in @ Wv.T
        K = k_in @ Wk.T
        Q = q_in @ Wq.T
        Vh = V.reshape(b, kv_s, H, HD).transpose(0, 2, 1, 3)
        Kh = K.reshape(b, kv_s, H, HD).transpose(0, 2, 1, 3)
        Qh = Q.reshape(b, q_s, H, HD).transpose(0, 2, 1, 3)
        scores = jnp.einsum('bhqd,bhkd->bhqk', Qh, Kh) * SCALE
        scores = jnp.where(mask == 0, jnp.float32(1e-20), scores)
        A = jax.nn.softmax(scores, axis=-1)
        out = jnp.einsum('bhqk,bhkd->bhqd', A, Vh)
        out = out.transpose(0, 2, 1, 3).reshape(b, q_s, H * HD)
        return out @ Wout.T

    def _L1_ffn_ref(x, gate_w, experts_gate_up, experts_down, shared_gate_w, shared_up_w, shared_down_w, shared_expert_gate_w):
        import jax, jax.numpy as jnp
        import numpy as np
        HIDDEN_SIZE = 256
        NUM_EXPERTS = 8
        MOE_INTERMEDIATE_SIZE = 352
        NUM_EXPERTS_PER_TOK = 2
        SHARED_EXPERT_INTERMEDIATE_SIZE = 704
        B, T = (2, 256)
        W_SCALE = 0.02
        Bx, Tx, H = x.shape
        E = gate_w.shape[0]
        I = experts_down.shape[2]
        x_flat = x.reshape(Bx * Tx, H)
        logits = x_flat @ gate_w.T
        scores = jax.nn.softmax(logits, axis=-1)
        _, topk_ids = jax.lax.top_k(scores, NUM_EXPERTS_PER_TOK)
        in_topk = jax.nn.one_hot(topk_ids, E, dtype=x.dtype).sum(axis=1)
        w = scores * in_topk
        gu = jnp.einsum('nh,eih->nei', x_flat, experts_gate_up)
        g, u = (gu[..., :I], gu[..., I:])
        h = jax.nn.silu(g) * u
        expert_out = jnp.einsum('nei,ehi->neh', h, experts_down)
        out = jnp.einsum('neh,ne->nh', expert_out, w)
        shared = jax.nn.silu(x_flat @ shared_gate_w.T) * (x_flat @ shared_up_w.T) @ shared_down_w.T
        shared_weight = jax.nn.sigmoid(x_flat @ shared_expert_gate_w.T)
        out = out + shared_weight * shared
        return out.reshape(Bx, Tx, H)
    x = x + _L0_xattn_ref(_layernorm(x, axis=-1), ctx_1024, ctx_1024, L0_xattn_Wq, L0_xattn_bq, L0_xattn_Wk, L0_xattn_bk, L0_xattn_Wv, L0_xattn_bv, L0_xattn_pos_k, L0_xattn_pos_v, L0_xattn_W_fc, L0_xattn_b_fc)
    x = x + _L0_ffn_ref(_layernorm(x, axis=-1), L0_ffn_w_gate, L0_ffn_w_up, L0_ffn_w_down)
    x = x + _L1_xattn_ref(ctx_1024, ctx_1024, _layernorm(x, axis=-1), mask_SxS2_ik1, L1_xattn_Wv, L1_xattn_Wk, L1_xattn_Wq, L1_xattn_Wout)
    x = x + _L1_ffn_ref(_layernorm(x, axis=-1), L1_ffn_gate_w, L1_ffn_experts_gate_up, L1_ffn_experts_down, L1_ffn_shared_gate_w, L1_ffn_shared_up_w, L1_ffn_shared_down_w, L1_ffn_shared_expert_gate_w)
    return x

_drawn_inputs = setup_inputs


def setup_inputs(seed=0):
    import zlib

    import numpy as np

    out = dict(_drawn_inputs(seed))
    spreads = {'L0_xattn_bq': (0.0, 0.429),
     'L0_xattn_bk': (0.0, 0.8),
     'L0_xattn_bv': (0.0, 0.1),
     'L0_xattn_b_fc': (0.0, 0.1)}
    factors = {'L0_xattn_pos_k': 8.0,
     'L1_ffn_gate_w': 8.0,
     'L1_ffn_experts_gate_up': 8.0,
     'L1_ffn_experts_down': 8.0,
     'L1_ffn_shared_gate_w': 4.987,
     'L1_ffn_shared_up_w': 4.898,
     'L1_ffn_shared_down_w': 4.911,
     'L1_ffn_shared_expert_gate_w': 8.0}
    for name, (base, spread) in spreads.items():
        noise = np.random.default_rng([zlib.crc32(name.encode()), seed]).standard_normal(out[name].shape)
        drawn = base * np.exp(spread * noise) if base else spread * noise
        out[name] = jnp.asarray(drawn.astype(out[name].dtype))
    for name, factor in factors.items():
        out[name] = (out[name] * factor).astype(out[name].dtype)
    return out
```

```python
from contextlib import ExitStack

import concourse.bass as bass
from concourse import mybir

ALU = mybir.AluOpType
ACT = mybir.ActivationFunctionType
F32 = mybir.dt.float32
F16 = mybir.dt.float16
I32 = mybir.dt.int32
X = mybir.AxisListType.X
ABSMAX = bass.bass_isa.ReduceOp.absmax

P = 128
B, S, D = 16, 256, 256
H, DH = 16, 16
K = 64
KT = D // P
NT = B * S // P
SC = 512
NS = B * S // SC
TS = SC // P
EPS = 1e-5
SCALE = DH ** -0.5
MASKED = 1e-20
IN = 8
GN = S // IN
GC = 4
NC = GN // GC
NB2 = 2 * NC
QBLOCK = 32
W_QMAX = 7.0
QMAX = 32767.0
SIG_STEPS = 65536.0
TINY = 1e-12
MAGIC = 1.5 * 2.0 ** 23
X_STEP, X_BY, GATE_STEP, GATE_BY, UP_STEP, UP_BY, GATED_STEP, GATED_BY, PROD_STEP, OUT_STEP, OUT_BY = range(11)
ENGINES = 5
HI, LO = 0, 1
SPLIT = ((HI, HI), (HI, LO), (LO, HI))
W_UP = 64.0


def tokens(ap):
    return ap.rearrange("b s d -> (b s) d").rearrange("(t p) d -> p t d", p=P)


def build(nc, a, out):
    with ExitStack() as ctx:
        def sb(name, shape, dt=F32, stack=ctx):
            return stack.enter_context(nc.sbuf_tensor(name, shape, dt))

        semaphores = {}

        def sem(name):
            if name not in semaphores:
                semaphores[name] = ctx.enter_context(nc.semaphore(name))
            return semaphores[name]

        def dram(name, shape):
            return nc.dram_tensor(name, shape, F32, kind="Internal").ap()

        x_sb = sb("x_sb", [P, NT, D])
        ident = sb("ident", [P, P])
        block = sb("block16", [P, 8])
        block_rev = sb("block16_rev", [P, 8])
        stats = sb("stats", [P, NT, 6])
        mv = sb("mv", [P, NT, 2])
        sd = sb("sd", [P, NT])
        rstd = sb("rstd", [P, NT])
        eps = sb("eps", [P, 1])
        psum = ctx.enter_context(nc.psum_tensor("psum", [P, 8, 512], F32))

        q_dr = dram("q_dr", [B, H * DH, S])
        k_dr = dram("k_dr", [B, H * DH, S])
        v_dr = dram("v_dr", [B * S, H * DH])
        h_dr = dram("h_dr", [B, H * DH, S])
        r_dr = dram("r_dr", [B, H * DH, S])
        extv_dr = dram("extv_dr", [2 * S, DH])

        phase_end = sem("phase_end")
        x_loaded = sem("x_loaded")
        consts_set = sem("consts_set")
        out_stored = sem("out_stored")

        def phase_barrier(eng, k):
            eng.drain().then_inc(phase_end, 1)
            eng.wait_ge(phase_end, ENGINES * (k + 1))

        apart = {}

        def wait_apart(eng, semaphore, value):
            if eng not in apart:
                apart[eng] = sem(f"apart_{len(apart)}")
            eng.wait_ge(semaphore, value)
            eng.sem_inc(apart[eng], 1)

        def norm_stats(n):
            stats_done, mv_done = sem(f"stats_done{n}"), sem(f"mv_done{n}")
            sd_done, rstd_done = sem(f"sd_done{n}"), sem(f"rstd_done{n}")

            def vector(dve):
                with dve.Fori(0, NT // 4, 1) as t:
                    for j in range(4):
                        ins = nc.vector.bn_stats(stats[:, t * 4 + j, :], x_sb[:, t * 4 + j, :])
                    ins.then_inc(stats_done, 1)
                dve.wait_ge(stats_done, NT // 4)
                for t in range(NT):
                    ins = nc.vector.bn_aggr(mv[:, t, :], stats[:, t, :])
                ins.then_inc(mv_done, 1)
                dve.wait_ge(sd_done, 1)
                nc.vector.reciprocal(rstd[:, :], sd[:, :]).then_inc(rstd_done, 1)
                dve.wait_ge(rstd_done, 1)

            def scalar(act):
                act.wait_ge(mv_done, 1)
                nc.scalar.activation(sd[:, :], mv[:, :, 1], ACT.Sqrt, bias=eps[:, 0:1]).then_inc(sd_done, 1)

            return vector, scalar

        def projections(n, wq_ap, wk_ap, wv_ap, bq_ap=None, bk_ap=None, bv_ap=None):
            biased = bq_ap is not None
            xn_ready, ctx_loaded, w_loaded = sem("xn_ready"), sem("ctx_loaded"), sem("w_loaded")
            xt_ps, ct_ps, xt_sb, ct_sb = sem("xt_ps"), sem("ct_ps"), sem("xt_sb"), sem("ct_sb")
            q_ps, k_ps, v_ps = sem("q_ps"), sem("k_ps"), sem("v_ps")
            q_out, k_out, v_out = sem("q_out"), sem("k_out"), sem("v_out")
            q_stored, k_stored, v_stored = sem("q_stored"), sem("k_stored"), sem("v_stored")
            w_ps, w_sb_done, bq_scaled = sem("w_ps"), sem("w_sb_done"), sem("bq_scaled")
            n_w = 9 if biased else 3

            def alloc(stack):
                t = {}
                for name, shape in (("w", [P, 3, KT, D]), ("w_raw", [P, 3, KT, D]), ("bqk", [P, 2, 2]),
                                    ("bv", [P, D]), ("xn", [P, TS, D]), ("cin", [P, TS, D]),
                                    ("xt", [P, KT, SC]), ("ct", [P, KT, SC]), ("qo", [P, 2, SC]),
                                    ("ko", [P, 2, SC]), ("vo", [P, TS, D])):
                    t[name] = sb(f"{name}{n}", shape, stack=stack)
                return t

            def sync(sp, t):
                if biased:
                    for i, w in enumerate((wq_ap, wk_ap, wv_ap)):
                        for kt in range(KT):
                            sp.dma_start(t["w"][:, i, kt, :].rearrange("p (h d) -> p h d", h=H),
                                         w[:, kt * P:(kt + 1) * P, :].rearrange("h p d -> p h d")
                                         ).then_inc(w_loaded, 16)
                    for i, v in enumerate((bq_ap, bk_ap)):
                        sp.dma_start(t["bqk"][:, i, :], v.rearrange("(t h) d -> (h d) t", t=2),
                                     allow_slow_non_contiguous=True).then_inc(w_loaded, 16)
                    sp.dma_start(t["bv"][:, :], bv_ap.rearrange("h d -> (h d)").partition_broadcast(P)
                                 ).then_inc(w_loaded, 16)
                else:
                    for i, w in enumerate((wq_ap, wk_ap, wv_ap)):
                        sp.dma_start(t["w_raw"][:, i, :, :],
                                     w.rearrange("(t p) n -> p t n", p=P)).then_inc(w_loaded, 16)
                ctx_t = tokens(a["ctx_1024"])
                for granted in (q_stored, k_stored, v_stored):
                    sp.sem_inc(granted, 16)
                q_t = q_dr.rearrange("b (t p) s -> p t b s", p=P)
                k_t = k_dr.rearrange("b (t p) s -> p t b s", p=P)
                v_t = v_dr.rearrange("(t p) d -> p t d", p=P)
                sp.dma_start(t["cin"][:, :, :], ctx_t[:, 0:TS, :]).then_inc(ctx_loaded, 16)
                with sp.Fori(0, NS, 1) as s:
                    sp.wait_ge(ct_ps, s + 1)
                    nxt = (s + 1) % NS
                    sp.dma_start(t["cin"][:, :, :], ctx_t[:, bass.ds(nxt * TS, TS), :]).then_inc(ctx_loaded, 16)
                    sp.wait_ge(q_out, s + 1)
                    for hh in range(2):
                        sp.dma_start(q_t[:, hh, bass.ds(2 * s, 2), :],
                                     t["qo"][:, hh, :].rearrange("p (b s) -> p b s", b=2)).then_inc(q_stored, 16)
                    sp.wait_ge(v_out, s + 2)
                    sp.dma_start(v_t[:, bass.ds(s * TS, TS), :], t["vo"][:, :, :]).then_inc(v_stored, 16)
                    sp.wait_ge(k_out, s + 2)
                    for hh in range(2):
                        sp.dma_start(k_t[:, hh, bass.ds(2 * s, 2), :],
                                     t["ko"][:, hh, :].rearrange("p (b s) -> p b s", b=2)).then_inc(k_stored, 16)
                sp.wait_ge(q_stored, 32 * NS + 16)
                sp.wait_ge(k_stored, 32 * NS + 16)
                sp.wait_ge(v_stored, 16 * NS + 16)
                sp.wait_ge(ctx_loaded, 16 * (NS + 1))

            def tensor(pe, t):
                def feature_major(which, src):
                    for hh in range(2):
                        for kt in range(KT):
                            ins = nc.tensor.matmul(psum[:, 4 + hh, :], t["w"][:, which, kt, hh * P:(hh + 1) * P],
                                                   src[:, kt, :], start=(kt == 0), stop=(kt == KT - 1))
                    return ins

                pe.wait_ge(w_loaded, 16 * n_w)
                if not biased:
                    for i in range(3):
                        for ot in range(2):
                            for kt in range(KT):
                                ins = nc.tensor.transpose(psum[:, i * 2 + kt, ot * P:(ot + 1) * P],
                                                          t["w_raw"][:, i, ot, kt * P:(kt + 1) * P], ident[:, :])
                    ins.then_inc(w_ps, 1)
                    pe.wait_ge(w_sb_done, 1)
                for granted in (xt_ps, q_ps, k_ps):
                    pe.sem_inc(granted, 1)
                with pe.Fori(0, NS, 1) as s:
                    pe.wait_ge(xn_ready, s + 1)
                    for kt in range(KT):
                        for j in range(TS):
                            ins = nc.tensor.transpose(psum[:, kt, j * P:(j + 1) * P],
                                                      t["xn"][:, j, kt * P:(kt + 1) * P], ident[:, :])
                    ins.then_inc(xt_ps, 1)
                    pe.wait_ge(ctx_loaded, 16 * (s + 1))
                    for kt in range(KT):
                        for j in range(TS):
                            ins = nc.tensor.transpose(psum[:, 2 + kt, j * P:(j + 1) * P],
                                                      t["cin"][:, j, kt * P:(kt + 1) * P], ident[:, :])
                    ins.then_inc(ct_ps, 1)
                    pe.wait_ge(xt_sb, s + 1)
                    pe.wait_ge(k_out, s + 1)
                    feature_major(0, t["xt"]).then_inc(q_ps, 1)
                    pe.wait_ge(ct_sb, s + 1)
                    pe.wait_ge(v_out, s + 1)
                    for j in range(TS):
                        for kt in range(KT):
                            ins = nc.tensor.matmul(psum[:, 6 + j // 2, (j % 2) * D:(j % 2 + 1) * D],
                                                   t["ct"][:, kt, j * P:(j + 1) * P], t["w"][:, 2, kt, :],
                                                   start=(kt == 0), stop=(kt == KT - 1))
                    ins.then_inc(v_ps, 1)
                    pe.wait_ge(q_out, s + 1)
                    feature_major(1, t["ct"]).then_inc(k_ps, 1)

            def scalar(act, t):
                if biased:
                    act.wait_ge(w_loaded, 16 * n_w)
                    nc.scalar.mul(t["bqk"][:, 0, :], t["bqk"][:, 0, :], SCALE).then_inc(bq_scaled, 1)
                    act.wait_ge(bq_scaled, 1)
                with act.Fori(0, NS, 1) as s:
                    act.wait_ge(xt_ps, s + 2)
                    act.wait_ge(q_ps, s + 1)
                    nc.scalar.copy(t["xt"][:, :, :], psum[:, 0:2, :]).then_inc(xt_sb, 1)
                    act.wait_ge(q_ps, s + 2)
                    act.wait_ge(q_stored, 32 * s + 16)
                    for hh in range(2):
                        if biased:
                            ins = nc.scalar.activation(t["qo"][:, hh, :], psum[:, 4 + hh, :], ACT.Identity,
                                                       bias=t["bqk"][:, 0, hh:hh + 1], scale=SCALE)
                        else:
                            ins = nc.scalar.mul(t["qo"][:, hh, :], psum[:, 4 + hh, :], SCALE)
                    ins.then_inc(q_out, 1)

            def vector(dve, t):
                if not biased:
                    dve.wait_ge(w_ps, 1)
                    ins = nc.vector.tensor_copy(t["w"][:, :, :, :].rearrange("p i k n -> p (i k) n"),
                                                psum[:, 0:6, 0:D])
                    ins.then_inc(w_sb_done, 1)
                else:
                    dve.wait_ge(w_loaded, 16 * n_w)
                dve.sem_inc(k_out, 1)
                dve.sem_inc(v_out, 1)
                with dve.Fori(0, NS, 1) as s:
                    dve.wait_ge(xt_ps, s + 1)
                    for j in range(TS):
                        ins = nc.vector.tensor_scalar(t["xn"][:, j, :], x_sb[:, s * TS + j, :],
                                                      mv[:, s * TS + j, 0:1], rstd[:, bass.ds(s * TS + j, 1)],
                                                      ALU.subtract, ALU.mult)
                    ins.then_inc(xn_ready, 1)
                    dve.wait_ge(ct_ps, s + 1)
                    dve.wait_ge(k_ps, s + 1)
                    nc.vector.tensor_copy(t["ct"][:, :, :], psum[:, 2:4, :]).then_inc(ct_sb, 1)
                    dve.wait_ge(v_ps, s + 1)
                    dve.wait_ge(v_stored, 16 * s + 16)
                    v_in = psum[:, 6:8, :].rearrange("p a (j d) -> p (a j) d", j=2)
                    if biased:
                        ins = nc.vector.tensor_tensor(t["vo"][:, :, :], v_in,
                                                      t["bv"][:, :].unsqueeze(1).broadcast_to((P, TS, D)), ALU.add)
                    else:
                        ins = nc.vector.tensor_copy(t["vo"][:, :, :], v_in)
                    ins.then_inc(v_out, 1)
                    dve.wait_ge(k_ps, s + 2)
                    dve.wait_ge(k_stored, 32 * s + 16)
                    if biased:
                        for hh in range(2):
                            ins = nc.vector.tensor_scalar(t["ko"][:, hh, :], psum[:, 4 + hh, :],
                                                          t["bqk"][:, 1, hh:hh + 1], None, ALU.add)
                    else:
                        ins = nc.vector.tensor_copy(t["ko"][:, :, :], psum[:, 4:6, :])
                    ins.then_inc(k_out, 1)

            return alloc, sync, tensor, scalar, vector

        def relative_tables():
            ext_written, tables_loaded = sem("ext_written"), sem("tables_loaded")
            regrouped, pk_loaded, pk_ps, pk_t, ext_filled = (
                sem("regrouped"), sem("pk_loaded"), sem("pk_ps"), sem("pk_t"), sem("ext_filled"))
            lo = S - 1 - K
            hi = S - 1 + K

            def alloc(stack):
                return {"kw": sb("pos_k_skewed", [P, S + GN - 1], stack=stack),
                        "vw": sb("pos_v_by_key", [P, 2, GN, P], stack=stack)}

            def alloc_raw(stack, t):
                t["raw"] = sb("pos_v_by_query", [P, 2, S * DH], stack=stack)
                t["pk"] = sb("pos_k_rows", [2 * K, DH], stack=stack)
                t["pk_last"] = sb("pos_k_last", [1, DH], stack=stack)
                t["pkt"] = sb("pos_k_t", [DH, 2 * K + 1], stack=stack)
                t["extk"] = sb("pos_k_ext", [DH, 2 * S], stack=stack)

            def gpsimd(pool, t):
                pool.wait_ge(tables_loaded, 16 * (IN + 2))
                for kt in range(2):
                    ins = nc.gpsimd.tensor_copy(
                        t["vw"][:, kt, :, :].rearrange("p g (r d) -> p g r d", r=IN),
                        t["raw"][:, kt, :].rearrange("p (r g d) -> p g r d", r=IN, g=GN))
                ins.then_inc(regrouped, 1)

            def sync(sp, t):
                pk, pv = a["L0_xattn_pos_k"], a["L0_xattn_pos_v"]
                sp.dma_start(t["pk"][:, :], pk[0:2 * K, :]).then_inc(pk_loaded, 16)
                sp.dma_start(t["pk_last"][0:1, :], pk[2 * K:2 * K + 1, :]).then_inc(pk_loaded, 16)
                sp.dma_start(extv_dr[lo:hi + 1, :], pv).then_inc(ext_written, 16)
                sp.dma_start(extv_dr[0:lo, :], pv[0:1, :].broadcast_to((lo, DH))).then_inc(ext_written, 16)
                sp.dma_start(extv_dr[hi + 1:2 * S, :],
                             pv[2 * K:2 * K + 1, :].broadcast_to((2 * S - hi - 1, DH))).then_inc(ext_written, 16)
                sp.wait_ge(ext_written, 16 * 3)
                sp.wait_ge(ext_filled, 1)
                for i in range(IN):
                    off = S - GN - GN * i
                    sp.dma_start(t["kw"][i * DH:(i + 1) * DH, :], t["extk"][:, off:off + S + GN - 1]
                                 ).then_inc(tables_loaded, 16)
                for kt in range(2):
                    rows = bass.AP(extv_dr.tensor, kt * P * DH, [[DH, P], [1, S * DH]])
                    sp.dma_start(t["raw"][:, kt, :], rows).then_inc(tables_loaded, 16)

            def tensor(pe, t):
                pe.wait_ge(pk_loaded, 32)
                nc.tensor.transpose(psum[0:DH, 0, 0:2 * K], t["pk"][:, :], ident[:, :])
                nc.tensor.transpose(psum[0:DH, 0, 2 * K:2 * K + 1], t["pk_last"][0:1, :], ident[0:1, 0:1]
                                    ).then_inc(pk_ps, 1)
                pe.wait_ge(ext_filled, 1)

            def vector(dve, t):
                dve.wait_ge(pk_ps, 1)
                nc.vector.tensor_copy(t["pkt"][:, :], psum[0:DH, 0, 0:2 * K + 1]).then_inc(pk_t, 1)
                dve.wait_ge(pk_t, 1)
                nc.vector.tensor_copy(t["extk"][:, lo:hi + 1], t["pkt"][:, :])
                nc.vector.tensor_copy(t["extk"][:, 0:lo], t["pkt"][:, 0:1].broadcast_to((DH, lo)))
                nc.vector.tensor_copy(t["extk"][:, hi + 1:2 * S],
                                      t["pkt"][:, 2 * K:2 * K + 1].broadcast_to((DH, 2 * S - hi - 1))
                                      ).then_inc(ext_filled, 1)

            return alloc, alloc_raw, sync, gpsimd, tensor, vector, regrouped

        def attention(n_, relative, tables=None, tables_ready=None):
            in_loaded = [sem(f"qkv_loaded_{i}") for i in range(2)]
            in_dmas = 3 + (IN if relative else 0)
            mask_loaded = sem("mask_loaded")
            qd_ready, v_padded, s_ps = sem("qd_ready"), sem("v_padded"), sem("s_ps")
            masked, max_done, exp_done = sem("masked"), sem("max_done"), sem("exp_done")
            recip_done, w_ready, t_ps = sem("recip_done"), sem("w_ready"), sem("t_ps")
            wt_dve, wt_act, v_done = sem("wt_dve"), sem("wt_act"), sem("v_done")
            x_out, x_masked, zeroed = sem("x_out"), sem("x_masked"), sem("zeroed")
            h_stored = [sem(f"h_stored_{i}") for i in range(2)]
            out_dmas = 1 + (IN if relative else 0)

            def alloc(stack):
                t = {"q": [sb(f"q_b{n_}_{i}", [P, 2, S], stack=stack) for i in range(2)],
                     "k": [sb(f"k_b{n_}_{i}", [P, 2, S], stack=stack) for i in range(2)],
                     "v": [sb(f"v_b{n_}_{i}", [P, 2, D], stack=stack) for i in range(2)],
                     "vz": [sb(f"v_padded_b{n_}_{i}", [P, 2, H, 32], stack=stack) for i in range(2)],
                     "qd": [sb(f"q_blocks{n_}_{i}", [P, 512], stack=stack) for i in range(2)],
                     "negmax": sb(f"negmax{n_}", [P, 2, GC], stack=stack),
                     "sums": sb(f"sums{n_}", [P, 2, GC], stack=stack),
                     "recip": sb(f"recip{n_}", [P, 2, GC], stack=stack),
                     "w": [sb(f"weights{n_}_{i}", [P, GC, S], stack=stack) for i in range(3)],
                     "wt": [sb(f"weights_t{n_}_{i}", [P, 2, 512], stack=stack) for i in range(2)],
                     "h": [sb(f"heads{n_}_{i}", [P, 2, S], stack=stack) for i in range(2)]}
                if relative:
                    t["q2"] = [sb(f"q_by_i{n_}_{i}", [P, H, GN], stack=stack) for i in range(2)]
                    t["qd2"] = [sb(f"q_blocks_rel{n_}_{i}", [P, 512], stack=stack) for i in range(2)]
                    t["xm"] = sb(f"x_masked_t{n_}", [P, 512], stack=stack)
                    t["r"] = [sb(f"rel_heads{n_}_{i}", [P, H, GN], stack=stack) for i in range(2)]
                else:
                    t["mask"] = sb(f"mask{n_}", [P, 2, S], I32, stack=stack)
                    t["ms"] = [sb(f"masked_scores{n_}_{i}", [P, 2, 2 * S], stack=stack) for i in range(2)]
                return t

            def sync(sp, t):
                q_t = q_dr.rearrange("b (t p) s -> p b t s", p=P)
                k_t = k_dr.rearrange("b (t p) s -> p b t s", p=P)
                v_t = v_dr.rearrange("(b t p) d -> p b t d", p=P, t=2)
                h_t = h_dr.rearrange("b (t p) s -> p b t s", p=P)
                q2_t = q_dr.rearrange("b (h d) (i g) -> d b h i g", h=H, i=IN)
                r_t = r_dr.rearrange("b (h d) (i g) -> d b h i g", h=H, i=IN)

                def load(b, bb):
                    sp.dma_start(t["q"][bb][:, :, :], q_t[:, b]).then_inc(in_loaded[bb], 16)
                    sp.dma_start(t["k"][bb][:, :, :], k_t[:, b]).then_inc(in_loaded[bb], 16)
                    sp.dma_start(t["v"][bb][:, :, :], v_t[:, b]).then_inc(in_loaded[bb], 16)
                    if relative:
                        for i in range(IN):
                            sp.dma_start(t["q2"][bb][i * DH:(i + 1) * DH, :, :], q2_t[:, b, :, i, :]
                                         ).then_inc(in_loaded[bb], 16)

                if not relative:
                    sp.dma_start(t["mask"][:, :, :], a["mask_SxS2_ik1"].rearrange("(t p) k -> p t k", p=P)
                                 ).then_inc(mask_loaded, 16)
                for bb in range(2):
                    load(bb, bb)
                    sp.sem_inc(h_stored[bb], 16)
                with sp.Fori(0, B // 2, 1) as it:
                    for bb in range(2):
                        sp.wait_ge(x_out, it * NB2 + NC * (bb + 1) + 1)
                        sp.dma_start(h_t[:, it * 2 + bb], t["h"][bb][:, :, :]).then_inc(h_stored[bb], 16)
                        if relative:
                            for r in range(IN):
                                sp.dma_start(r_t[:, it * 2 + bb, :, IN - 1 - r, :],
                                             t["r"][bb][r * DH:(r + 1) * DH, :, :]).then_inc(h_stored[bb], 16)
                        load((it * 2 + bb + 2) % B, bb)
                for bb in range(2):
                    sp.wait_ge(h_stored[bb], 16 + 16 * out_dmas * (B // 2))
                    sp.wait_ge(in_loaded[bb], 16 * in_dmas * (B // 2 + 1))

            def gpsimd(pool, t):
                for bb in range(2):
                    ins = nc.gpsimd.memset(t["vz"][bb][:, :, :, :], 0.0)
                ins.then_inc(zeroed, 1)
                if not relative:
                    for i in range(2):
                        ins = nc.gpsimd.memset(t["ms"][i][:, :, :], MASKED)
                    ins.then_inc(zeroed, 1)
                pool.wait_ge(zeroed, 1 if relative else 2)
                pool.sem_inc(v_done, NB2)
                with pool.Fori(0, B // 2, 1) as it:
                    def q_blocks(n):
                        bb, c, buf = n // NC, n % NC, n % 2
                        if c == 0:
                            pool.wait_ge(in_loaded[bb], 16 * in_dmas * (it + 1))
                        if n >= 2:
                            pool.wait_ge(s_ps, it * NB2 + n - 1)
                        if relative:
                            for hh in range(2):
                                out_ = t["qd"][buf][:, hh * 256:(hh + 1) * 256].rearrange("p (g h i) -> p g h i", g=GC, h=8)
                                src = t["q"][bb][:, hh, :].rearrange("p (i g) -> p g i", g=GN)[:, GC * c:GC * (c + 1), :]
                                nc.gpsimd.tensor_tensor(
                                    out_, src.unsqueeze(2).broadcast_to((P, GC, 8, IN)),
                                    block[:, :].unsqueeze(1).unsqueeze(3).broadcast_to((P, GC, 8, IN)), ALU.mult)
                            out_ = t["qd2"][buf][:, :].rearrange("p (g h i) -> p g h i", g=GC, h=H)
                            src = t["q2"][bb][:, :, GC * c:GC * (c + 1)].rearrange("p h g -> p g h")
                            ins = nc.gpsimd.tensor_tensor(
                                out_, src.unsqueeze(3).broadcast_to((P, GC, H, IN)),
                                block[:, :].unsqueeze(1).unsqueeze(1).broadcast_to((P, GC, H, IN)), ALU.mult)
                        else:
                            out_ = t["qd"][buf][:, :].rearrange("p (h q) -> p h q", h=2)
                            src = t["q"][bb][:, c // 4, :]
                            m = block[:, 2 * (c % 4):2 * (c % 4) + 2]
                            ins = nc.gpsimd.tensor_tensor(out_, src.unsqueeze(1).broadcast_to((P, 2, S)),
                                                          m.unsqueeze(2).broadcast_to((P, 2, S)), ALU.mult)
                        ins.then_inc(qd_ready, 1)

                    def scale(n):
                        pool.wait_ge(recip_done, it * NB2 + n + 1)
                        nc.gpsimd.tensor_tensor(
                            t["w"][n % 3][:, :, :], t["w"][n % 3][:, :, :],
                            t["recip"][:, n % 2, :].unsqueeze(2).broadcast_to((P, GC, S)), ALU.mult).then_inc(w_ready, 1)

                    q_blocks(0)
                    for n in range(NB2):
                        if n + 1 < NB2:
                            q_blocks(n + 1)
                        if n >= 1:
                            scale(n - 1)
                    scale(NB2 - 1)

            def tensor(pe, t):
                if relative:
                    pe.wait_ge(tables_ready, 1)
                with pe.Fori(0, B // 2, 1) as it:
                    def scores(n):
                        bb, c, buf = n // NC, n % NC, n % 2
                        if c == 0:
                            pe.wait_ge(in_loaded[bb], 16 * in_dmas * (it + 1))
                        pe.wait_ge(qd_ready, it * NB2 + n + 1)
                        if n >= 2:
                            pe.wait_ge(exp_done, it * NB2 + n - 1)
                        for g in range(GC):
                            s_g = psum[:, buf * 2 + g // 2, (g % 2) * S:(g % 2 + 1) * S]
                            if relative:
                                off = GN - 1 - (GC * c + g)
                                nc.tensor.matmul(s_g, t["qd2"][buf][:, g * P:(g + 1) * P],
                                                 tables["kw"][:, off:off + S], start=True, stop=False,
                                                 skip_group_check=True)
                                for hh in range(2):
                                    ins = nc.tensor.matmul(
                                        psum[hh * 64:(hh + 1) * 64, buf * 2 + g // 2, (g % 2) * S:(g % 2 + 1) * S],
                                        t["qd"][buf][:, hh * 256 + g * 64:hh * 256 + (g + 1) * 64],
                                        t["k"][bb][:, hh, :], start=False, stop=True, skip_group_check=True)
                            else:
                                ins = nc.tensor.matmul(s_g, t["qd"][buf][:, g * P:(g + 1) * P],
                                                       t["k"][bb][:, c // 4, :], start=True, stop=True)
                        ins.then_inc(s_ps, 1)

                    def transposes(n):
                        pe.wait_ge(w_ready, it * NB2 + n + 1)
                        if n >= 1:
                            pe.wait_ge(wt_dve, it * NB2 + n)
                            pe.wait_ge(wt_act, it * NB2 + n)
                        for kt in range(2):
                            for g in range(GC):
                                ins = nc.tensor.transpose(psum[:, 4 + kt, g * P:(g + 1) * P],
                                                          t["w"][n % 3][:, g, kt * P:(kt + 1) * P], ident[:, :])
                        ins.then_inc(t_ps, 1)

                    def values(n):
                        bb, c = n // NC, n % NC
                        if c == 0:
                            pe.wait_ge(v_padded, it * 2 + bb + 1)
                        pe.wait_ge(wt_dve, it * NB2 + n + 1)
                        pe.wait_ge(wt_act, it * NB2 + n + 1)
                        pe.wait_ge(x_out, it * NB2 + n + 1)
                        wt = t["wt"][n % 2]
                        if relative:
                            for hh in range(2):
                                for h in range(8):
                                    for kt in range(2):
                                        head = hh * 8 + h
                                        rhs = wt[:, kt, :].rearrange("p (g c) -> p g c", g=GC)[:, :, head * IN:(head + 1) * IN]
                                        j = h // 2
                                        nc.tensor.matmul(psum[32 * j:32 * j + 32, 6, hh * 32:(hh + 1) * 32],
                                                         t["vz"][bb][:, kt, head, :], rhs,
                                                         start=(h % 2 == 0 and kt == 0), stop=(h % 2 == 1 and kt == 1),
                                                         tile_position=(0, 32 * j))
                            for g in range(GC):
                                for kt in range(2):
                                    ins = nc.tensor.matmul(psum[:, 7, g * P:(g + 1) * P],
                                                           tables["vw"][:, kt, GN - 1 - (GC * c + g), :],
                                                           wt[:, kt, g * P:(g + 1) * P], start=(kt == 0), stop=(kt == 1))
                        else:
                            j = c % 4
                            for h2 in range(2):
                                for kt in range(2):
                                    ins = nc.tensor.matmul(psum[32 * j:32 * j + 32, 6 + c // 4, 0:S],
                                                           t["vz"][bb][:, kt, 2 * c + h2, :],
                                                           wt[:, kt, h2 * S:(h2 + 1) * S],
                                                           start=(h2 == 0 and kt == 0), stop=(h2 == 1 and kt == 1),
                                                           tile_position=(0, 32 * j))
                        ins.then_inc(v_done, 1)

                    for n in range(NB2):
                        scores(n)
                        if n >= 2:
                            transposes(n - 2)
                        if n >= 3:
                            values(n - 3)
                    transposes(NB2 - 2)
                    values(NB2 - 3)
                    transposes(NB2 - 1)
                    values(NB2 - 2)
                    values(NB2 - 1)

            def scalar(act, t):
                act.wait_ge(zeroed, 1 if relative else 2)
                with act.Fori(0, B // 2, 1) as it:
                    def pad_v(bb):
                        act.wait_ge(in_loaded[bb], 16 * in_dmas * (it + 1))
                        act.wait_ge(v_done, it * NB2 + NC * (bb + 1))
                        for kt in range(2):
                            for h2 in range(2):
                                dst = t["vz"][bb][:, kt, :, :].rearrange("p (j e) c -> p j e c", e=2)
                                src = t["v"][bb][:, kt, :].rearrange("p (j e d) -> p j e d", e=2, d=DH)
                                ins = nc.scalar.copy(dst[:, :, h2, h2 * DH:(h2 + 1) * DH], src[:, :, h2, :])
                        ins.then_inc(v_padded, 1)

                    def exps(n):
                        act.wait_ge(max_done, it * NB2 + n + 1)
                        if n >= 3:
                            act.wait_ge(t_ps, it * NB2 + n - 2)
                        for g in range(GC):
                            if relative:
                                src = psum[:, (n % 2) * 2 + g // 2, (g % 2) * S:(g % 2 + 1) * S]
                            else:
                                src = t["ms"][n % 2][:, g // 2, (g % 2) * S:(g % 2 + 1) * S]
                            ins = nc.scalar.activation(t["w"][n % 3][:, g, :], src, ACT.Exp,
                                                       bias=t["negmax"][:, n % 2, g:g + 1],
                                                       accum_out=t["sums"][:, n % 2, g:g + 1])
                        ins.then_inc(exp_done, 1)

                    def evacuate(n):
                        act.wait_ge(t_ps, it * NB2 + n + 1)
                        act.wait_ge(v_done, it * NB2 + NB2 + n - 1)
                        nc.scalar.copy(t["wt"][n % 2][:, 1, :], psum[:, 5, :]).then_inc(wt_act, 1)

                    pad_v(0)
                    for n in range(NB2):
                        exps(n)
                        if n == NC:
                            pad_v(1)
                        if n >= 2:
                            evacuate(n - 2)
                    evacuate(NB2 - 2)
                    evacuate(NB2 - 1)

            def vector(dve, t):
                dve.sem_inc(x_out, 1)
                if not relative:
                    dve.wait_ge(mask_loaded, 16)
                    dve.wait_ge(zeroed, 2)
                with dve.Fori(0, B // 2, 1) as it:
                    def maxima(n):
                        if relative:
                            dve.wait_ge(s_ps, it * NB2 + n + 1)
                        else:
                            if n >= 2:
                                dve.wait_ge(exp_done, it * NB2 + n - 1)
                            wait_apart(dve, s_ps, it * NB2 + n + 1)
                        src = psum[:, (n % 2) * 2:(n % 2) * 2 + 2, :]
                        if not relative:
                            nc.vector.copy_predicated(t["ms"][n % 2][:, :, :],
                                                      t["mask"][:, :, :].rearrange("p t k -> p (t k)").unsqueeze(1)
                                                      .broadcast_to((P, 2, 2 * S)), src).then_inc(masked, 1)
                            dve.wait_ge(masked, it * NB2 + n + 1)
                            src = t["ms"][n % 2][:, :, :]
                        nc.vector.tensor_reduce(t["negmax"][:, n % 2, :],
                                                src.rearrange("p a (g k) -> p (a g) k", g=2), X, ALU.max,
                                                negate=True).then_inc(max_done, 1)

                    def reciprocals(n):
                        dve.wait_ge(exp_done, it * NB2 + n + 1)
                        nc.vector.reciprocal(t["recip"][:, n % 2, :], t["sums"][:, n % 2, :]).then_inc(recip_done, 1)

                    def evacuate(n):
                        dve.wait_ge(t_ps, it * NB2 + n + 1)
                        dve.wait_ge(v_done, it * NB2 + NB2 + n - 1)
                        nc.vector.tensor_copy(t["wt"][n % 2][:, 0, :], psum[:, 4, :]).then_inc(wt_dve, 1)

                    def heads(n):
                        bb, c = n // NC, n % NC
                        dve.wait_ge(v_done, it * NB2 + NB2 + n + 1)
                        if c == 0:
                            dve.wait_ge(h_stored[bb], it * 16 * out_dmas + 16)
                        if relative:
                            dst = t["h"][bb][:, :, :].rearrange("p t (i g) -> p t g i", g=GN)[:, :, GC * c:GC * (c + 1), :]
                            nc.vector.tensor_copy(dst, psum[:, 6, 0:64].rearrange("p (t g i) -> p t g i", t=2, g=GC))
                            nc.vector.tensor_tensor(
                                t["xm"][:, :].rearrange("p (m i) -> p m i", i=IN),
                                psum[:, 7, :].rearrange("p (m i) -> p m i", i=IN),
                                block_rev[:, :].unsqueeze(1).broadcast_to((P, GC * H, IN)), ALU.mult
                            ).then_inc(x_masked, 1)
                            dve.wait_ge(x_masked, it * NB2 + n + 1)
                            nc.vector.tensor_reduce(
                                t["r"][bb][:, :, GC * c:GC * (c + 1)].rearrange("p h g -> p g h"),
                                t["xm"][:, :].rearrange("p (g h i) -> p g h i", g=GC, h=H), X, ALU.add
                            ).then_inc(x_out, 1)
                        elif c % 4 == 3:
                            nc.vector.tensor_copy(t["h"][bb][:, c // 4, :], psum[:, 6 + c // 4, 0:S]).then_inc(x_out, 1)
                        else:
                            dve.sem_inc(x_out, 1)

                    for n in range(NB2):
                        maxima(n)
                        if n >= 1:
                            reciprocals(n - 1)
                        if n >= 2:
                            evacuate(n - 2)
                        if n >= 3:
                            heads(n - 3)
                    reciprocals(NB2 - 1)
                    evacuate(NB2 - 2)
                    heads(NB2 - 3)
                    evacuate(NB2 - 1)
                    heads(NB2 - 2)
                    heads(NB2 - 1)

            return alloc, sync, gpsimd, tensor, scalar, vector

        def merge_heads(n_, w_ap, transposed, parts, bias_ap=None):
            h_loaded = [sem(f"h_loaded_{i}") for i in range(2)]
            w_loaded, o_ps, x_added = sem("fc_loaded"), sem("o_ps"), sem("x_added")
            w_ps, w_done, ones_set = sem("fc_ps"), sem("fc_done"), sem("ones_set")
            np_ = len(parts)

            def alloc(stack):
                return {"w": sb(f"w_fc{n_}", [P, KT, D], stack=stack), "raw": sb(f"w_fc_raw{n_}", [P, KT, D], stack=stack),
                        "bias": sb(f"b_fc{n_}", [1, D], stack=stack), "ones": sb(f"ones{n_}", [1, P], stack=stack),
                        "h": [sb(f"h_in{n_}_{i}", [P, np_, 2, SC], stack=stack) for i in range(2)]}

            def sync(sp, t):
                dst = t["raw"] if transposed else t["w"]
                sp.dma_start(dst[:, :, :], w_ap.rearrange("(t p) n -> p t n", p=P)).then_inc(w_loaded, 16)
                if bias_ap is not None:
                    sp.dma_start(t["bias"][0:1, :], bias_ap.unsqueeze(0)).then_inc(w_loaded, 16)
                sp.sem_inc(o_ps, 2)
                with sp.Fori(0, NS // 2, 1) as it:
                    for j in range(2):
                        sp.wait_ge(o_ps, it * 2 + j + 1)
                        for i, part in enumerate(parts):
                            src = part.rearrange("b (t p) s -> p t b s", p=P)
                            for hh in range(2):
                                sp.dma_start(t["h"][j][:, i, hh, :].rearrange("p (b s) -> p b s", b=2),
                                             src[:, hh, bass.ds((it * 2 + j) * 2, 2), :]).then_inc(h_loaded[j], 16)

            def tensor(pe, t):
                pe.wait_ge(w_loaded, 32 if bias_ap is not None else 16)
                if transposed:
                    for ot in range(2):
                        for kt in range(KT):
                            ins = nc.tensor.transpose(psum[:, kt, ot * P:(ot + 1) * P],
                                                      t["raw"][:, ot, kt * P:(kt + 1) * P], ident[:, :])
                    ins.then_inc(w_ps, 1)
                    pe.wait_ge(w_done, 1)
                if bias_ap is not None:
                    pe.wait_ge(ones_set, 1)
                with pe.Fori(0, NS // 2, 1) as it:
                    for j in range(2):
                        pe.wait_ge(h_loaded[j], 32 * np_ * (it + 1))
                        pe.wait_ge(x_added, it * 2 + j + 1)
                        for m in range(TS):
                            o = psum[:, 2 + 2 * j + m // 2, (m % 2) * D:(m % 2 + 1) * D]
                            if bias_ap is not None:
                                nc.tensor.matmul(o, t["ones"][0:1, :], t["bias"][0:1, :], start=True, stop=False)
                            for i in range(np_):
                                for kt in range(KT):
                                    ins = nc.tensor.matmul(o, t["h"][j][:, i, kt, m * P:(m + 1) * P], t["w"][:, kt, :],
                                                           start=(bias_ap is None and i == 0 and kt == 0),
                                                           stop=(i == np_ - 1 and kt == KT - 1))
                        ins.then_inc(o_ps, 1)

            def vector(dve, t):
                if transposed:
                    dve.wait_ge(w_ps, 1)
                    nc.vector.tensor_copy(t["w"][:, :, :], psum[:, 0:2, 0:D]).then_inc(w_done, 1)
                if bias_ap is not None:
                    nc.vector.memset(t["ones"][0:1, :], 1.0).then_inc(ones_set, 1)
                dve.sem_inc(x_added, 2)
                with dve.Fori(0, NS // 2, 1) as it:
                    for j in range(2):
                        dve.wait_ge(o_ps, it * 2 + j + 3)
                        xs = x_sb[:, bass.ds((it * 2 + j) * TS, TS), :]
                        o = psum[:, 2 + 2 * j:4 + 2 * j, :].rearrange("p a (m d) -> p (a m) d", m=2)
                        nc.vector.tensor_tensor(xs, o, xs, ALU.add).then_inc(x_added, 1)

            return alloc, sync, tensor, vector

        def quantised_ffn():
            w_loaded, w_amax, w_step_done, w_recip = sem("fw_loaded"), sem("fw_amax"), sem("fw_step"), sem("fw_recip")
            w_div, w_round, w_quant, w_ps, w_sb_done = (sem("fw_div"), sem("fw_round"), sem("fw_quant"), sem("fw_ps"),
                                                        sem("fw_sb"))
            xn_ready, xt_ps, xt_sb, x_max = sem("fxn_ready"), sem("fxt_ps"), sem("fxt_sb"), sem("fx_max")
            fold, amax_part, amax_all, sc_step, scaled = (sem("amax_fold"), sem("amax_part"), sem("amax_all"),
                                                          sem("scale_step"), sem("scaled"))
            x_round, x_quant, magic_set, acc_set = sem("x_round"), sem("x_quant"), sem("magic_set"), sem("acc_set")
            m_ps, m_used = sem("m_ps"), sem("m_used")
            g_ps, g_round, g_val, g_sig, g_y, g_clip, g_prod = (sem("g_ps"), sem("g_round"), sem("g_val"), sem("g_sig"),
                                                                sem("g_y"), sem("g_clip"), sem("g_prod"))
            g_max = sem("g_max")
            u_ps, u_round, p_round, u_int, u_prod, u_max = (sem("u_ps"), sem("u_round"), sem("p_round"), sem("u_int"),
                                                            sem("u_prod"), sem("u_max"))
            o_round, o_int_dve, o_int_pool, d_ps, d_added = (sem("o_round"), sem("o_int_dve"), sem("o_int_pool"),
                                                             sem("d_ps"), sem("d_added"))
            F = 768
            FT = F // P
            NP = FT // 2
            NI = 2 * NP

            def alloc(stack):
                t = {"wg": sb("wg_t", [P, KT, F], stack=stack), "wu": sb("wu_t", [P, KT, F], stack=stack),
                     "wd": sb("wd_t", [P, FT, D], stack=stack), "xt": sb("xq_t", [P, KT, B * S], stack=stack),
                     "am": sb("amax_new", [P, 12], stack=stack), "acc": sb("amax_sofar", [P, 12], stack=stack),
                     "ar": sb("amax_row", [P, 8], stack=stack), "aa": sb("amax_whole", [P, 8], stack=stack),
                     "sc": sb("scales", [P, 16], stack=stack),
                     "magic": sb("magic", [P, 1], stack=stack)}
                with ExitStack() as inner:
                    t["raw"] = sb("fw_raw", [P, 3, F * D // P], stack=inner)
                    t["wq"] = sb("fw_q", [P, 3, F * D // P], stack=inner)
                    t["wam"] = sb("fw_amax_t", [P, 3, F * D // P // QBLOCK], stack=inner)
                    t["wsc"] = sb("fw_scale_t", [P, 3, F * D // P // QBLOCK], stack=inner)
                    t["xn"] = sb("fxn", [P, TS, D], stack=inner)
                t["p"] = sb("gated", [P, FT, B * S], stack=stack)
                with ExitStack() as inner:
                    t["a"] = [sb(f"ff_a{i}", [P, 2 * SC], stack=inner) for i in range(2)]
                    t["b"] = [sb(f"ff_b{i}", [P, 2 * SC], stack=inner) for i in range(2)]
                    t["c"] = [sb(f"ff_c{i}", [P, 2 * SC], stack=inner) for i in range(2)]
                with ExitStack() as inner:
                    t["o"] = [sb(f"ff_o{i}", [P, FT, SC], stack=inner) for i in range(2)]
                return t

            def sync(sp, t):
                for i, nm in enumerate(("L0_ffn_w_gate", "L0_ffn_w_up", "L0_ffn_w_down")):
                    w = a[nm]
                    sp.dma_start(t["raw"][:, i, :].rearrange("p (t n) -> p t n", n=w.shape[1]),
                                 w.rearrange("(t p) n -> p t n", p=P)).then_inc(w_loaded, 16)

            def gpsimd(pool, t):
                nc.gpsimd.memset(t["magic"][:, :], MAGIC).then_inc(magic_set, 1)
                for k, (c0, n) in enumerate(((0, 1), (1, 2), (3, 1), (4, 1))):
                    pool.wait_ge(amax_part, k + 1)
                    nc.gpsimd.partition_all_reduce(t["aa"][:, c0:c0 + n], t["ar"][:, c0:c0 + n], P, ABSMAX
                                                   ).then_inc(amax_all, 1)
                    if k == 2:
                        with pool.Fori(0, NS // 2, 1) as it:
                            for i in range(NI):
                                pool.wait_ge(u_round, it * NI + i + 4)
                                nc.gpsimd.tensor_tensor(t["a"][i % 2][:, :], t["a"][i % 2][:, :],
                                                        t["magic"][:, :].broadcast_to((P, 2 * SC)), ALU.subtract
                                                        ).then_inc(u_int, 1)
                with pool.Fori(0, NS // 2, 1) as it:
                    for j in range(2):
                        pool.wait_ge(o_round, it * 2 + j + 1)
                        o2 = t["o"][j][:, NP:FT, :]
                        nc.gpsimd.tensor_tensor(o2, o2, t["magic"][:, :].unsqueeze(2).broadcast_to((P, FT - NP, SC)),
                                                ALU.subtract).then_inc(o_int_pool, 1)

            def bank_pair(i):
                return psum[:, 2 * (i % 3):2 * (i % 3) + 2, :]

            def product(w, xq, s, pr, i, done):
                for e in range(2):
                    f = pr * 2 + e
                    for kt in range(KT):
                        ins = nc.tensor.matmul(psum[:, 2 * (i % 3) + e, :], w[:, kt, f * P:(f + 1) * P],
                                               xq[:, kt, bass.ds(s * SC, SC)], start=(kt == 0), stop=(kt == KT - 1))
                ins.then_inc(done, 1)

            def tensor(pe, t):
                pe.wait_ge(w_quant, 3)
                for i in range(2):
                    for f in range(FT):
                        for kt in range(KT):
                            idx = (i * FT + f) * KT + kt
                            ins = nc.tensor.transpose(psum[:, idx // 4, (idx % 4) * P:(idx % 4 + 1) * P],
                                                      t["wq"][:, i, f * D + kt * P:f * D + (kt + 1) * P], ident[:, :])
                ins.then_inc(w_ps, 1)
                pe.wait_ge(w_sb_done, 1)
                for ot in range(KT):
                    for f in range(FT):
                        idx = f * KT + ot
                        ins = nc.tensor.transpose(psum[:, idx // 4, (idx % 4) * P:(idx % 4 + 1) * P],
                                                  t["wq"][:, 2, ot * F + f * P:ot * F + (f + 1) * P], ident[:, :])
                ins.then_inc(w_ps, 1)
                pe.wait_ge(w_sb_done, 2)
                pe.sem_inc(xt_ps, 1)
                with pe.Fori(0, NS, 1) as s:
                    pe.wait_ge(xn_ready, s + 1)
                    pe.wait_ge(xt_sb, s + 1)
                    for kt in range(KT):
                        for j in range(TS):
                            ins = nc.tensor.transpose(psum[:, kt, j * P:(j + 1) * P],
                                                      t["xn"][:, j, kt * P:(kt + 1) * P], ident[:, :])
                    ins.then_inc(xt_ps, 1)
                pe.wait_ge(x_quant, 1)
                with pe.Fori(0, NS, 1) as s:
                    for i in range(NI):
                        pe.wait_ge(m_used, s * NI + i + 1)
                        product((t["wg"], t["wu"])[i // NP], t["xt"], s, i % NP, i, m_ps)
                pe.wait_ge(m_used, NS * NI + 3)
                with pe.Fori(0, NS // 2, 1) as it:
                    for i in range(NI):
                        pe.wait_ge(g_round, it * NI + i + 1)
                        product(t["wg"], t["xt"], it * 2 + i // NP, i % NP, i, g_ps)
                pe.wait_ge(g_round, NS // 2 * NI + 3)
                with pe.Fori(0, NS // 2, 1) as it:
                    for i in range(NI):
                        pe.wait_ge(u_round, it * NI + i + 1)
                        product(t["wu"], t["xt"], it * 2 + i // NP, i % NP, i, u_ps)
                pe.wait_ge(u_round, NS // 2 * NI + 3)
                pe.sem_inc(d_ps, 2)
                with pe.Fori(0, NS // 2, 1) as it:
                    for j in range(2):
                        pe.wait_ge(o_int_dve, it * 2 + j + 1)
                        pe.wait_ge(o_int_pool, it * 2 + j + 1)
                        pe.wait_ge(d_added, it * 2 + j + 1)
                        for m in range(TS):
                            for f in range(FT):
                                ins = nc.tensor.matmul(psum[:, 2 * j + m // 2, (m % 2) * D:(m % 2 + 1) * D],
                                                       t["o"][j][:, f, m * P:(m + 1) * P], t["wd"][:, f, :],
                                                       start=(f == 0), stop=(f == FT - 1))
                        ins.then_inc(d_ps, 1)

            def scalar(act, t):
                act.wait_ge(w_ps, 1)
                for w, b0 in ((t["wg"], 0), (t["wu"], 3)):
                    for kt in range(KT):
                        src = psum[:, b0:b0 + 3, :].rearrange("p a (f k m) -> p (a f) k m", f=2, k=KT)
                        ins = nc.scalar.copy(w[:, kt, :].rearrange("p (f m) -> p f m", f=FT), src[:, :, kt, :])
                ins.then_inc(w_sb_done, 1)
                act.wait_ge(w_ps, 2)
                nc.scalar.copy(t["wd"][:, :, :], psum[:, 0:3, :].rearrange("p a (f n) -> p (a f) n", f=2)
                               ).then_inc(w_sb_done, 1)
                act.wait_ge(magic_set, 1)
                act.sem_inc(xt_sb, 1)
                act.sem_inc(g_round, 3)
                act.sem_inc(u_round, 3)
                with act.Fori(0, NS, 1) as s:
                    wait_apart(act, xt_ps, s + 2)
                    nc.scalar.copy(t["xt"][:, :, bass.ds(s * SC, SC)], psum[:, 0:2, :]).then_inc(xt_sb, 1)
                magic = t["magic"][:, 0:1]
                act.wait_ge(scaled, 2)
                with act.Fori(0, NS // 2, 1) as it:
                    def round_gate(i):
                        act.wait_ge(g_ps, it * NI + i + 1)
                        if i >= 2:
                            act.wait_ge(g_val, it * NI + i - 1)
                        nc.scalar.activation(t["a"][i % 2][:, :].rearrange("p (a n) -> p a n", a=2), bank_pair(i),
                                             ACT.Identity, bias=magic, scale=t["sc"][:, GATE_BY:GATE_BY + 1]
                                             ).then_inc(g_round, 1)

                    def sigmoid(i):
                        act.wait_ge(g_val, it * NI + i + 1)
                        act.wait_ge(g_prod, it * NI + i + 1)
                        nc.scalar.activation(t["c"][i % 2][:, :], t["b"][i % 2][:, :], ACT.Sigmoid).then_inc(g_sig, 1)
                        act.wait_ge(g_sig, it * NI + i + 1)
                        nc.scalar.activation(t["c"][i % 2][:, :], t["c"][i % 2][:, :], ACT.Identity,
                                             bias=magic, scale=SIG_STEPS).then_inc(g_y, 1)

                    for i in range(NI):
                        round_gate(i)
                        if i >= 1:
                            sigmoid(i - 1)
                    sigmoid(NI - 1)
                act.wait_ge(scaled, 3)
                with act.Fori(0, NS // 2, 1) as it:
                    for i in range(NI):
                        s, pr = it * 2 + i // NP, i % NP
                        wait_apart(act, u_prod, it * NI + i + 1)
                        nc.scalar.activation(t["b"][i % 2][:, :].rearrange("p (e n) -> p e n", e=2),
                                             t["p"][:, 2 * pr:2 * pr + 2, bass.ds(s * SC, SC)], ACT.Identity,
                                             bias=magic, scale=t["sc"][:, GATED_BY:GATED_BY + 1]).then_inc(p_round, 1)
                        act.wait_ge(u_ps, it * NI + i + 1)
                        nc.scalar.activation(t["a"][i % 2][:, :].rearrange("p (a n) -> p a n", a=2), bank_pair(i),
                                             ACT.Identity, bias=magic, scale=t["sc"][:, UP_BY:UP_BY + 1]
                                             ).then_inc(u_round, 1)
                act.wait_ge(scaled, 4)
                with act.Fori(0, NS // 2, 1) as it:
                    for j in range(2):
                        wait_apart(act, d_ps, it * 2 + j + 1)
                        nc.scalar.activation(t["o"][j][:, :, :], t["p"][:, :, bass.ds((it * 2 + j) * SC, SC)],
                                             ACT.Identity, bias=magic, scale=t["sc"][:, OUT_BY:OUT_BY + 1]
                                             ).then_inc(o_round, 1)

            def vector(dve, t):
                nb = F * D // P // QBLOCK
                blocked = [t[n_][:, :, :].rearrange("p i (b q) -> p (i b) q", q=QBLOCK) for n_ in ("raw", "wq")]
                wam, wsc = (t[n_][:, :, :].rearrange("p i b -> p (i b)") for n_ in ("wam", "wsc"))
                dve.wait_ge(w_loaded, 48)
                nc.vector.tensor_reduce(wam, blocked[0], X, ALU.max, apply_absolute_value=True).then_inc(w_amax, 1)
                dve.wait_ge(w_amax, 1)
                nc.vector.tensor_scalar(wsc, wam, 1.0 / W_QMAX, TINY, ALU.mult, ALU.max).then_inc(w_step_done, 1)
                dve.wait_ge(w_step_done, 1)
                nc.vector.reciprocal(wam, wsc).then_inc(w_recip, 1)
                dve.wait_ge(w_recip, 1)
                shape = (P, 3 * nb, QBLOCK)
                nc.vector.tensor_tensor(blocked[1], blocked[0], wam.unsqueeze(2).broadcast_to(shape), ALU.mult
                                        ).then_inc(w_div, 1)
                dve.wait_ge(w_div, 1)
                flat = t["wq"][:, :, :].rearrange("p i n -> p (i n)")
                nc.vector.tensor_scalar(flat, flat, MAGIC, MAGIC, ALU.add, ALU.subtract).then_inc(w_round, 1)
                dve.wait_ge(w_round, 1)
                nc.vector.tensor_tensor(blocked[1], blocked[1], wsc.unsqueeze(2).broadcast_to(shape), ALU.mult
                                        ).then_inc(w_quant, 3)
                nc.vector.memset(t["acc"][:, :], 0.0).then_inc(acc_set, 1)
                dve.wait_ge(acc_set, 1)

                def keep_max(n, count):
                    nc.vector.tensor_tensor(t["acc"][:, 0:n], t["acc"][:, 0:n], t["am"][:, 0:n], ALU.max
                                            ).then_inc(fold, 1)
                    dve.wait_ge(fold, count)

                def whole_max(k, groups):
                    for c, lo, hi in groups:
                        ins = nc.vector.tensor_reduce(t["ar"][:, c:c + 1], t["acc"][:, lo:hi], X, ALU.max)
                    ins.then_inc(amax_part, 1)
                    dve.wait_ge(amax_all, k)
                    nc.vector.memset(t["acc"][:, :], 0.0)

                steps = [0]

                def small(ins):
                    steps[0] += 1
                    ins.then_inc(sc_step, 1)
                    dve.wait_ge(sc_step, steps[0])

                def col(i):
                    return t["sc"][:, i:i + 1]

                def whole(i):
                    return t["aa"][:, i:i + 1]

                with dve.Fori(0, NS, 1) as s:
                    dve.wait_ge(xt_ps, s + 1)
                    for j in range(TS):
                        ins = nc.vector.tensor_scalar(t["xn"][:, j, :], x_sb[:, s * TS + j, :],
                                                      mv[:, s * TS + j, 0:1], rstd[:, bass.ds(s * TS + j, 1)],
                                                      ALU.subtract, ALU.mult)
                    ins.then_inc(xn_ready, 1)
                    dve.wait_ge(xn_ready, s + 1)
                    nc.vector.tensor_reduce(t["am"][:, 0:1], t["xn"][:, :, :].rearrange("p t n -> p (t n)"), X,
                                            ALU.max, apply_absolute_value=True).then_inc(x_max, 1)
                    dve.wait_ge(x_max, s + 1)
                    keep_max(1, s + 1)
                whole_max(1, ((0, 0, 1),))
                small(nc.vector.tensor_scalar(col(X_STEP), whole(0), 1.0 / QMAX, TINY, ALU.mult, ALU.max))
                small(nc.vector.reciprocal(col(X_BY), col(X_STEP)))
                dve.wait_ge(xt_sb, NS + 1)
                xt = t["xt"][:, :, :].rearrange("p k n -> p (k n)")
                nc.vector.tensor_scalar(xt, xt, col(X_BY), MAGIC, ALU.mult, ALU.add).then_inc(x_round, 1)
                dve.wait_ge(x_round, 1)
                nc.vector.tensor_scalar(xt, xt, MAGIC, None, ALU.subtract).then_inc(x_quant, 1)
                dve.sem_inc(m_used, 3)
                with dve.Fori(0, NS, 1) as s:
                    for i in range(NI):
                        dve.wait_ge(m_ps, s * NI + i + 1)
                        nc.vector.tensor_reduce(t["am"][:, i:i + 1], bank_pair(i), mybir.AxisListType.XY, ALU.max,
                                                apply_absolute_value=True).then_inc(m_used, 1)
                    dve.wait_ge(m_used, s * NI + NI + 3)
                    keep_max(NI, s + NS + 1)
                whole_max(2, ((1, 0, NP), (2, NP, NI)))
                for c, step, by in ((1, GATE_STEP, GATE_BY), (2, UP_STEP, UP_BY)):
                    small(nc.vector.tensor_scalar(col(step), whole(c), col(X_STEP), 1.0 / QMAX, ALU.mult, ALU.mult))
                    small(nc.vector.tensor_scalar(col(step), col(step), TINY, None, ALU.max))
                    small(nc.vector.reciprocal(col(by), col(step)))
                    small(nc.vector.tensor_scalar(col(by), col(by), col(X_STEP), None, ALU.mult))
                dve.sem_inc(scaled, 2)
                dve.sem_inc(g_prod, 2)
                with dve.Fori(0, NS // 2, 1) as it:
                    def gate_value(i):
                        dve.wait_ge(g_round, it * NI + i + 4)
                        nc.vector.tensor_scalar(t["b"][i % 2][:, :], t["a"][i % 2][:, :], MAGIC, col(GATE_STEP),
                                                ALU.subtract, ALU.mult).then_inc(g_val, 1)

                    def gated(i):
                        s, pr = it * 2 + i // NP, i % NP
                        c = t["c"][i % 2][:, :]
                        dve.wait_ge(g_y, it * NI + i + 1)
                        nc.vector.tensor_scalar(c, c, MAGIC + SIG_STEPS - 1, MAGIC, ALU.min, ALU.subtract
                                                ).then_inc(g_clip, 1)
                        dve.wait_ge(g_clip, it * NI + i + 1)
                        dst = t["p"][:, 2 * pr:2 * pr + 2, bass.ds(s * SC, SC)]
                        nc.vector.tensor_tensor(dst, c.rearrange("p (e n) -> p e n", e=2),
                                                t["b"][i % 2][:, :].rearrange("p (e n) -> p e n", e=2), ALU.mult
                                                ).then_inc(g_prod, 1)
                        wait_apart(dve, g_prod, it * NI + i + 3)
                        nc.vector.tensor_reduce(t["am"][:, i:i + 1], dst, mybir.AxisListType.XY, ALU.max,
                                                apply_absolute_value=True).then_inc(g_max, 1)

                    for i in range(NI):
                        gate_value(i)
                        if i >= 1:
                            gated(i - 1)
                    gated(NI - 1)
                    dve.wait_ge(g_max, it * NI + NI)
                    keep_max(NI, it + 2 * NS + 1)
                whole_max(3, ((3, 0, NI),))
                small(nc.vector.tensor_scalar(col(GATED_STEP), whole(3), 1.0 / SIG_STEPS, 1.0 / QMAX, ALU.mult, ALU.mult))
                small(nc.vector.tensor_scalar(col(GATED_STEP), col(GATED_STEP), TINY, None, ALU.max))
                small(nc.vector.reciprocal(col(GATED_BY), col(GATED_STEP)))
                small(nc.vector.tensor_scalar(col(GATED_BY), col(GATED_BY), 1.0 / SIG_STEPS, None, ALU.mult))
                dve.sem_inc(scaled, 1)
                dve.sem_inc(u_prod, 2)
                with dve.Fori(0, NS // 2, 1) as it:
                    def product_up(i):
                        s, pr = it * 2 + i // NP, i % NP
                        dst = t["p"][:, 2 * pr:2 * pr + 2, bass.ds(s * SC, SC)]
                        dve.wait_ge(p_round, it * NI + i + 1)
                        wait_apart(dve, u_int, it * NI + i + 1)
                        nc.vector.scalar_tensor_tensor(dst, t["b"][i % 2][:, :].rearrange("p (e n) -> p e n", e=2), MAGIC,
                                                       t["a"][i % 2][:, :].rearrange("p (e n) -> p e n", e=2),
                                                       ALU.subtract, ALU.mult).then_inc(u_prod, 1)
                        wait_apart(dve, u_prod, it * NI + i + 3)
                        nc.vector.tensor_reduce(t["am"][:, i:i + 1], dst, mybir.AxisListType.XY, ALU.max,
                                                apply_absolute_value=True).then_inc(u_max, 1)

                    for i in range(NI):
                        product_up(i)
                    dve.wait_ge(u_max, it * NI + NI)
                    keep_max(NI, it + 2 * NS + NS // 2 + 1)
                whole_max(4, ((4, 0, NI),))
                small(nc.vector.tensor_scalar(col(PROD_STEP), col(GATED_STEP), col(UP_STEP), None, ALU.mult))
                small(nc.vector.tensor_scalar(col(OUT_STEP), whole(4), col(PROD_STEP), 1.0 / QMAX, ALU.mult, ALU.mult))
                small(nc.vector.tensor_scalar(col(OUT_STEP), col(OUT_STEP), TINY, None, ALU.max))
                small(nc.vector.reciprocal(col(OUT_BY), col(OUT_STEP)))
                small(nc.vector.tensor_scalar(col(OUT_BY), col(OUT_BY), col(PROD_STEP), None, ALU.mult))
                dve.sem_inc(scaled, 1)
                dve.sem_inc(d_added, 2)
                with dve.Fori(0, NS // 2, 1) as it:
                    for j in range(2):
                        dve.wait_ge(o_round, it * 2 + j + 1)
                        o1 = t["o"][j][:, 0:NP, :].rearrange("p f n -> p (f n)")
                        nc.vector.tensor_scalar(o1, o1, MAGIC, None, ALU.subtract).then_inc(o_int_dve, 1)
                    for j in range(2):
                        wait_apart(dve, d_ps, it * 2 + j + 3)
                        for e in range(2):
                            xs = x_sb[:, bass.ds((it * 2 + j) * TS + 2 * e, 2), :]
                            o = psum[:, 2 * j + e, :].rearrange("p (m d) -> p m d", m=2)
                            ins = nc.vector.scalar_tensor_tensor(xs, o, col(OUT_STEP), xs, ALU.mult, ALU.add)
                        ins.then_inc(d_added, 1)

            return alloc, sync, gpsimd, tensor, scalar, vector

        def experts():
            NE, NX, FI = 8, 10, 352
            FTS = [(0, 128), (128, 128), (256, 96)]
            raw_loaded = [sem(f"xw_raw{i}") for i in range(2)]
            xw_ps, w_hi, w_lo, r_loaded, r_ps, r_sb = (sem("xw_ps"), sem("xw_hi"), sem("xw_lo"), sem("xr_loaded"),
                                                          sem("xr_ps"), sem("xr_sb"))
            xn_ready, xt_ps, xt_sb, xt_kept, l_ps, l_sb = (sem("xxn_ready"), sem("xxt_ps"), sem("xxt_sb"), sem("xxt_kept"),
                                                          sem("xl_ps"), sem("xl_sb"))
            step, exp_done, tri_set = sem("router_step"), sem("router_exp"), sem("tri_set")
            h_hi, h_lo = sem("xh_hi"), sem("xh_lo")
            gu_ps, silu_done, h_done, dn_ps, x_done = sem("gu_ps"), sem("silu_done"), sem("xh_done"), sem("dn_ps"), sem("x_done")

            def alloc(stack):
                t = {"wg": [sb(f"xwg{i}", [P, NX, KT, FI], F16, stack=stack) for i in (HI, LO)],
                     "wu": [sb(f"xwu{i}", [P, NX, KT, FI], F16, stack=stack) for i in (HI, LO)],
                     "wd": [sb(f"xwd{i}", [P, NX, 3, D], F16, stack=stack) for i in (HI, LO)],
                     "xt": [sb(f"xx_t{i}", [P, KT, B * S], F16, stack=stack) for i in (HI, LO)],
                     "wts": sb("expert_weights", [P, NT, NX], stack=stack)}
                with ExitStack() as inner:
                    t["raw_g"] = [sb(f"raw_g{i}", [P, 3, D], stack=inner) for i in range(2)]
                    t["raw_u"] = [sb(f"raw_u{i}", [P, 3, D], stack=inner) for i in range(2)]
                    t["raw_d"] = [sb(f"raw_d{i}", [P, 2, FI], stack=inner) for i in range(2)]
                    t["raw_r"] = sb("raw_r", [NE + 1, D], stack=inner)
                    t["wr"] = sb("router_w", [P, KT, NE + 1], stack=inner)
                    t["xn"] = sb("xxn", [P, TS, D], stack=inner)
                    t["xs"] = sb("xxt_step", [P, KT, SC], stack=inner)
                    for name, shape in (("lg", [P, NT, NE + 1]), ("mx", [P, NT]), ("ex", [P, NT, NE]), ("sg", [P, NT]),
                                        ("sum", [P, NT]), ("gt", [P, NT, NE, NE]), ("eq", [P, NT, NE, NE]),
                                        ("rank", [P, NT, NE]), ("tri", [P, NE, NE])):
                        t[name] = sb(f"router_{name}_", shape, stack=inner)
                with ExitStack() as inner:
                    t["s"] = [sb(f"silu{i}", [P, SC], stack=inner) for i in range(3)]
                    t["h"] = [sb(f"xh{i}", [P, SC], stack=inner) for i in range(3)]
                    t["hs"] = [[sb(f"xh_{i}_{part}", [P, 3, SC], F16, stack=inner) for part in (HI, LO)]
                               for i in range(2)]
                return t

            def sources(e):
                if e < NE:
                    gu = a["L1_ffn_experts_gate_up"][e]
                    return gu[0:FI, :], gu[FI:2 * FI, :], a["L1_ffn_experts_down"][e]
                lo = (e - NE) * FI
                return (a["L1_ffn_shared_gate_w"][lo:lo + FI, :], a["L1_ffn_shared_up_w"][lo:lo + FI, :],
                        a["L1_ffn_shared_down_w"][:, lo:lo + FI])

            def sync(sp, t):
                sp.dma_start(t["raw_r"][0:NE, :], a["L1_ffn_gate_w"]).then_inc(r_loaded, 16)
                sp.dma_start(t["raw_r"][NE:NE + 1, :], a["L1_ffn_shared_expert_gate_w"]).then_inc(r_loaded, 16)
                for e in range(NX):
                    if e >= 2:
                        sp.wait_ge(xw_ps, e - 1)
                    g, u, d = sources(e)
                    for raw, w in ((t["raw_g"], g), (t["raw_u"], u)):
                        sp.dma_start(raw[e % 2][:, 0:2, :], w[0:2 * P, :].rearrange("(t p) n -> p t n", p=P)
                                     ).then_inc(raw_loaded[e % 2], 16)
                        sp.dma_start(raw[e % 2][0:FI - 2 * P, 2, :], w[2 * P:FI, :]).then_inc(raw_loaded[e % 2], 16)
                    sp.dma_start(t["raw_d"][e % 2][:, :, :], d.rearrange("(t p) f -> p t f", p=P)
                                 ).then_inc(raw_loaded[e % 2], 16)
                out_t = tokens(out)
                with sp.Fori(0, NS, 1) as s:
                    sp.wait_ge(x_done, (s + 1) * NX + 1)
                    sp.dma_start(out_t[:, bass.ds(s * TS, TS), :], x_sb[:, bass.ds(s * TS, TS), :]).then_inc(out_stored, 16)
                sp.wait_ge(out_stored, 16 * NS)

            def gpsimd(pool, t):
                nc.gpsimd.memset(t["tri"][:, :, :], 1.0).then_inc(tri_set, 1)
                pool.wait_ge(tri_set, 1)
                nc.gpsimd.affine_select(out=t["tri"][:, :, :], in_=t["tri"][:, :, :], compare_op=ALU.is_ge, fill=0.0,
                                        base=-1, pattern=[[1, NE], [-1, NE]], channel_multiplier=0).then_inc(tri_set, 1)
                pool.sem_inc(h_lo, 3)
                with pool.Fori(0, NS, 1) as s:
                    for m in range(3 * NX):
                        e, f = m // 3, m % 3
                        n = FTS[f][1]
                        hs = t["hs"][e % 2]
                        pool.wait_ge(h_hi, s * 3 * NX + m + 1)
                        nc.gpsimd.tensor_tensor(hs[LO][0:n, f, :], t["h"][m % 3][0:n, :], hs[HI][0:n, f, :],
                                                ALU.subtract).then_inc(h_lo, 1)

            def tensor(pe, t):
                pe.wait_ge(r_loaded, 32)
                for kt in range(KT):
                    ins = nc.tensor.transpose(psum[:, 7, kt * 16:kt * 16 + NE + 1], t["raw_r"][:, kt * P:(kt + 1) * P],
                                              ident[0:NE + 1, 0:NE + 1])
                ins.then_inc(r_ps, 1)
                for e in range(NX):
                    pe.wait_ge(raw_loaded[e % 2], 80 * (e // 2 + 1))
                    if e >= 1:
                        pe.wait_ge(w_lo, e)
                    for b0, raw in ((0, t["raw_g"]), (2, t["raw_u"])):
                        for kt in range(KT):
                            for f, (lo, n) in enumerate(FTS):
                                nc.tensor.transpose(psum[:, b0 + kt, lo:lo + n], raw[e % 2][0:n, f, kt * P:(kt + 1) * P],
                                                    ident[0:n, 0:n])
                    for f, (lo, n) in enumerate(FTS):
                        for ot in range(2):
                            ins = nc.tensor.transpose(psum[0:n, 4 + f // 2, (f % 2) * D + ot * P:(f % 2) * D + (ot + 1) * P],
                                                      t["raw_d"][e % 2][:, ot, lo:lo + n], ident[:, :])
                    ins.then_inc(xw_ps, 1)
                pe.wait_ge(w_lo, NX)
                pe.wait_ge(r_sb, 1)
                pe.sem_inc(l_ps, 1)
                pe.sem_inc(xt_ps, 1)
                with pe.Fori(0, NS, 1) as s:
                    pe.wait_ge(xn_ready, s + 1)
                    pe.wait_ge(xt_sb, s + 1)
                    for kt in range(KT):
                        for j in range(TS):
                            ins = nc.tensor.transpose(psum[:, kt, j * P:(j + 1) * P],
                                                      t["xn"][:, j, kt * P:(kt + 1) * P], ident[:, :])
                    ins.then_inc(xt_ps, 1)
                    pe.wait_ge(xt_sb, s + 2)
                    pe.wait_ge(l_sb, s + 1)
                    for j in range(TS):
                        for kt in range(KT):
                            ins = nc.tensor.matmul(psum[:, 2, j * 16:j * 16 + NE + 1], t["xs"][:, kt, j * P:(j + 1) * P],
                                                   t["wr"][:, kt, :], start=(kt == 0), stop=(kt == KT - 1))
                    ins.then_inc(l_ps, 1)
                pe.wait_ge(l_sb, NS + 1)
                pe.wait_ge(xt_kept, NS + 1)
                pe.sem_inc(dn_ps, 2)
                with pe.Fori(0, NS, 1) as s:
                    def gate_up(e):
                        for f, (lo, n) in enumerate(FTS):
                            m = e * 3 + f
                            pe.wait_ge(h_done, s * 3 * NX + m + 1)
                            for i, w in enumerate((t["wg"], t["wu"])):
                                for kt in range(KT):
                                    for k, (pw, px) in enumerate(SPLIT):
                                        ins = nc.tensor.matmul(psum[0:n, 2 * (m % 3) + i, :], w[pw][:, e, kt, lo:lo + n],
                                                               t["xt"][px][:, kt, bass.ds(s * SC, SC)],
                                                               start=(kt == 0 and k == 0), stop=(kt == KT - 1 and k == 2))
                            ins.then_inc(gu_ps, 1)

                    def down(e):
                        pe.wait_ge(h_lo, s * 3 * NX + e * 3 + 3 + 3)
                        pe.wait_ge(x_done, s * NX + e + 1)
                        for j in range(TS):
                            for f, (lo, n) in enumerate(FTS):
                                for k, (ph, pw) in enumerate(SPLIT):
                                    ins = nc.tensor.matmul(psum[:, 6 + j // 2, (j % 2) * D:(j % 2 + 1) * D],
                                                           t["hs"][e % 2][ph][0:n, f, j * P:(j + 1) * P],
                                                           t["wd"][pw][0:n, e, f, :],
                                                           start=(f == 0 and k == 0), stop=(f == 2 and k == 2))
                        ins.then_inc(dn_ps, 1)

                    for e in range(NX):
                        gate_up(e)
                        if e >= 1:
                            down(e - 1)
                    down(NX - 1)

            def scalar(act, t):
                for e in range(NX):
                    act.wait_ge(xw_ps, e + 1)
                    nc.scalar.mul(t["wd"][HI][:, e, 0:2, :].rearrange("p f n -> p (f n)"), psum[:, 4, :], W_UP)
                    nc.scalar.mul(t["wd"][HI][0:FI - 2 * P, e, 2, :], psum[0:FI - 2 * P, 5, 0:D], W_UP)
                    nc.scalar.mul(t["wg"][HI][:, e, :, :], psum[:, 0:2, 0:FI], W_UP)
                    nc.scalar.mul(t["wu"][HI][:, e, :, :], psum[:, 2:4, 0:FI], W_UP).then_inc(w_hi, 1)
                act.sem_inc(xt_sb, 1)
                with act.Fori(0, NS, 1) as s:
                    act.wait_ge(xt_ps, s + 2)
                    act.wait_ge(xt_kept, s + 1)
                    act.wait_ge(l_ps, s + 1)
                    nc.scalar.copy(t["xs"][:, :, :], psum[:, 0:2, :])
                    nc.scalar.copy(t["xt"][HI][:, :, bass.ds(s * SC, SC)], psum[:, 0:2, :]).then_inc(xt_sb, 1)
                act.wait_ge(step, 2)
                nc.scalar.activation(t["ex"][:, :, :], t["ex"][:, :, :], ACT.Exp)
                nc.scalar.activation(t["sg"][:, :], t["lg"][:, :, NE], ACT.Exp, scale=-1.0).then_inc(exp_done, 1)

                def high_part(s, m):
                    e, f = m // 3, m % 3
                    n = FTS[f][1]
                    act.wait_ge(h_done, s * 3 * NX + m + 4)
                    if f == 0:
                        act.wait_ge(dn_ps, s * NX + e + 1)
                    nc.scalar.copy(t["hs"][e % 2][HI][0:n, f, :], t["h"][m % 3][0:n, :]).then_inc(h_hi, 1)

                with act.Fori(0, NS, 1) as s:
                    for m in range(3 * NX):
                        n = FTS[m % 3][1]
                        act.wait_ge(gu_ps, s * 3 * NX + m + 1)
                        act.wait_ge(h_done, s * 3 * NX + m + 1)
                        nc.scalar.activation(t["s"][m % 3][0:n, :], psum[0:n, 2 * (m % 3), :], ACT.Silu,
                                             scale=1.0 / W_UP).then_inc(silu_done, 1)
                        if m >= 1:
                            high_part(s, m - 1)
                    high_part(s, 3 * NX - 1)

            def vector(dve, t):
                dve.wait_ge(r_ps, 1)
                nc.vector.tensor_copy(t["wr"][:, :, :], psum[:, 7, 0:32].rearrange("p (k n) -> p k n", k=2)[:, :, 0:NE + 1]
                                      ).then_inc(r_sb, 1)
                for e in range(NX):
                    dve.wait_ge(w_hi, e + 1)
                    n = FI - 2 * P
                    for dst, part, src in (
                            (t["wd"][LO][:, e, 0:2, :].rearrange("p f n -> p (f n)"),
                             t["wd"][HI][:, e, 0:2, :].rearrange("p f n -> p (f n)"), psum[:, 4, :]),
                            (t["wd"][LO][0:n, e, 2, :], t["wd"][HI][0:n, e, 2, :], psum[0:n, 5, 0:D]),
                            (t["wg"][LO][:, e, :, :], t["wg"][HI][:, e, :, :], psum[:, 0:2, 0:FI]),
                            (t["wu"][LO][:, e, :, :], t["wu"][HI][:, e, :, :], psum[:, 2:4, 0:FI])):
                        ins = nc.vector.scalar_tensor_tensor(dst, src, W_UP, part, ALU.mult, ALU.subtract)
                    ins.then_inc(w_lo, 1)
                dve.sem_inc(l_sb, 1)
                dve.sem_inc(xt_kept, 1)
                with dve.Fori(0, NS, 1) as s:
                    dve.wait_ge(xt_ps, s + 1)
                    for j in range(TS):
                        ins = nc.vector.tensor_scalar(t["xn"][:, j, :], x_sb[:, s * TS + j, :],
                                                      mv[:, s * TS + j, 0:1], rstd[:, bass.ds(s * TS + j, 1)],
                                                      ALU.subtract, ALU.mult)
                    ins.then_inc(xn_ready, 1)
                    dve.wait_ge(xt_sb, s + 2)
                    rows = bass.ds(s * SC, SC)
                    nc.vector.tensor_tensor(t["xt"][LO][:, :, rows], t["xs"][:, :, :], t["xt"][HI][:, :, rows],
                                            ALU.subtract).then_inc(xt_kept, 1)
                    wait_apart(dve, l_ps, s + 2)
                    nc.vector.tensor_copy(t["lg"][:, bass.ds(s * TS, TS), :],
                                          psum[:, 2, 0:64].rearrange("p (j n) -> p j n", j=TS)[:, :, 0:NE + 1]
                                          ).then_inc(l_sb, 1)
                dve.wait_ge(l_sb, NS + 1)
                lg = t["lg"][:, :, 0:NE]
                steps = [0]

                def small(ins):
                    steps[0] += 1
                    ins.then_inc(step, 1)
                    dve.wait_ge(step, steps[0])

                small(nc.vector.tensor_reduce(t["mx"][:, :], lg, X, ALU.max))
                small(nc.vector.tensor_tensor(t["ex"][:, :, :], lg, t["mx"][:, :].unsqueeze(2).broadcast_to((P, NT, NE)),
                                              ALU.subtract))
                dve.wait_ge(exp_done, 1)
                small(nc.vector.tensor_reduce(t["sum"][:, :], t["ex"][:, :, :], X, ALU.add))
                small(nc.vector.reciprocal(t["mx"][:, :], t["sum"][:, :]))
                small(nc.vector.tensor_tensor(t["ex"][:, :, :], t["ex"][:, :, :],
                                              t["mx"][:, :].unsqueeze(2).broadcast_to((P, NT, NE)), ALU.mult))
                pair = (P, NT, NE, NE)
                of_j = t["ex"][:, :, :].unsqueeze(2).broadcast_to(pair)
                of_i = t["ex"][:, :, :].unsqueeze(3).broadcast_to(pair)
                small(nc.vector.tensor_tensor(t["gt"][:, :, :, :], of_j, of_i, ALU.is_gt))
                small(nc.vector.tensor_tensor(t["eq"][:, :, :, :], of_j, of_i, ALU.is_equal))
                dve.wait_ge(tri_set, 2)
                eq = t["eq"][:, :, :, :].rearrange("p t i j -> p t (i j)")
                small(nc.vector.tensor_tensor(eq, eq, t["tri"][:, :, :].rearrange("p i j -> p (i j)").unsqueeze(1)
                                              .broadcast_to((P, NT, NE * NE)), ALU.mult))
                small(nc.vector.tensor_tensor(t["gt"][:, :, :, :], t["gt"][:, :, :, :], t["eq"][:, :, :, :], ALU.add))
                small(nc.vector.tensor_reduce(t["rank"][:, :, :], t["gt"][:, :, :, :], X, ALU.add))
                small(nc.vector.tensor_scalar(t["rank"][:, :, :], t["rank"][:, :, :], 1.5, None, ALU.is_lt))
                small(nc.vector.tensor_tensor(t["wts"][:, :, 0:NE], t["ex"][:, :, :], t["rank"][:, :, :], ALU.mult))
                small(nc.vector.tensor_scalar(t["sum"][:, :], t["sg"][:, :], 1.0, None, ALU.add))
                small(nc.vector.reciprocal(t["mx"][:, :], t["sum"][:, :]))
                small(nc.vector.tensor_copy(t["wts"][:, :, NE:NX], t["mx"][:, :].unsqueeze(2).broadcast_to((P, NT, 2))))
                small(nc.vector.tensor_scalar(t["wts"][:, :, :], t["wts"][:, :, :], 1.0 / W_UP, None, ALU.mult))
                dve.sem_inc(h_done, 3)
                dve.sem_inc(x_done, 1)
                with dve.Fori(0, NS, 1) as s:
                    def gated(e):
                        for f, (lo, n) in enumerate(FTS):
                            m = e * 3 + f
                            dve.wait_ge(silu_done, s * 3 * NX + m + 1)
                            dve.wait_ge(h_lo, s * 3 * NX + m + 1)
                            nc.vector.scalar_tensor_tensor(t["h"][m % 3][0:n, :], psum[0:n, 2 * (m % 3) + 1, :],
                                                           1.0 / W_UP, t["s"][m % 3][0:n, :], ALU.mult, ALU.mult
                                                           ).then_inc(h_done, 1)

                    def add(e):
                        wait_apart(dve, dn_ps, s * NX + e + 3)
                        for j in range(TS):
                            xs = x_sb[:, s * TS + j, :]
                            ins = nc.vector.scalar_tensor_tensor(xs, psum[:, 6 + j // 2, (j % 2) * D:(j % 2 + 1) * D],
                                                                 t["wts"][:, s * TS + j, e:e + 1], xs, ALU.mult, ALU.add)
                        ins.then_inc(x_done, 1)

                    for e in range(NX):
                        gated(e)
                        if e >= 1:
                            add(e - 1)
                    add(NX - 1)

            return alloc, sync, gpsimd, tensor, scalar, vector

        stats0_v, stats0_s = norm_stats(0)
        proj0 = projections(0, a["L0_xattn_Wq"], a["L0_xattn_Wk"], a["L0_xattn_Wv"],
                            a["L0_xattn_bq"], a["L0_xattn_bk"], a["L0_xattn_bv"])
        rel_alloc, rel_alloc_raw, rel_sync, rel_pool, rel_pe, rel_dve, rel_ready = relative_tables()
        with ExitStack() as rel_stack:
            rel_t = rel_alloc(rel_stack)
            with ExitStack() as stack:
                rel_alloc_raw(stack, rel_t)
                proj0_t = proj0[0](stack)
            att0 = attention(0, True, rel_t, rel_ready)
            with ExitStack() as stack:
                att0_t = att0[0](stack)
        fc0 = merge_heads(0, a["L0_xattn_W_fc"], False, (h_dr, r_dr), a["L0_xattn_b_fc"])
        with ExitStack() as stack:
            fc0_t = fc0[0](stack)
        stats1_v, stats1_s = norm_stats(1)
        ffn0 = quantised_ffn()
        with ExitStack() as stack:
            ffn0_t = ffn0[0](stack)
        stats2_v, stats2_s = norm_stats(2)
        proj1 = projections(1, a["L1_xattn_Wq"], a["L1_xattn_Wk"], a["L1_xattn_Wv"])
        with ExitStack() as stack:
            proj1_t = proj1[0](stack)
        att1 = attention(1, False)
        with ExitStack() as stack:
            att1_t = att1[0](stack)
        fc1 = merge_heads(1, a["L1_xattn_Wout"], True, (h_dr,))
        with ExitStack() as stack:
            fc1_t = fc1[0](stack)
        stats3_v, stats3_s = norm_stats(3)
        moe = experts()
        with ExitStack() as stack:
            moe_t = moe[0](stack)

        kept = {"phase_end", "out_stored", "x_loaded", "consts_set"}
        blk = ctx.enter_context(nc.Block())

        @blk.sync
        def _(sp):
            x_t = tokens(a["x"])
            for i in range(4):
                sp.dma_start(x_sb[:, i * 8:(i + 1) * 8, :], x_t[:, i * 8:(i + 1) * 8, :]).then_inc(x_loaded, 16)
            rel_sync(sp, rel_t)
            proj0[1](sp, proj0_t)
            phase_barrier(sp, 0)
            att0[1](sp, att0_t)
            phase_barrier(sp, 1)
            fc0[1](sp, fc0_t)
            phase_barrier(sp, 2)
            phase_barrier(sp, 3)
            ffn0[1](sp, ffn0_t)
            phase_barrier(sp, 4)
            proj1[1](sp, proj1_t)
            phase_barrier(sp, 5)
            att1[1](sp, att1_t)
            phase_barrier(sp, 6)
            fc1[1](sp, fc1_t)
            phase_barrier(sp, 7)
            moe[1](sp, moe_t)

        @blk.gpsimd
        def _(pool):
            nc.gpsimd.memset(ident[:, :], 0.0)
            nc.gpsimd.memset(block[:, :], 1.0)
            nc.gpsimd.memset(block_rev[:, :], 1.0)
            nc.gpsimd.memset(eps[:, :], EPS).then_inc(consts_set, 1)
            pool.wait_ge(consts_set, 1)
            nc.gpsimd.affine_select(out=ident[:, :], in_=ident[:, :], compare_op=ALU.not_equal, fill=1.0, base=0,
                                    pattern=[[-1, P]], channel_multiplier=1)
            nc.gpsimd.affine_select(out=block[:, :], in_=block[:, :], compare_op=ALU.is_ge, fill=0.0, base=0,
                                    pattern=[[-16, 8]], channel_multiplier=1)
            nc.gpsimd.affine_select(out=block_rev[:, :], in_=block_rev[:, :], compare_op=ALU.is_ge, fill=0.0,
                                    base=-112, pattern=[[16, 8]], channel_multiplier=1).then_inc(consts_set, 1)
            pool.wait_ge(consts_set, 2)
            nc.gpsimd.affine_select(out=block[:, :], in_=block[:, :], compare_op=ALU.is_ge, fill=0.0, base=15,
                                    pattern=[[16, 8]], channel_multiplier=-1)
            nc.gpsimd.affine_select(out=block_rev[:, :], in_=block_rev[:, :], compare_op=ALU.is_ge, fill=0.0,
                                    base=127, pattern=[[-16, 8]], channel_multiplier=-1).then_inc(consts_set, 1)
            rel_pool(pool, rel_t)
            phase_barrier(pool, 0)
            att0[2](pool, att0_t)
            phase_barrier(pool, 1)
            phase_barrier(pool, 2)
            for name, used in semaphores.items():
                if name not in kept:
                    pool.sem_clear(used)
            phase_barrier(pool, 3)
            ffn0[2](pool, ffn0_t)
            phase_barrier(pool, 4)
            phase_barrier(pool, 5)
            att1[2](pool, att1_t)
            phase_barrier(pool, 6)
            phase_barrier(pool, 7)
            moe[2](pool, moe_t)

        @blk.scalar
        def _(act):
            act.wait_ge(consts_set, 3)
            stats0_s(act)
            proj0[3](act, proj0_t)
            phase_barrier(act, 0)
            att0[4](act, att0_t)
            phase_barrier(act, 1)
            phase_barrier(act, 2)
            phase_barrier(act, 3)
            stats1_s(act)
            ffn0[4](act, ffn0_t)
            phase_barrier(act, 4)
            stats2_s(act)
            proj1[3](act, proj1_t)
            phase_barrier(act, 5)
            att1[4](act, att1_t)
            phase_barrier(act, 6)
            phase_barrier(act, 7)
            stats3_s(act)
            moe[4](act, moe_t)

        @blk.vector
        def _(dve):
            dve.wait_ge(x_loaded, 64)
            dve.wait_ge(consts_set, 3)
            rel_dve(dve, rel_t)
            stats0_v(dve)
            proj0[4](dve, proj0_t)
            phase_barrier(dve, 0)
            att0[5](dve, att0_t)
            phase_barrier(dve, 1)
            fc0[3](dve, fc0_t)
            phase_barrier(dve, 2)
            phase_barrier(dve, 3)
            stats1_v(dve)
            ffn0[5](dve, ffn0_t)
            phase_barrier(dve, 4)
            stats2_v(dve)
            proj1[4](dve, proj1_t)
            phase_barrier(dve, 5)
            att1[5](dve, att1_t)
            phase_barrier(dve, 6)
            fc1[3](dve, fc1_t)
            phase_barrier(dve, 7)
            stats3_v(dve)
            moe[5](dve, moe_t)

        @blk.tensor
        def _(pe):
            pe.wait_ge(consts_set, 3)
            rel_pe(pe, rel_t)
            proj0[2](pe, proj0_t)
            phase_barrier(pe, 0)
            att0[3](pe, att0_t)
            phase_barrier(pe, 1)
            fc0[2](pe, fc0_t)
            phase_barrier(pe, 2)
            phase_barrier(pe, 3)
            ffn0[3](pe, ffn0_t)
            phase_barrier(pe, 4)
            proj1[2](pe, proj1_t)
            phase_barrier(pe, 5)
            att1[3](pe, att1_t)
            phase_barrier(pe, 6)
            fc1[2](pe, fc1_t)
            phase_barrier(pe, 7)
            moe[3](pe, moe_t)


_INS = ['x', 'ctx_1024', 'mask_SxS2_ik1', 'L0_xattn_Wq', 'L0_xattn_bq', 'L0_xattn_Wk', 'L0_xattn_bk', 'L0_xattn_Wv',
        'L0_xattn_bv', 'L0_xattn_pos_k', 'L0_xattn_pos_v', 'L0_xattn_W_fc', 'L0_xattn_b_fc', 'L0_ffn_w_gate',
        'L0_ffn_w_up', 'L0_ffn_w_down', 'L1_xattn_Wv', 'L1_xattn_Wk', 'L1_xattn_Wq', 'L1_xattn_Wout',
        'L1_ffn_gate_w', 'L1_ffn_experts_gate_up', 'L1_ffn_experts_down', 'L1_ffn_shared_gate_w',
        'L1_ffn_shared_up_w', 'L1_ffn_shared_down_w', 'L1_ffn_shared_expert_gate_w']


def kernel(**inputs):
    import numpy as _np
    import concourse.bacc as _bacc
    from concourse import mybir as _mybir
    from concourse.bass_utils import run_bass_kernel_spmd as _run

    nc = _bacc.Bacc("TRN2", target_bir_lowering=False, num_devices=1)
    arrays, aps = {}, {}
    for name in _INS:
        arr = _np.ascontiguousarray(inputs[name])
        arrays[f"in_{name}"] = arr
        aps[name] = nc.dram_tensor(f"in_{name}", arr.shape, _mybir.dt.from_np(arr.dtype), kind="ExternalInput").ap()
    out = nc.dram_tensor("out_0", (16, 256, 256), _mybir.dt.float32, kind="ExternalOutput").ap()
    build(nc, aps, out)
    r = _run(nc, [arrays], core_ids=[0])
    return r.results[0]["out_0"]
```

```python
from contextlib import ExitStack

import concourse.bass as bass
from concourse import mybir

ALU = mybir.AluOpType
ACT = mybir.ActivationFunctionType
F32 = mybir.dt.float32
F16 = mybir.dt.float16
I32 = mybir.dt.int32
X = mybir.AxisListType.X
ABSMAX = bass.bass_isa.ReduceOp.absmax

P = 128
B, S, D = 16, 256, 256
H, DH = 16, 16
K = 64
KT = D // P
NT = B * S // P
SC = 512
NS = B * S // SC
TS = SC // P
EPS = 1e-5
SCALE = DH ** -0.5
MASKED = 1e-20
IN = 8
GN = S // IN
GC = 4
NC = GN // GC
NB2 = 2 * NC
QBLOCK = 32
W_QMAX = 7.0
QMAX = 32767.0
SIG_STEPS = 65536.0
TINY = 1e-12
MAGIC = 1.5 * 2.0 ** 23
X_STEP, X_BY, GATE_STEP, GATE_BY, UP_STEP, UP_BY, GATED_STEP, GATED_BY, PROD_STEP, OUT_STEP, OUT_BY = range(11)
ENGINES = 5
HI, LO = 0, 1
SPLIT = ((HI, HI), (HI, LO), (LO, HI))
W_UP = 64.0
A_UP = 1024.0


def tokens(ap):
    return ap.rearrange("b s d -> (b s) d").rearrange("(t p) d -> p t d", p=P)


def build(nc, a, out):
    with ExitStack() as ctx:
        def sb(name, shape, dt=F32, stack=ctx):
            return stack.enter_context(nc.sbuf_tensor(name, shape, dt))

        semaphores = {}

        def sem(name):
            if name not in semaphores:
                semaphores[name] = ctx.enter_context(nc.semaphore(name))
            return semaphores[name]

        def dram(name, shape, dt=F32):
            return nc.dram_tensor(name, shape, dt, kind="Internal").ap()

        x_sb = sb("x_sb", [P, NT, D])
        ident = sb("ident", [P, P])
        block = sb("block16", [P, 8])
        block_rev = sb("block16_rev", [P, 8])
        stats = sb("stats", [P, NT, 6])
        mv = sb("mv", [P, NT, 2])
        sd = sb("sd", [P, NT])
        rstd = sb("rstd", [P, NT])
        eps = sb("eps", [P, 1])
        psum = ctx.enter_context(nc.psum_tensor("psum", [P, 8, 512], F32))

        q0_dr = dram("q0_dr", [B, H * DH, S, 2], F16)
        q1_dr = [dram(f"q1_dr{i}", [B, H * DH, S], F16) for i in (HI, LO)]
        k_dr = [dram(f"k_dr{i}", [B, H * DH, S], F16) for i in (HI, LO)]
        v_dr = dram("v_dr", [B * S, H * DH])
        h_dr = dram("h_dr", [B, H * DH, S])
        r_dr = dram("r_dr", [B, H * DH, S])
        extv_dr = dram("extv_dr", [2 * S, DH])

        phase_end, phase_begun = sem("phase_end"), sem("phase_begun")
        x_loaded = sem("x_loaded")
        consts_set = sem("consts_set")
        out_stored = sem("out_stored")

        def phase_barrier(eng, k):
            eng.drain().then_inc(phase_end, 1)
            eng.wait_ge(phase_end, ENGINES * (k + 1))
            eng.sem_inc(phase_begun, 1)

        apart = {}

        def wait_apart(eng, semaphore, value):
            if eng not in apart:
                apart[eng] = sem(f"apart_{len(apart)}")
            eng.wait_ge(semaphore, value)
            eng.sem_inc(apart[eng], 1)

        def norm_stats(n):
            stats_done, mv_done = sem("stats_done"), sem("mv_done")
            sd_done, rstd_done = sem("sd_done"), sem("rstd_done")

            def vector(dve):
                with dve.Fori(0, NT // 4, 1) as t:
                    for j in range(4):
                        ins = nc.vector.bn_stats(stats[:, t * 4 + j, :], x_sb[:, t * 4 + j, :])
                    ins.then_inc(stats_done, 1)
                dve.wait_ge(stats_done, NT // 4)
                for t in range(NT):
                    ins = nc.vector.bn_aggr(mv[:, t, :], stats[:, t, :])
                ins.then_inc(mv_done, 1)
                dve.wait_ge(sd_done, 1)
                nc.vector.reciprocal(rstd[:, :], sd[:, :]).then_inc(rstd_done, 1)
                dve.wait_ge(rstd_done, 1)

            def scalar(act):
                act.wait_ge(mv_done, 1)
                nc.scalar.activation(sd[:, :], mv[:, :, 1], ACT.Sqrt, bias=eps[:, 0:1]).then_inc(sd_done, 1)

            return vector, scalar

        def projections(n, wq_ap, wk_ap, wv_ap, bq_ap=None, bk_ap=None, bv_ap=None):
            biased = bq_ap is not None
            xn_ready, ctx_loaded, w_loaded = sem("xn_ready"), sem("ctx_loaded"), sem("w_loaded")
            xt_ps, ct_ps, xt_sb, ct_sb = sem("xt_ps"), sem("ct_ps"), sem("xt_sb"), sem("ct_sb")
            q_ps, k_ps, v_ps = sem("q_ps"), sem("k_ps"), sem("v_ps")
            q_out, k_out, v_out = sem("q_out"), sem("k_out"), sem("v_out")
            q_stored, k_stored, v_stored = sem("q_stored"), sem("k_stored"), sem("v_stored")
            w_ps, w_sb_done, bq_scaled = sem("w_ps"), sem("w_sb_done"), sem("bq_scaled")
            q_hi, k_hi = sem("q_hi"), sem("k_hi")
            w_hi, xt_hi, ct_hi = sem("w_hi"), sem("xt_hi"), sem("ct_hi")
            n_w = 9 if biased else 3
            q_dmas = 2 if biased else 4

            def alloc(stack):
                t = {}
                for name, shape in (("w_raw", [P, 3, KT, D]), ("bqk", [P, 2, 2]),
                                    ("bv", [P, D]), ("xn", [P, TS, D]), ("cin", [P, TS, D]),
                                    ("qo", [P, 2, SC]), ("ko", [P, 2, SC]), ("vo", [P, TS, D])):
                    t[name] = sb(f"{name}{n}", shape, stack=stack)
                for name, shape in (("w", [P, 3, KT, D]), ("xt", [P, KT, SC]), ("ct", [P, KT, SC])):
                    t[name] = [sb(f"{name}{n}_{i}", shape, F16, stack=stack) for i in (HI, LO)]
                if biased:
                    t["q_both"] = sb(f"q_both{n}", [P, 2, SC, 2], F16, stack=stack)
                    t["qs"] = [t["q_both"][:, :, :, i] for i in (HI, LO)]
                else:
                    t["qs"] = [sb(f"q_part{n}_{i}", [P, 2, SC], F16, stack=stack)[:, :, :] for i in (HI, LO)]
                t["ks"] = [sb(f"k_part{n}_{i}", [P, 2, SC], F16, stack=stack)[:, :, :] for i in (HI, LO)]
                return t

            def sync(sp, t):
                if biased:
                    for i, w in enumerate((wq_ap, wk_ap, wv_ap)):
                        for kt in range(KT):
                            sp.dma_start(t["w_raw"][:, i, kt, :].rearrange("p (h d) -> p h d", h=H),
                                         w[:, kt * P:(kt + 1) * P, :].rearrange("h p d -> p h d")
                                         ).then_inc(w_loaded, 16)
                    for i, v in enumerate((bq_ap, bk_ap)):
                        sp.dma_start(t["bqk"][:, i, :], v.rearrange("(t h) d -> (h d) t", t=2),
                                     allow_slow_non_contiguous=True).then_inc(w_loaded, 16)
                    sp.dma_start(t["bv"][:, :], bv_ap.rearrange("h d -> (h d)").partition_broadcast(P)
                                 ).then_inc(w_loaded, 16)
                else:
                    for i, w in enumerate((wq_ap, wk_ap, wv_ap)):
                        sp.dma_start(t["w_raw"][:, i, :, :],
                                     w.rearrange("(t p) n -> p t n", p=P)).then_inc(w_loaded, 16)
                ctx_t = tokens(a["ctx_1024"])
                for granted in (q_stored, k_stored, v_stored):
                    sp.sem_inc(granted, 16)
                q0_t = q0_dr.rearrange("b (t p) s e -> p t b (s e)", p=P)
                q1_t = [q.rearrange("b (t p) s -> p t b s", p=P) for q in q1_dr]
                k_t = [k.rearrange("b (t p) s -> p t b s", p=P) for k in k_dr]
                v_t = v_dr.rearrange("(t p) d -> p t d", p=P)
                sp.dma_start(t["cin"][:, :, :], ctx_t[:, 0:TS, :]).then_inc(ctx_loaded, 16)
                with sp.Fori(0, NS, 1) as s:
                    sp.wait_ge(ct_ps, s + 1)
                    nxt = (s + 1) % NS
                    sp.dma_start(t["cin"][:, :, :], ctx_t[:, bass.ds(nxt * TS, TS), :]).then_inc(ctx_loaded, 16)
                    sp.wait_ge(q_out, s + 1)
                    for hh in range(2):
                        if biased:
                            sp.dma_start(q0_t[:, hh, bass.ds(2 * s, 2), :],
                                         t["q_both"][:, hh, :, :].rearrange("p (b s) e -> p b (s e)", b=2)
                                         ).then_inc(q_stored, 16)
                        else:
                            for i in (HI, LO):
                                sp.dma_start(q1_t[i][:, hh, bass.ds(2 * s, 2), :],
                                             t["qs"][i][:, hh, :].rearrange("p (b s) -> p b s", b=2)
                                             ).then_inc(q_stored, 16)
                    sp.wait_ge(v_out, s + 2)
                    sp.dma_start(v_t[:, bass.ds(s * TS, TS), :], t["vo"][:, :, :]).then_inc(v_stored, 16)
                    sp.wait_ge(k_out, s + 2)
                    for hh in range(2):
                        for i in (HI, LO):
                            sp.dma_start(k_t[i][:, hh, bass.ds(2 * s, 2), :],
                                         t["ks"][i][:, hh, :].rearrange("p (b s) -> p b s", b=2)
                                         ).then_inc(k_stored, 16)
                sp.wait_ge(q_stored, 16 * q_dmas * NS + 16)
                sp.wait_ge(k_stored, 64 * NS + 16)
                sp.wait_ge(v_stored, 16 * NS + 16)
                sp.wait_ge(ctx_loaded, 16 * (NS + 1))

            def tensor(pe, t):
                def feature_major(which, src):
                    for hh in range(2):
                        for kt in range(KT):
                            for k, (pw, px) in enumerate(SPLIT):
                                ins = nc.tensor.matmul(psum[:, 4 + hh, :], t["w"][pw][:, which, kt, hh * P:(hh + 1) * P],
                                                       src[px][:, kt, :], start=(kt == 0 and k == 0),
                                                       stop=(kt == KT - 1 and k == 2))
                    return ins

                pe.wait_ge(w_loaded, 16 * n_w)
                if not biased:
                    for i in range(3):
                        for ot in range(2):
                            for kt in range(KT):
                                ins = nc.tensor.transpose(psum[:, i * 2 + kt, ot * P:(ot + 1) * P],
                                                          t["w_raw"][:, i, ot, kt * P:(kt + 1) * P], ident[:, :])
                    ins.then_inc(w_ps, 1)
                pe.wait_ge(w_sb_done, 1)
                for granted in (xt_ps, q_ps, k_ps):
                    pe.sem_inc(granted, 1)
                with pe.Fori(0, NS, 1) as s:
                    pe.wait_ge(xn_ready, s + 1)
                    for kt in range(KT):
                        for j in range(TS):
                            ins = nc.tensor.transpose(psum[:, kt, j * P:(j + 1) * P],
                                                      t["xn"][:, j, kt * P:(kt + 1) * P], ident[:, :])
                    ins.then_inc(xt_ps, 1)
                    pe.wait_ge(ctx_loaded, 16 * (s + 1))
                    for kt in range(KT):
                        for j in range(TS):
                            ins = nc.tensor.transpose(psum[:, 2 + kt, j * P:(j + 1) * P],
                                                      t["cin"][:, j, kt * P:(kt + 1) * P], ident[:, :])
                    ins.then_inc(ct_ps, 1)
                    pe.wait_ge(xt_sb, s + 1)
                    pe.wait_ge(k_hi, s + 1)
                    feature_major(0, t["xt"]).then_inc(q_ps, 1)
                    pe.wait_ge(ct_sb, s + 1)
                    pe.wait_ge(v_out, s + 1)
                    for j in range(TS):
                        for kt in range(KT):
                            for k, (pc, pw) in enumerate(SPLIT):
                                ins = nc.tensor.matmul(psum[:, 6 + j // 2, (j % 2) * D:(j % 2 + 1) * D],
                                                       t["ct"][pc][:, kt, j * P:(j + 1) * P], t["w"][pw][:, 2, kt, :],
                                                       start=(kt == 0 and k == 0), stop=(kt == KT - 1 and k == 2))
                    ins.then_inc(v_ps, 1)
                    pe.wait_ge(q_hi, s + 1)
                    feature_major(1, t["ct"]).then_inc(k_ps, 1)

            def scalar(act, t):
                if biased:
                    act.wait_ge(w_loaded, 16 * n_w)
                    nc.scalar.mul(t["bqk"][:, 0, :], t["bqk"][:, 0, :], SCALE).then_inc(bq_scaled, 1)
                    act.wait_ge(bq_scaled, 1)
                    ins = nc.scalar.mul(t["w"][HI][:, :, :, :], t["w_raw"][:, :, :, :], W_UP)
                else:
                    act.wait_ge(w_ps, 1)
                    ins = nc.scalar.mul(t["w"][HI][:, :, :, :].rearrange("p i k n -> p (i k) n"), psum[:, 0:6, 0:D], W_UP)
                ins.then_inc(w_hi, 1)
                act.sem_inc(k_hi, 1)

                def evacuate(whole, high, which, scale, done):
                    for dst in (whole, high):
                        for hh in range(2):
                            src = psum[:, 4 + hh, :]
                            if biased:
                                ins = nc.scalar.activation(dst[:, hh, :], src, ACT.Identity,
                                                           bias=t["bqk"][:, which, hh:hh + 1], scale=scale)
                            else:
                                ins = nc.scalar.mul(dst[:, hh, :], src, scale)
                    ins.then_inc(done, 1)

                with act.Fori(0, NS, 1) as s:
                    act.wait_ge(xt_ps, s + 2)
                    act.wait_ge(q_ps, s + 1)
                    nc.scalar.copy(t["xt"][HI][:, :, :], psum[:, 0:2, :]).then_inc(xt_hi, 1)
                    act.wait_ge(ct_ps, s + 1)
                    act.wait_ge(k_ps, s + 1)
                    nc.scalar.copy(t["ct"][HI][:, :, :], psum[:, 2:4, :]).then_inc(ct_hi, 1)
                    act.wait_ge(q_ps, s + 2)
                    act.wait_ge(q_stored, 16 * q_dmas * s + 16)
                    evacuate(t["qo"], t["qs"][HI], 0, SCALE / W_UP, q_hi)
                    act.wait_ge(k_ps, s + 2)
                    act.wait_ge(k_stored, 64 * s + 16)
                    evacuate(t["ko"], t["ks"][HI], 1, 1.0 / W_UP, k_hi)

            def vector(dve, t):
                dve.wait_ge(w_hi, 1)
                raw = t["w_raw"][:, :, :, :].rearrange("p i k n -> p (i k) n") if biased else psum[:, 0:6, 0:D]
                hi, lo = (w[:, :, :, :].rearrange("p i k n -> p (i k) n") for w in t["w"])
                nc.vector.scalar_tensor_tensor(lo, raw, W_UP, hi, ALU.mult, ALU.subtract).then_inc(w_sb_done, 1)
                if biased:
                    dve.wait_ge(w_loaded, 16 * n_w)
                dve.sem_inc(k_out, 1)
                dve.sem_inc(v_out, 1)
                with dve.Fori(0, NS, 1) as s:
                    dve.wait_ge(xt_ps, s + 1)
                    for j in range(TS):
                        ins = nc.vector.tensor_scalar(t["xn"][:, j, :], x_sb[:, s * TS + j, :],
                                                      mv[:, s * TS + j, 0:1], rstd[:, bass.ds(s * TS + j, 1)],
                                                      ALU.subtract, ALU.mult)
                    ins.then_inc(xn_ready, 1)
                    dve.wait_ge(xt_hi, s + 1)
                    nc.vector.tensor_tensor(t["xt"][LO][:, :, :], psum[:, 0:2, :], t["xt"][HI][:, :, :], ALU.subtract
                                            ).then_inc(xt_sb, 1)
                    dve.wait_ge(ct_hi, s + 1)
                    nc.vector.tensor_tensor(t["ct"][LO][:, :, :], psum[:, 2:4, :], t["ct"][HI][:, :, :], ALU.subtract
                                            ).then_inc(ct_sb, 1)
                    dve.wait_ge(q_hi, s + 1)
                    nc.vector.tensor_tensor(t["qs"][LO], t["qo"][:, :, :], t["qs"][HI], ALU.subtract
                                            ).then_inc(q_out, 1)
                    dve.wait_ge(v_ps, s + 1)
                    dve.wait_ge(v_stored, 16 * s + 16)
                    v_in = psum[:, 6:8, :].rearrange("p a (j d) -> p (a j) d", j=2)
                    if biased:
                        ins = nc.vector.scalar_tensor_tensor(t["vo"][:, :, :], v_in, 1.0 / W_UP,
                                                             t["bv"][:, :].unsqueeze(1).broadcast_to((P, TS, D)),
                                                             ALU.mult, ALU.add)
                    else:
                        ins = nc.vector.tensor_scalar(t["vo"][:, :, :], v_in, 1.0 / W_UP, None, ALU.mult)
                    ins.then_inc(v_out, 1)
                    dve.wait_ge(k_hi, s + 2)
                    nc.vector.tensor_tensor(t["ks"][LO], t["ko"][:, :, :], t["ks"][HI], ALU.subtract
                                            ).then_inc(k_out, 1)

            return alloc, sync, tensor, scalar, vector

        def relative_tables():
            ext_written, tables_loaded = sem("ext_written"), sem("tables_loaded")
            regrouped, pk_loaded, pk_ps, pk_t, ext_filled = (
                sem("regrouped"), sem("pk_loaded"), sem("pk_ps"), sem("pk_t"), sem("ext_filled"))
            up_set, raw_up, pk_parts = sem("up_set"), sem("raw_up"), sem("pk_parts")
            lo = S - 1 - K
            hi = S - 1 + K

            def alloc(stack):
                return {"kw": [sb(f"pos_k_skewed{i}", [P, S + GN - 1], F16, stack=stack) for i in (HI, LO)],
                        "vw": [sb(f"pos_v_by_key{i}", [P, 2, GN, P], F16, stack=stack) for i in (HI, LO)]}

            def alloc_raw(stack, t):
                t["raw"] = sb("pos_v_by_query", [P, 2, S * DH], stack=stack)
                t["pk"] = sb("pos_k_rows", [2 * K, DH], stack=stack)
                t["pk_last"] = sb("pos_k_last", [1, DH], stack=stack)
                t["pkt"] = sb("pos_k_t", [DH, 2 * K + 1], stack=stack)
                t["pkp"] = [sb(f"pos_k_t{i}", [DH, 2 * K + 1], F16, stack=stack) for i in (HI, LO)]
                t["extk"] = [sb(f"pos_k_ext{i}", [DH, 2 * S], F16, stack=stack) for i in (HI, LO)]
                t["up"] = sb("w_up", [P, 1], stack=stack)

            def gpsimd(pool, t):
                nc.gpsimd.memset(t["up"][:, :], W_UP).then_inc(up_set, 1)
                pool.wait_ge(up_set, 1)
                pool.wait_ge(tables_loaded, 16 * (2 * IN + 2))
                raw = t["raw"][:, :, :]
                shape = (P, 2, S * DH)
                nc.gpsimd.tensor_tensor(raw, raw, t["up"][:, :].unsqueeze(2).broadcast_to(shape), ALU.mult
                                        ).then_inc(raw_up, 1)
                pool.wait_ge(raw_up, 1)
                by_key = [[v[:, kt, :, :].rearrange("p g (r d) -> p g r d", r=IN) for kt in range(2)] for v in t["vw"]]
                by_query = [t["raw"][:, kt, :].rearrange("p (r g d) -> p g r d", r=IN, g=GN) for kt in range(2)]
                for kt in range(2):
                    ins = nc.gpsimd.tensor_copy(by_key[HI][kt], by_query[kt])
                ins.then_inc(raw_up, 1)
                pool.wait_ge(raw_up, 2)
                for kt in range(2):
                    for i in range(IN):
                        ins = nc.gpsimd.tensor_tensor(by_key[LO][kt][:, :, i, :], by_query[kt][:, :, i, :],
                                                      by_key[HI][kt][:, :, i, :], ALU.subtract)
                ins.then_inc(regrouped, 1)

            def sync(sp, t):
                pk, pv = a["L0_xattn_pos_k"], a["L0_xattn_pos_v"]
                sp.dma_start(t["pk"][:, :], pk[0:2 * K, :]).then_inc(pk_loaded, 16)
                sp.dma_start(t["pk_last"][0:1, :], pk[2 * K:2 * K + 1, :]).then_inc(pk_loaded, 16)
                sp.dma_start(extv_dr[lo:hi + 1, :], pv).then_inc(ext_written, 16)
                sp.dma_start(extv_dr[0:lo, :], pv[0:1, :].broadcast_to((lo, DH))).then_inc(ext_written, 16)
                sp.dma_start(extv_dr[hi + 1:2 * S, :],
                             pv[2 * K:2 * K + 1, :].broadcast_to((2 * S - hi - 1, DH))).then_inc(ext_written, 16)
                sp.wait_ge(ext_written, 16 * 3)
                sp.wait_ge(ext_filled, 1)
                for i in range(IN):
                    off = S - GN - GN * i
                    for part in (HI, LO):
                        sp.dma_start(t["kw"][part][i * DH:(i + 1) * DH, :], t["extk"][part][:, off:off + S + GN - 1]
                                     ).then_inc(tables_loaded, 16)
                for kt in range(2):
                    rows = bass.AP(extv_dr.tensor, kt * P * DH, [[DH, P], [1, S * DH]])
                    sp.dma_start(t["raw"][:, kt, :], rows).then_inc(tables_loaded, 16)

            def tensor(pe, t):
                pe.wait_ge(pk_loaded, 32)
                nc.tensor.transpose(psum[0:DH, 0, 0:2 * K], t["pk"][:, :], ident[:, :])
                nc.tensor.transpose(psum[0:DH, 0, 2 * K:2 * K + 1], t["pk_last"][0:1, :], ident[0:1, 0:1]
                                    ).then_inc(pk_ps, 1)
                pe.wait_ge(ext_filled, 1)

            def vector(dve, t):
                dve.wait_ge(pk_ps, 1)
                nc.vector.tensor_copy(t["pkt"][:, :], psum[0:DH, 0, 0:2 * K + 1]).then_inc(pk_t, 1)
                dve.wait_ge(pk_t, 1)
                nc.vector.tensor_copy(t["pkp"][HI][:, :], t["pkt"][:, :]).then_inc(pk_parts, 1)
                dve.wait_ge(pk_parts, 1)
                nc.vector.tensor_tensor(t["pkp"][LO][:, :], t["pkt"][:, :], t["pkp"][HI][:, :], ALU.subtract
                                        ).then_inc(pk_parts, 1)
                dve.wait_ge(pk_parts, 2)
                for part in (HI, LO):
                    ext, src = t["extk"][part], t["pkp"][part]
                    nc.vector.tensor_copy(ext[:, lo:hi + 1], src[:, :])
                    nc.vector.tensor_copy(ext[:, 0:lo], src[:, 0:1].broadcast_to((DH, lo)))
                    ins = nc.vector.tensor_copy(ext[:, hi + 1:2 * S],
                                                src[:, 2 * K:2 * K + 1].broadcast_to((DH, 2 * S - hi - 1)))
                ins.then_inc(ext_filled, 1)

            return alloc, alloc_raw, sync, gpsimd, tensor, vector, regrouped

        def attention(n_, relative, tables=None, tables_ready=None):
            in_loaded = [sem(f"qkv_loaded_{i}") for i in range(2)]
            in_dmas = 4 + IN if relative else 1 + 4 * len(SPLIT)
            NW = 4
            KR = len(SPLIT) * 2 * DH
            mask_loaded = sem("mask_loaded")
            qd_ready, v_padded, s_ps = sem("qd_ready"), sem("v_padded"), sem("s_ps")
            masked, max_done, exp_done = sem("masked"), sem("max_done"), sem("exp_done")
            recip_done, w_ready, t_ps = sem("recip_done"), sem("w_ready"), sem("t_ps")
            wt_hi, wt_lo, v_done = sem("wt_hi"), sem("wt_lo"), sem("v_done")
            v_hi, q_zeroed, parity_set = sem("v_hi"), sem("q_zeroed"), sem("parity_set")
            NIT, LAG = B // 2, 3

            def rounds(eng, stages):
                def round_(it, n):
                    for lag, f in stages:
                        if not isinstance(it, int) or 0 <= it * NB2 + n - lag < NIT * NB2:
                            f(it, n - lag)

                for n in range(LAG):
                    round_(0, n)
                with eng.Fori(0, NIT - 1, 1) as it:
                    for n in range(LAG, LAG + NB2):
                        round_(it, n)
                for n in range(LAG, LAG + NB2):
                    round_(NIT - 1, n)
            x_out, x_masked, zeroed = sem("x_out"), sem("x_masked"), sem("zeroed")
            h_stored = [sem(f"h_stored_{i}") for i in range(2)]
            out_dmas = 1 + IN if relative else 3

            def alloc(stack):
                def parts(name, shape):
                    return [[sb(f"{name}{n_}_{i}_{part}", shape, F16, stack=stack) for part in (HI, LO)]
                            for i in range(2)]

                t = {"v": [sb(f"v_b{n_}_{i}", [P, 2, D], stack=stack) for i in range(2)],
                     "vz": parts("v_parts_b", [P, 2, D] if relative else [P, 2, H, 32]),
                     "negmax": sb(f"negmax{n_}", [P, 2, GC], stack=stack),
                     "sums": sb(f"sums{n_}", [P, 2, GC], stack=stack),
                     "recip": sb(f"recip{n_}", [P, 2, GC], stack=stack),
                     "w": [sb(f"weights{n_}_{i}", [P, GC, S], stack=stack) for i in range(NW)],
                     "wt": parts("weights_t", [P, 2, 512]),
                     "h": [sb(f"heads{n_}_{i}", [P, 2, S], stack=stack) for i in range(2)]}
                if relative:
                    t["q"] = [sb(f"q_b{n_}_{i}", [P, 2, S, 2], F16, stack=stack) for i in range(2)]
                    t["k"] = parts("k_b", [P, 2, S])
                    t["q2"] = [sb(f"q_by_i{n_}_{i}", [P, H, GN, 2], F16, stack=stack) for i in range(2)]
                    t["qd"] = parts("q_blocks", [P, 512])
                    t["qd2"] = parts("q_blocks_rel", [P, 512])
                    t["parity"] = sb(f"parity{n_}", [P, 2], stack=stack)
                    t["xv"] = sb(f"x_odd{n_}", [P, 64], stack=stack)
                    t["xm"] = sb(f"x_masked_t{n_}", [P, 512], stack=stack)
                    t["r"] = [sb(f"rel_heads{n_}_{i}", [P, H, GN], stack=stack) for i in range(2)]
                else:
                    t["q"] = [sb(f"q_b{n_}_{i}", [KR, NC, 2, S], F16, stack=stack) for i in range(2)]
                    t["k"] = [sb(f"k_b{n_}_{i}", [KR, NC, S], F16, stack=stack) for i in range(2)]
                    t["mask"] = sb(f"mask{n_}", [P, 2, S], I32, stack=stack)
                    t["ms"] = [sb(f"masked_scores{n_}_{i}", [P, 2, 2 * S], stack=stack) for i in range(2)]
                return t

            def sync(sp, t):
                v_t = v_dr.rearrange("(b t p) d -> p b t d", p=P, t=2)
                h_t = h_dr.rearrange("b (t p) s -> p b t s", p=P)
                r_t = r_dr.rearrange("b (h d) (i g) -> d b h i g", h=H, i=IN)
                if relative:
                    q_t = q0_dr.rearrange("b (t p) s e -> p b t (s e)", p=P)
                    q2_t = q0_dr.rearrange("b (h d) (i g) e -> d b h i (g e)", h=H, i=IN)
                    k_t = [k.rearrange("b (t p) s -> p b t s", p=P) for k in k_dr]
                else:
                    by_pair = "b (e c d) s -> d b e c s"
                    q_t = [q.rearrange(by_pair, e=2, c=NC) for q in q1_dr]
                    k_t = [k.rearrange(by_pair, e=2, c=NC) for k in k_dr]

                def load(b, bb):
                    done = in_loaded[bb]
                    sp.dma_start(t["v"][bb][:, :, :], v_t[:, b]).then_inc(done, 16)
                    if relative:
                        sp.dma_start(t["q"][bb][:, :, :, :].rearrange("p t s e -> p t (s e)"), q_t[:, b]
                                     ).then_inc(done, 16)
                        for i in (HI, LO):
                            sp.dma_start(t["k"][bb][i][:, :, :], k_t[i][:, b]).then_inc(done, 16)
                        for i in range(IN):
                            sp.dma_start(t["q2"][bb][i * DH:(i + 1) * DH, :, :, :].rearrange("d h g e -> d h (g e)"),
                                         q2_t[:, b, :, i, :]).then_inc(done, 16)
                    else:
                        for k, (pq, pk) in enumerate(SPLIT):
                            for e in range(2):
                                rows = slice((2 * k + e) * DH, (2 * k + e + 1) * DH)
                                sp.dma_start(t["q"][bb][rows, :, e, :], q_t[pq][:, b, e]).then_inc(done, 16)
                                sp.dma_start(t["k"][bb][rows, :, :], k_t[pk][:, b, e]).then_inc(done, 16)

                if not relative:
                    sp.dma_start(t["mask"][:, :, :], a["mask_SxS2_ik1"].rearrange("(t p) k -> p t k", p=P)
                                 ).then_inc(mask_loaded, 16)
                if not relative:
                    sp.wait_ge(q_zeroed, 1)
                for bb in range(2):
                    load(bb, bb)
                    sp.sem_inc(h_stored[bb], 16)
                with sp.Fori(0, B // 2, 1) as it:
                    for bb in range(2):
                        sp.wait_ge(x_out, it * NB2 + NC * (bb + 1) + 1)
                        if relative:
                            sp.dma_start(h_t[:, it * 2 + bb], t["h"][bb][:, :, :]).then_inc(h_stored[bb], 16)
                        else:
                            sp.dma_start(h_t[:, it * 2 + bb, 0], t["h"][bb][:, 0, :]).then_inc(h_stored[bb], 16)
                            for lo, hi in ((0, 64), (64, 0)):
                                sp.dma_start(h_t[lo:lo + 64, it * 2 + bb, 1], t["h"][bb][hi:hi + 64, 1, :]
                                             ).then_inc(h_stored[bb], 16)
                        if relative:
                            for r in range(IN):
                                sp.dma_start(r_t[:, it * 2 + bb, :, IN - 1 - r, :],
                                             t["r"][bb][r * DH:(r + 1) * DH, :, :]).then_inc(h_stored[bb], 16)
                        load((it * 2 + bb + 2) % B, bb)
                for bb in range(2):
                    sp.wait_ge(h_stored[bb], 16 + 16 * out_dmas * (B // 2))
                    sp.wait_ge(in_loaded[bb], 16 * in_dmas * (B // 2 + 1))

            def gpsimd(pool, t):
                if not relative:
                    for vz in t["vz"]:
                        for i in (HI, LO):
                            nc.gpsimd.memset(vz[i][:, :, :, :], 0.0)
                    for i in range(2):
                        ins = nc.gpsimd.memset(t["ms"][i][:, :, :], MASKED)
                    ins.then_inc(zeroed, 1)
                    pool.wait_ge(zeroed, 1)
                pool.sem_inc(v_done, NB2)

                def q_blocks(it, n):
                    bb, c, buf = n // NC % 2, n % NC, n % 2
                    if c == 0:
                        pool.wait_ge(in_loaded[bb], 16 * in_dmas * (it + n // NB2 + 1))
                    pool.wait_ge(s_ps, it * NB2 + n + 1)
                    for i in (HI, LO):
                        for hh in range(2):
                            out_ = t["qd"][buf][i][:, hh * 256:(hh + 1) * 256].rearrange("p (g h i) -> p g h i", g=GC, h=8)
                            src = t["q"][bb][:, hh, :, i].rearrange("p (i g) -> p g i", g=GN)[:, GC * c:GC * (c + 1), :]
                            nc.gpsimd.tensor_tensor(
                                out_, src.unsqueeze(2).broadcast_to((P, GC, 8, IN)),
                                block[:, :].unsqueeze(1).unsqueeze(3).broadcast_to((P, GC, 8, IN)), ALU.mult)
                        out_ = t["qd2"][buf][i][:, :].rearrange("p (g h i) -> p g h i", g=GC, h=H)
                        src = t["q2"][bb][:, :, GC * c:GC * (c + 1), i].rearrange("p h g -> p g h")
                        ins = nc.gpsimd.tensor_tensor(
                            out_, src.unsqueeze(3).broadcast_to((P, GC, H, IN)),
                            block[:, :].unsqueeze(1).unsqueeze(1).broadcast_to((P, GC, H, IN)), ALU.mult)
                    ins.then_inc(qd_ready, 1)

                def scale(it, n):
                    pool.wait_ge(recip_done, it * NB2 + n + 1)
                    nc.gpsimd.tensor_tensor(
                        t["w"][n % NW][:, :, :], t["w"][n % NW][:, :, :],
                        t["recip"][:, n % 2, :].unsqueeze(2).broadcast_to((P, GC, S)), ALU.mult).then_inc(w_ready, 1)

                def low_v(it, n):
                    if n % NC != 0:
                        return
                    bb = n // NC % 2
                    pool.wait_ge(v_hi, it * 2 + n // NC + 1)
                    if relative:
                        ins = nc.gpsimd.tensor_tensor(t["vz"][bb][LO][:, :, :], t["v"][bb][:, :, :],
                                                      t["vz"][bb][HI][:, :, :], ALU.subtract)
                    else:
                        for kt in range(2):
                            for h2 in range(2):
                                (hi, lo) = (z[:, kt, :, :].rearrange("p (j e) c -> p j e c", e=2)
                                            [:, :, h2, h2 * DH:(h2 + 1) * DH] for z in t["vz"][bb])
                                src = t["v"][bb][:, kt, :].rearrange("p (j e d) -> p j e d", e=2, d=DH)[:, :, h2, :]
                                ins = nc.gpsimd.tensor_tensor(lo, src, hi, ALU.subtract)
                    ins.then_inc(v_padded, 1)

                rounds(pool, [(0, q_blocks), (2, low_v)] if relative else [(1, scale), (1, low_v)])

            def tensor(pe, t):
                pe.sem_inc(s_ps, 2)
                if relative:
                    pe.wait_ge(tables_ready, 1)
                def scores(it, n):
                    bb, c, buf = n // NC % 2, n % NC, n % 2
                    if c == 0:
                        pe.wait_ge(in_loaded[bb], 16 * in_dmas * (it + n // NB2 + 1))
                    if relative:
                        pe.wait_ge(qd_ready, it * NB2 + n + 1)
                    if n >= 2:
                        pe.wait_ge(exp_done if relative else masked, it * NB2 + n - 1)
                    for g in range(GC):
                        s_g = psum[:, buf * 2 + g // 2, (g % 2) * S:(g % 2 + 1) * S]
                        if relative:
                            off = GN - 1 - (GC * c + g)
                            for k, (pq, pk) in enumerate(SPLIT):
                                nc.tensor.matmul(s_g, t["qd2"][buf][pq][:, g * P:(g + 1) * P],
                                                 tables["kw"][pk][:, off:off + S], start=(k == 0), stop=False,
                                                 skip_group_check=True)
                            for pq, pk in SPLIT:
                                for hh in range(2):
                                    ins = nc.tensor.matmul(
                                        psum[hh * 64:(hh + 1) * 64, buf * 2 + g // 2, (g % 2) * S:(g % 2 + 1) * S],
                                        t["qd"][buf][pq][:, hh * 256 + g * 64:hh * 256 + (g + 1) * 64],
                                        t["k"][bb][pk][:, hh, :], start=False, stop=True, skip_group_check=True)
                        else:
                            ins = nc.tensor.matmul(s_g, t["q"][bb][:, c, g // 2, (g % 2) * P:(g % 2 + 1) * P],
                                                   t["k"][bb][:, c, :], start=True, stop=True)
                    ins.then_inc(s_ps, 1)

                def transposes(it, n):
                    pe.wait_ge(w_ready, it * NB2 + n + 1)
                    for kt in range(2):
                        pe.wait_ge(wt_lo, 2 * (it * NB2 + n) + kt + 1)
                        for g in range(GC):
                            ins = nc.tensor.transpose(psum[:, 4 + kt, g * P:(g + 1) * P],
                                                      t["w"][n % NW][:, g, kt * P:(kt + 1) * P], ident[:, :])
                        ins.then_inc(t_ps, 1)

                def values(it, n):
                    bb, c = n // NC % 2, n % NC
                    if c == 0:
                        pe.wait_ge(v_padded, it * 2 + n // NC + 1)
                    pe.wait_ge(wt_lo, 2 * (it * NB2 + n) + 4)
                    pe.wait_ge(x_out, it * NB2 + n + 1)
                    wt = t["wt"][n % 2]
                    if relative:
                        for hh in range(2):
                            for kt in range(2):
                                for k, (pv, pw) in enumerate(SPLIT):
                                    for j in range(4):
                                        pair = hh * 4 + j
                                        rhs = wt[pw][:, kt, :].rearrange("p (g c) -> p g c", g=GC)[
                                            :, :, pair * 2 * IN:(pair + 1) * 2 * IN]
                                        nc.tensor.matmul(psum[32 * j:32 * j + 32, 6, hh * 64:(hh + 1) * 64],
                                                         t["vz"][bb][pv][:, kt, pair * 32:(pair + 1) * 32], rhs,
                                                         start=(kt == 0 and k == 0), stop=(kt == 1 and k == 2),
                                                         tile_position=(0, 32 * j), skip_group_check=True)
                        for g in range(GC):
                            for kt in range(2):
                                for k, (pv, pw) in enumerate(SPLIT):
                                    ins = nc.tensor.matmul(psum[:, 7, g * P:(g + 1) * P],
                                                           tables["vw"][pv][:, kt, GN - 1 - (GC * c + g), :],
                                                           wt[pw][:, kt, g * P:(g + 1) * P],
                                                           start=(kt == 0 and k == 0), stop=(kt == 1 and k == 2))
                    else:
                        for kt in range(2):
                            for k, (pv, pw) in enumerate(SPLIT):
                                for e in range(2):
                                    j = (c // 2 + 2 * e) % 4
                                    ins = nc.tensor.matmul(psum[32 * j:32 * j + 32, 6 + e, 0:S],
                                                           t["vz"][bb][pv][:, kt, NC * e + c, :],
                                                           wt[pw][:, kt, e * S:(e + 1) * S],
                                                           start=(c % 2 == 0 and kt == 0 and k == 0),
                                                           stop=(c % 2 == 1 and kt == 1 and k == 2),
                                                           tile_position=(0, 32 * j), skip_group_check=True)
                    ins.then_inc(v_done, 1)

                rounds(pe, [(0, scores), (2, transposes), (3, values)])

            def scalar(act, t):
                if not relative:
                    act.wait_ge(zeroed, 1)

                def high_v(it, n):
                    if n % NC != 0:
                        return
                    bb = n // NC % 2
                    act.wait_ge(in_loaded[bb], 16 * in_dmas * (it + n // NB2 + 1))
                    act.wait_ge(v_done, it * NB2 + NC * (n // NC + 1))
                    if relative:
                        ins = nc.scalar.copy(t["vz"][bb][HI][:, :, :], t["v"][bb][:, :, :])
                    else:
                        for kt in range(2):
                            for h2 in range(2):
                                dst = t["vz"][bb][HI][:, kt, :, :].rearrange("p (j e) c -> p j e c", e=2)
                                src = t["v"][bb][:, kt, :].rearrange("p (j e d) -> p j e d", e=2, d=DH)
                                ins = nc.scalar.copy(dst[:, :, h2, h2 * DH:(h2 + 1) * DH], src[:, :, h2, :])
                    ins.then_inc(v_hi, 1)

                def exps(it, n):
                    act.wait_ge(max_done, it * NB2 + n + 1)
                    for g in range(GC):
                        if relative:
                            src = psum[:, (n % 2) * 2 + g // 2, (g % 2) * S:(g % 2 + 1) * S]
                        else:
                            src = t["ms"][n % 2][:, g // 2, (g % 2) * S:(g % 2 + 1) * S]
                        ins = nc.scalar.activation(t["w"][n % NW][:, g, :], src, ACT.Exp,
                                                   bias=t["negmax"][:, n % 2, g:g + 1],
                                                   accum_out=t["sums"][:, n % 2, g:g + 1])
                    ins.then_inc(exp_done, 1)

                def scale(it, n):
                    act.wait_ge(recip_done, it * NB2 + n + 1)
                    for g in range(GC):
                        w = t["w"][n % NW][:, g, :]
                        ins = nc.scalar.mul(w, w, t["recip"][:, n % 2, g:g + 1])
                    ins.then_inc(w_ready, 1)

                def evacuate(it, n):
                    act.wait_ge(v_done, it * NB2 + NB2 + n - 1)
                    for kt in range(2):
                        act.wait_ge(t_ps, 2 * (it * NB2 + n) + kt + 1)
                        nc.scalar.mul(t["wt"][n % 2][HI][:, kt, :], psum[:, 4 + kt, :], A_UP).then_inc(wt_hi, 1)

                rounds(act, [(0, high_v), (2, evacuate), (0, exps)] + ([(1, scale)] if relative else []))

            def vector(dve, t):
                dve.sem_inc(x_out, 1)
                dve.sem_inc(wt_lo, 2)
                if not relative:
                    for q in t["q"]:
                        ins = nc.vector.memset(q[:, :, :, :], 0.0)
                    ins.then_inc(q_zeroed, 1)
                    dve.wait_ge(mask_loaded, 16)
                    dve.wait_ge(zeroed, 1)
                else:
                    nc.vector.tensor_reduce(t["parity"][:, :], block[:, :].rearrange("p (j e) -> p e j", e=2), X, ALU.add
                                            ).then_inc(parity_set, 1)
                    dve.wait_ge(parity_set, 1)
                    nc.vector.tensor_scalar(t["parity"][:, :], t["parity"][:, :], 1.0 / A_UP, None, ALU.mult
                                            ).then_inc(parity_set, 1)
                    dve.wait_ge(parity_set, 2)
                def maxima(it, n):
                    if relative:
                        dve.wait_ge(s_ps, it * NB2 + n + 3)
                    else:
                        if n >= 2:
                            dve.wait_ge(exp_done, it * NB2 + n - 1)
                        wait_apart(dve, s_ps, it * NB2 + n + 3)
                    src = psum[:, (n % 2) * 2:(n % 2) * 2 + 2, :]
                    if not relative:
                        nc.vector.copy_predicated(t["ms"][n % 2][:, :, :],
                                                  t["mask"][:, :, :].rearrange("p t k -> p (t k)").unsqueeze(1)
                                                  .broadcast_to((P, 2, 2 * S)), src).then_inc(masked, 1)
                        dve.wait_ge(masked, it * NB2 + n + 1)
                        src = t["ms"][n % 2][:, :, :]
                    nc.vector.tensor_reduce(t["negmax"][:, n % 2, :],
                                            src.rearrange("p a (g k) -> p (a g) k", g=2), X, ALU.max,
                                            negate=True).then_inc(max_done, 1)

                def reciprocals(it, n):
                    dve.wait_ge(exp_done, it * NB2 + n + 1)
                    nc.vector.reciprocal(t["recip"][:, n % 2, :], t["sums"][:, n % 2, :]).then_inc(recip_done, 1)

                def evacuate(it, n):
                    for kt in range(2):
                        dve.wait_ge(wt_hi, 2 * (it * NB2 + n) + kt + 1)
                        nc.vector.scalar_tensor_tensor(t["wt"][n % 2][LO][:, kt, :], psum[:, 4 + kt, :], A_UP,
                                                       t["wt"][n % 2][HI][:, kt, :], ALU.mult, ALU.subtract
                                                       ).then_inc(wt_lo, 1)

                def heads(it, n):
                    bb, c = n // NC % 2, n % NC
                    dve.wait_ge(v_done, it * NB2 + NB2 + n + 1)
                    if c == 0:
                        dve.wait_ge(h_stored[bb], (it + n // NB2) * 16 * out_dmas + 16)
                    if relative:
                        dst = t["h"][bb][:, :, :].rearrange("p t (i g) -> p t g i", g=GN)[:, :, GC * c:GC * (c + 1), :]
                        even, odd = (psum[:, 6, 0:128].rearrange("p (t g e i) -> p t g e i", t=2, g=GC, e=2)[:, :, :, e, :]
                                     for e in range(2))
                        xv = t["xv"][:, :].rearrange("p (t g i) -> p t g i", t=2, g=GC)
                        nc.vector.tensor_scalar(xv, odd, t["parity"][:, 1:2], None, ALU.mult)
                        nc.vector.scalar_tensor_tensor(
                            t["xm"][:, :].rearrange("p (m i) -> p m i", i=IN),
                            psum[:, 7, :].rearrange("p (m i) -> p m i", i=IN), 1.0 / (A_UP * W_UP),
                            block_rev[:, :].unsqueeze(1).broadcast_to((P, GC * H, IN)), ALU.mult, ALU.mult
                        ).then_inc(x_masked, 1)
                        dve.wait_ge(x_masked, it * NB2 + n + 1)
                        for half in range(2):
                            nc.vector.scalar_tensor_tensor(dst[:, half], even[:, half], t["parity"][:, 0:1], xv[:, half],
                                                           ALU.mult, ALU.add)
                        nc.vector.tensor_reduce(
                            t["r"][bb][:, :, GC * c:GC * (c + 1)].rearrange("p h g -> p g h"),
                            t["xm"][:, :].rearrange("p (g h i) -> p g h i", g=GC, h=H), X, ALU.add
                        ).then_inc(x_out, 1)
                    elif c == NC - 1:
                        nc.vector.tensor_scalar(t["h"][bb][:, :, :], psum[:, 6:8, 0:S], 1.0 / A_UP, None,
                                                ALU.mult).then_inc(x_out, 1)
                    else:
                        dve.sem_inc(x_out, 1)

                rounds(dve, [(0, maxima), (1, reciprocals), (2, evacuate), (3, heads)])

            return alloc, sync, gpsimd, tensor, scalar, vector

        def merge_heads(n_, w_ap, transposed, parts, bias_ap=None):
            h_loaded = [sem(f"h_loaded_{i}") for i in range(2)]
            w_loaded, o_ps, x_added = sem("fc_loaded"), sem("o_ps"), sem("x_added")
            w_ps, w_hi, w_done, ones_set = sem("fc_ps"), sem("fc_hi"), sem("fc_done"), sem("ones_set")
            h_sum, h_hi, h_lo = sem("h_sum"), sem("h_hi"), sem("h_lo")
            np_ = len(parts)

            def alloc(stack):
                return {"w": [sb(f"w_fc{n_}_{i}", [P, KT, D], F16, stack=stack) for i in (HI, LO)],
                        "raw": sb(f"w_fc_raw{n_}", [P, KT, D], stack=stack),
                        "bias": sb(f"b_fc{n_}", [1, D], stack=stack), "ones": sb(f"ones{n_}", [1, P], stack=stack),
                        "h": [sb(f"h_in{n_}_{i}", [P, np_, 2, SC], stack=stack) for i in range(2)],
                        "hs": [[sb(f"h_part{n_}_{i}_{part}", [P, 2, SC], F16, stack=stack) for part in (HI, LO)]
                               for i in range(2)]}

            def sync(sp, t):
                sp.dma_start(t["raw"][:, :, :], w_ap.rearrange("(t p) n -> p t n", p=P)).then_inc(w_loaded, 16)
                if bias_ap is not None:
                    sp.dma_start(t["bias"][0:1, :], bias_ap.unsqueeze(0)).then_inc(w_loaded, 16)
                sp.sem_inc(h_lo, 2)
                with sp.Fori(0, NS // 2, 1) as it:
                    for j in range(2):
                        sp.wait_ge(h_lo, it * 2 + j + 1)
                        for i, part in enumerate(parts):
                            src = part.rearrange("b (t p) s -> p t b s", p=P)
                            for hh in range(2):
                                sp.dma_start(t["h"][j][:, i, hh, :].rearrange("p (b s) -> p b s", b=2),
                                             src[:, hh, bass.ds((it * 2 + j) * 2, 2), :]).then_inc(h_loaded[j], 16)

            def gpsimd(pool, t):
                with pool.Fori(0, NS // 2, 1) as it:
                    for j in range(2):
                        h = t["h"][j]
                        if np_ == 2:
                            pool.wait_ge(h_loaded[j], 32 * np_ * (it + 1))
                            nc.gpsimd.tensor_tensor(h[:, 0], h[:, 0], h[:, 1], ALU.add).then_inc(h_sum, 1)
                        pool.wait_ge(h_hi, it * 2 + j + 1)
                        nc.gpsimd.tensor_tensor(t["hs"][j][LO][:, :, :], h[:, 0], t["hs"][j][HI][:, :, :], ALU.subtract
                                                ).then_inc(h_lo, 1)

            def scalar(act, t):
                if transposed:
                    act.wait_ge(w_ps, 1)
                    src = psum[:, 0:2, 0:D]
                else:
                    act.wait_ge(w_loaded, 32 if bias_ap is not None else 16)
                    src = t["raw"][:, :, :]
                nc.scalar.mul(t["w"][HI][:, :, :], src, W_UP).then_inc(w_hi, 1)
                act.sem_inc(o_ps, 2)
                with act.Fori(0, NS // 2, 1) as it:
                    for j in range(2):
                        if np_ == 2:
                            act.wait_ge(h_sum, it * 2 + j + 1)
                        else:
                            act.wait_ge(h_loaded[j], 32 * (it + 1))
                        act.wait_ge(o_ps, it * 2 + j + 1)
                        nc.scalar.copy(t["hs"][j][HI][:, :, :], t["h"][j][:, 0]).then_inc(h_hi, 1)

            def tensor(pe, t):
                if transposed:
                    pe.wait_ge(w_loaded, 16)
                    for ot in range(2):
                        for kt in range(KT):
                            ins = nc.tensor.transpose(psum[:, kt, ot * P:(ot + 1) * P],
                                                      t["raw"][:, ot, kt * P:(kt + 1) * P], ident[:, :])
                    ins.then_inc(w_ps, 1)
                pe.wait_ge(w_done, 1)
                if bias_ap is not None:
                    pe.wait_ge(w_loaded, 32)
                    pe.wait_ge(ones_set, 1)
                with pe.Fori(0, NS // 2, 1) as it:
                    for j in range(2):
                        pe.wait_ge(h_lo, it * 2 + j + 3)
                        pe.wait_ge(x_added, it * 2 + j + 1)
                        for m in range(TS):
                            o = psum[:, 2 + 2 * j + m // 2, (m % 2) * D:(m % 2 + 1) * D]
                            if bias_ap is not None:
                                nc.tensor.matmul(o, t["ones"][0:1, :], t["bias"][0:1, :], start=True, stop=False)
                            for kt in range(KT):
                                for k, (ph, pw) in enumerate(SPLIT):
                                    ins = nc.tensor.matmul(o, t["hs"][j][ph][:, kt, m * P:(m + 1) * P],
                                                           t["w"][pw][:, kt, :],
                                                           start=(bias_ap is None and kt == 0 and k == 0),
                                                           stop=(kt == KT - 1 and k == 2))
                        ins.then_inc(o_ps, 1)

            def vector(dve, t):
                dve.wait_ge(w_hi, 1)
                nc.vector.scalar_tensor_tensor(t["w"][LO][:, :, :], psum[:, 0:2, 0:D] if transposed else t["raw"][:, :, :],
                                               W_UP, t["w"][HI][:, :, :], ALU.mult, ALU.subtract).then_inc(w_done, 1)
                if bias_ap is not None:
                    nc.vector.memset(t["ones"][0:1, :], W_UP).then_inc(ones_set, 1)
                dve.sem_inc(x_added, 2)
                with dve.Fori(0, NS // 2, 1) as it:
                    for j in range(2):
                        wait_apart(dve, o_ps, it * 2 + j + 3)
                        for e in range(2):
                            xs = x_sb[:, bass.ds((it * 2 + j) * TS + 2 * e, 2), :]
                            o = psum[:, 2 + 2 * j + e, :].rearrange("p (m d) -> p m d", m=2)
                            ins = nc.vector.scalar_tensor_tensor(xs, o, 1.0 / W_UP, xs, ALU.mult, ALU.add)
                        ins.then_inc(x_added, 1)

            return alloc, sync, gpsimd, tensor, scalar, vector

        def quantised_ffn():
            w_loaded, w_amax, w_step_done, w_recip = sem("w_loaded"), sem("fw_amax"), sem("fw_step"), sem("fw_recip")
            w_div, w_round, w_quant, w_ps, w_sb_done = (sem("fw_div"), sem("fw_round"), sem("fw_quant"), sem("w_ps"),
                                                        sem("fw_sb"))
            xn_ready, xt_ps, xt_sb, x_max = sem("xn_ready"), sem("xt_ps"), sem("xt_sb"), sem("fx_max")
            fold, amax_part, amax_all, sc_step, scaled = (sem("amax_fold"), sem("amax_part"), sem("amax_all"),
                                                          sem("scale_step"), sem("scaled"))
            x_round, x_quant, magic_set, acc_set = sem("x_round"), sem("x_quant"), sem("magic_set"), sem("acc_set")
            m_ps, m_used = sem("m_ps"), sem("m_used")
            g_ps, g_round, g_val, g_sig, g_y, g_clip, g_prod = (sem("g_ps"), sem("g_round"), sem("g_val"), sem("g_sig"),
                                                                sem("g_y"), sem("g_clip"), sem("g_prod"))
            g_max = sem("g_max")
            u_ps, u_round, p_round, u_int, u_prod, u_max = (sem("u_ps"), sem("u_round"), sem("p_round"), sem("u_int"),
                                                            sem("u_prod"), sem("u_max"))
            o_round, o_hi, o_int, d_ps, d_added = sem("o_round"), sem("o_hi"), sem("o_int"), sem("d_ps"), sem("d_added")
            x_hi, w_hi = sem("fx_hi"), sem("w_hi")
            F = 768
            FT = F // P
            NP = FT // 2
            NI = 2 * NP

            def alloc(stack):
                t = {"wg": [sb(f"wg_t{i}", [P, KT, F], F16, stack=stack) for i in (HI, LO)],
                     "wu": [sb(f"wu_t{i}", [P, KT, F], F16, stack=stack) for i in (HI, LO)],
                     "wd": [sb(f"wd_t{i}", [P, FT, D], F16, stack=stack) for i in (HI, LO)],
                     "am": sb("amax_new", [P, 12], stack=stack), "acc": sb("amax_sofar", [P, 12], stack=stack),
                     "ar": sb("amax_row", [P, 8], stack=stack), "aa": sb("amax_whole", [P, 8], stack=stack),
                     "sc": sb("scales", [P, 16], stack=stack),
                     "magic": sb("magic", [P, 1], stack=stack)}
                with ExitStack() as inner:
                    t["os"] = [[sb(f"ff_o_part{i}_{part}", [P, FT, SC], F16, stack=inner) for part in (HI, LO)]
                               for i in range(2)]
                t["xq"] = [sb(f"xq_t{i}", [P, KT, B * S], F16, stack=stack) for i in (HI, LO)]
                with ExitStack() as inner:
                    t["xt"] = sb("x_t", [P, KT, B * S], stack=inner)
                    t["raw"] = sb("fw_raw", [P, 3, F * D // P], stack=inner)
                    t["wq"] = sb("fw_q", [P, 3, F * D // P], stack=inner)
                    t["wam"] = sb("fw_amax_t", [P, 3, F * D // P // QBLOCK], stack=inner)
                    t["wsc"] = sb("fw_scale_t", [P, 3, F * D // P // QBLOCK], stack=inner)
                    t["xn"] = sb("fxn", [P, TS, D], stack=inner)
                t["p"] = sb("gated", [P, FT, B * S], stack=stack)
                with ExitStack() as inner:
                    t["a"] = [sb(f"ff_a{i}", [P, 2 * SC], stack=inner) for i in range(2)]
                    t["b"] = [sb(f"ff_b{i}", [P, 2 * SC], stack=inner) for i in range(2)]
                    t["c"] = [sb(f"ff_c{i}", [P, 2 * SC], stack=inner) for i in range(2)]
                return t

            def sync(sp, t):
                for i, nm in enumerate(("L0_ffn_w_gate", "L0_ffn_w_up", "L0_ffn_w_down")):
                    w = a[nm]
                    sp.dma_start(t["raw"][:, i, :].rearrange("p (t n) -> p t n", n=w.shape[1]),
                                 w.rearrange("(t p) n -> p t n", p=P)).then_inc(w_loaded, 16)

            def gpsimd(pool, t):
                nc.gpsimd.memset(t["magic"][:, :], MAGIC).then_inc(magic_set, 1)
                for k, (c0, n) in enumerate(((0, 1), (1, 2), (3, 1), (4, 1))):
                    pool.wait_ge(amax_part, k + 1)
                    nc.gpsimd.partition_all_reduce(t["aa"][:, c0:c0 + n], t["ar"][:, c0:c0 + n], P, ABSMAX
                                                   ).then_inc(amax_all, 1)
                    if k == 2:
                        with pool.Fori(0, NS // 2, 1) as it:
                            for i in range(NI):
                                pool.wait_ge(u_round, it * NI + i + 4)
                                nc.gpsimd.tensor_tensor(t["a"][i % 2][:, :], t["a"][i % 2][:, :],
                                                        t["magic"][:, :].broadcast_to((P, 2 * SC)), ALU.subtract
                                                        ).then_inc(u_int, 1)

            def gate_up_weights(t):
                for w, b0 in ((t["wg"], 0), (t["wu"], 3)):
                    for kt in range(KT):
                        src = psum[:, b0:b0 + 3, :].rearrange("p a (f k m) -> p (a f) k m", f=2, k=KT)
                        hi, lo = (w[i][:, kt, :].rearrange("p (f m) -> p f m", f=FT) for i in (HI, LO))
                        yield hi, lo, src[:, :, kt, :]

            def bank_pair(i):
                return psum[:, 2 * (i % 3):2 * (i % 3) + 2, :]

            def product(w, xq, s, pr, i, done):
                for e in range(2):
                    f = pr * 2 + e
                    for kt in range(KT):
                        for k, (pw, px) in enumerate(SPLIT):
                            ins = nc.tensor.matmul(psum[:, 2 * (i % 3) + e, :], w[pw][:, kt, f * P:(f + 1) * P],
                                                   xq[px][:, kt, bass.ds(s * SC, SC)],
                                                   start=(kt == 0 and k == 0), stop=(kt == KT - 1 and k == 2))
                ins.then_inc(done, 1)

            def tensor(pe, t):
                pe.wait_ge(w_quant, 3)
                for i in range(2):
                    for f in range(FT):
                        for kt in range(KT):
                            idx = (i * FT + f) * KT + kt
                            ins = nc.tensor.transpose(psum[:, idx // 4, (idx % 4) * P:(idx % 4 + 1) * P],
                                                      t["wq"][:, i, f * D + kt * P:f * D + (kt + 1) * P], ident[:, :])
                ins.then_inc(w_ps, 1)
                pe.wait_ge(w_sb_done, 1)
                for ot in range(KT):
                    for f in range(FT):
                        idx = f * KT + ot
                        ins = nc.tensor.transpose(psum[:, idx // 4, (idx % 4) * P:(idx % 4 + 1) * P],
                                                  t["wq"][:, 2, ot * F + f * P:ot * F + (f + 1) * P], ident[:, :])
                ins.then_inc(w_ps, 1)
                pe.wait_ge(w_sb_done, 2)
                pe.sem_inc(xt_ps, 1)
                with pe.Fori(0, NS, 1) as s:
                    pe.wait_ge(xn_ready, s + 1)
                    pe.wait_ge(xt_sb, s + 1)
                    for kt in range(KT):
                        for j in range(TS):
                            ins = nc.tensor.transpose(psum[:, kt, j * P:(j + 1) * P],
                                                      t["xn"][:, j, kt * P:(kt + 1) * P], ident[:, :])
                    ins.then_inc(xt_ps, 1)
                with pe.Fori(0, NS, 1) as s:
                    pe.wait_ge(x_quant, s + 1)
                    for i in range(NI):
                        pe.wait_ge(m_used, s * NI + i + 1)
                        product((t["wg"], t["wu"])[i // NP], t["xq"], s, i % NP, i, m_ps)
                pe.wait_ge(m_used, NS * NI + 3)
                with pe.Fori(0, NS // 2, 1) as it:
                    for i in range(NI):
                        pe.wait_ge(g_round, it * NI + i + 1)
                        product(t["wg"], t["xq"], it * 2 + i // NP, i % NP, i, g_ps)
                pe.wait_ge(g_round, NS // 2 * NI + 3)
                with pe.Fori(0, NS // 2, 1) as it:
                    for i in range(NI):
                        pe.wait_ge(u_round, it * NI + i + 1)
                        product(t["wu"], t["xq"], it * 2 + i // NP, i % NP, i, u_ps)
                pe.wait_ge(u_round, NS // 2 * NI + 3)
                pe.sem_inc(d_ps, 2)
                with pe.Fori(0, NS // 2, 1) as it:
                    for j in range(2):
                        pe.wait_ge(o_int, NP * (it * 2 + j) + NP + 2)
                        pe.wait_ge(d_added, it * 2 + j + 1)
                        for m in range(TS):
                            for f in range(FT):
                                for k, (po, pw) in enumerate(SPLIT):
                                    ins = nc.tensor.matmul(psum[:, 2 * j + m // 2, (m % 2) * D:(m % 2 + 1) * D],
                                                           t["os"][j][po][:, f, m * P:(m + 1) * P], t["wd"][pw][:, f, :],
                                                           start=(f == 0 and k == 0), stop=(f == FT - 1 and k == 2))
                        ins.then_inc(d_ps, 1)

            def scalar(act, t):
                act.wait_ge(w_ps, 1)
                for hi, lo, src in gate_up_weights(t):
                    ins = nc.scalar.mul(hi, src, W_UP)
                ins.then_inc(w_hi, 1)
                act.wait_ge(w_ps, 2)
                nc.scalar.mul(t["wd"][HI][:, :, :], psum[:, 0:3, :].rearrange("p a (f n) -> p (a f) n", f=2), W_UP
                              ).then_inc(w_hi, 1)
                act.wait_ge(magic_set, 1)
                act.sem_inc(xt_sb, 1)
                act.sem_inc(g_round, 3)
                act.sem_inc(u_round, 3)
                with act.Fori(0, NS, 1) as s:
                    wait_apart(act, xt_ps, s + 2)
                    nc.scalar.copy(t["xt"][:, :, bass.ds(s * SC, SC)], psum[:, 0:2, :]).then_inc(xt_sb, 1)
                magic = t["magic"][:, 0:1]
                act.wait_ge(scaled, 2)
                with act.Fori(0, NS // 2, 1) as it:
                    def round_gate(i):
                        act.wait_ge(g_ps, it * NI + i + 1)
                        if i >= 2:
                            act.wait_ge(g_val, it * NI + i - 1)
                        nc.scalar.activation(t["a"][i % 2][:, :].rearrange("p (a n) -> p a n", a=2), bank_pair(i),
                                             ACT.Identity, bias=magic, scale=t["sc"][:, GATE_BY:GATE_BY + 1]
                                             ).then_inc(g_round, 1)

                    def sigmoid(i):
                        act.wait_ge(g_val, it * NI + i + 1)
                        act.wait_ge(g_prod, it * NI + i + 1)
                        nc.scalar.activation(t["c"][i % 2][:, :], t["b"][i % 2][:, :], ACT.Sigmoid).then_inc(g_sig, 1)
                        act.wait_ge(g_sig, it * NI + i + 1)
                        nc.scalar.activation(t["c"][i % 2][:, :], t["c"][i % 2][:, :], ACT.Identity,
                                             bias=magic, scale=SIG_STEPS).then_inc(g_y, 1)

                    for i in range(NI):
                        round_gate(i)
                        if i >= 1:
                            sigmoid(i - 1)
                    sigmoid(NI - 1)
                act.wait_ge(scaled, 3)
                with act.Fori(0, NS // 2, 1) as it:
                    for i in range(NI):
                        s, pr = it * 2 + i // NP, i % NP
                        wait_apart(act, u_prod, it * NI + i + 1)
                        nc.scalar.activation(t["b"][i % 2][:, :].rearrange("p (e n) -> p e n", e=2),
                                             t["p"][:, 2 * pr:2 * pr + 2, bass.ds(s * SC, SC)], ACT.Identity,
                                             bias=magic, scale=t["sc"][:, GATED_BY:GATED_BY + 1]).then_inc(p_round, 1)
                        act.wait_ge(u_ps, it * NI + i + 1)
                        nc.scalar.activation(t["a"][i % 2][:, :].rearrange("p (a n) -> p a n", a=2), bank_pair(i),
                                             ACT.Identity, bias=magic, scale=t["sc"][:, UP_BY:UP_BY + 1]
                                             ).then_inc(u_round, 1)
                act.wait_ge(scaled, 4)
                with act.Fori(0, NS // 2, 1) as it:
                    for i in range(NI):
                        s, pr = it * 2 + i // NP, i % NP
                        wait_apart(act, o_int, it * NI + i + 1)
                        nc.scalar.activation(t["a"][i % 2][:, :].rearrange("p (e n) -> p e n", e=2),
                                             t["p"][:, 2 * pr:2 * pr + 2, bass.ds(s * SC, SC)],
                                             ACT.Identity, bias=magic, scale=t["sc"][:, OUT_BY:OUT_BY + 1]
                                             ).then_inc(o_round, 1)

            def vector(dve, t):
                nb = F * D // P // QBLOCK
                blocked = [t[n_][:, :, :].rearrange("p i (b q) -> p (i b) q", q=QBLOCK) for n_ in ("raw", "wq")]
                wam, wsc = (t[n_][:, :, :].rearrange("p i b -> p (i b)") for n_ in ("wam", "wsc"))
                dve.wait_ge(w_loaded, 48)
                nc.vector.tensor_reduce(wam, blocked[0], X, ALU.max, apply_absolute_value=True).then_inc(w_amax, 1)
                dve.wait_ge(w_amax, 1)
                nc.vector.tensor_scalar(wsc, wam, 1.0 / W_QMAX, TINY, ALU.mult, ALU.max).then_inc(w_step_done, 1)
                dve.wait_ge(w_step_done, 1)
                nc.vector.reciprocal(wam, wsc).then_inc(w_recip, 1)
                dve.wait_ge(w_recip, 1)
                shape = (P, 3 * nb, QBLOCK)
                nc.vector.tensor_tensor(blocked[1], blocked[0], wam.unsqueeze(2).broadcast_to(shape), ALU.mult
                                        ).then_inc(w_div, 1)
                dve.wait_ge(w_div, 1)
                flat = t["wq"][:, :, :].rearrange("p i n -> p (i n)")
                nc.vector.tensor_scalar(flat, flat, MAGIC, MAGIC, ALU.add, ALU.subtract).then_inc(w_round, 1)
                dve.wait_ge(w_round, 1)
                nc.vector.tensor_tensor(blocked[1], blocked[1], wsc.unsqueeze(2).broadcast_to(shape), ALU.mult
                                        ).then_inc(w_quant, 3)
                nc.vector.memset(t["acc"][:, :], 0.0).then_inc(acc_set, 1)
                dve.wait_ge(acc_set, 1)
                dve.wait_ge(w_hi, 1)
                for hi, lo, src in gate_up_weights(t):
                    ins = nc.vector.scalar_tensor_tensor(lo, src, W_UP, hi, ALU.mult, ALU.subtract)
                ins.then_inc(w_sb_done, 1)
                dve.wait_ge(w_hi, 2)
                nc.vector.scalar_tensor_tensor(t["wd"][LO][:, :, :], psum[:, 0:3, :].rearrange("p a (f n) -> p (a f) n", f=2),
                                               W_UP, t["wd"][HI][:, :, :], ALU.mult, ALU.subtract).then_inc(w_sb_done, 1)

                def keep_max(n, count):
                    nc.vector.tensor_tensor(t["acc"][:, 0:n], t["acc"][:, 0:n], t["am"][:, 0:n], ALU.max
                                            ).then_inc(fold, 1)
                    dve.wait_ge(fold, count)

                def whole_max(k, groups):
                    for c, lo, hi in groups:
                        ins = nc.vector.tensor_reduce(t["ar"][:, c:c + 1], t["acc"][:, lo:hi], X, ALU.max)
                    ins.then_inc(amax_part, 1)
                    dve.wait_ge(amax_all, k)
                    nc.vector.memset(t["acc"][:, :], 0.0)

                steps = [0]

                def small(ins):
                    steps[0] += 1
                    ins.then_inc(sc_step, 1)
                    dve.wait_ge(sc_step, steps[0])

                def col(i):
                    return t["sc"][:, i:i + 1]

                def whole(i):
                    return t["aa"][:, i:i + 1]

                with dve.Fori(0, NS, 1) as s:
                    dve.wait_ge(xt_ps, s + 1)
                    for j in range(TS):
                        ins = nc.vector.tensor_scalar(t["xn"][:, j, :], x_sb[:, s * TS + j, :],
                                                      mv[:, s * TS + j, 0:1], rstd[:, bass.ds(s * TS + j, 1)],
                                                      ALU.subtract, ALU.mult)
                    ins.then_inc(xn_ready, 1)
                    dve.wait_ge(xn_ready, s + 1)
                    nc.vector.tensor_reduce(t["am"][:, 0:1], t["xn"][:, :, :].rearrange("p t n -> p (t n)"), X,
                                            ALU.max, apply_absolute_value=True).then_inc(x_max, 1)
                    dve.wait_ge(x_max, s + 1)
                    keep_max(1, s + 1)
                whole_max(1, ((0, 0, 1),))
                small(nc.vector.tensor_scalar(col(X_STEP), whole(0), 1.0 / QMAX, TINY, ALU.mult, ALU.max))
                small(nc.vector.reciprocal(col(X_BY), col(X_STEP)))
                small(nc.vector.tensor_scalar(col(X_STEP), col(X_STEP), 1.0 / W_UP, None, ALU.mult))
                dve.wait_ge(xt_sb, NS + 1)
                for s in range(NS):
                    xt = t["xt"][:, :, s * SC:(s + 1) * SC]
                    hi, lo = (x[:, :, s * SC:(s + 1) * SC] for x in t["xq"])
                    nc.vector.tensor_scalar(xt, xt, col(X_BY), MAGIC, ALU.mult, ALU.add).then_inc(x_round, 1)
                    dve.wait_ge(x_round, s + 1)
                    nc.vector.tensor_scalar(hi, xt, MAGIC, None, ALU.subtract).then_inc(x_hi, 1)
                    dve.wait_ge(x_hi, s + 1)
                    nc.vector.scalar_tensor_tensor(lo, xt, MAGIC, hi, ALU.subtract, ALU.subtract).then_inc(x_quant, 1)
                dve.sem_inc(m_used, 3)
                with dve.Fori(0, NS, 1) as s:
                    for i in range(NI):
                        dve.wait_ge(m_ps, s * NI + i + 1)
                        nc.vector.tensor_reduce(t["am"][:, i:i + 1], bank_pair(i), mybir.AxisListType.XY, ALU.max,
                                                apply_absolute_value=True).then_inc(m_used, 1)
                    dve.wait_ge(m_used, s * NI + NI + 3)
                    keep_max(NI, s + NS + 1)
                whole_max(2, ((1, 0, NP), (2, NP, NI)))
                for c, step, by in ((1, GATE_STEP, GATE_BY), (2, UP_STEP, UP_BY)):
                    small(nc.vector.tensor_scalar(col(step), whole(c), col(X_STEP), 1.0 / QMAX, ALU.mult, ALU.mult))
                    small(nc.vector.tensor_scalar(col(step), col(step), TINY, None, ALU.max))
                    small(nc.vector.reciprocal(col(by), col(step)))
                    small(nc.vector.tensor_scalar(col(by), col(by), col(X_STEP), None, ALU.mult))
                dve.sem_inc(scaled, 2)
                dve.sem_inc(g_prod, 2)
                with dve.Fori(0, NS // 2, 1) as it:
                    def gate_value(i):
                        dve.wait_ge(g_round, it * NI + i + 4)
                        nc.vector.tensor_scalar(t["b"][i % 2][:, :], t["a"][i % 2][:, :], MAGIC, col(GATE_STEP),
                                                ALU.subtract, ALU.mult).then_inc(g_val, 1)

                    def gated(i):
                        s, pr = it * 2 + i // NP, i % NP
                        c = t["c"][i % 2][:, :]
                        dve.wait_ge(g_y, it * NI + i + 1)
                        nc.vector.tensor_scalar(c, c, MAGIC + SIG_STEPS - 1, MAGIC, ALU.min, ALU.subtract
                                                ).then_inc(g_clip, 1)
                        dve.wait_ge(g_clip, it * NI + i + 1)
                        dst = t["p"][:, 2 * pr:2 * pr + 2, bass.ds(s * SC, SC)]
                        nc.vector.tensor_tensor(dst, c.rearrange("p (e n) -> p e n", e=2),
                                                t["b"][i % 2][:, :].rearrange("p (e n) -> p e n", e=2), ALU.mult
                                                ).then_inc(g_prod, 1)
                        wait_apart(dve, g_prod, it * NI + i + 3)
                        nc.vector.tensor_reduce(t["am"][:, i:i + 1], dst, mybir.AxisListType.XY, ALU.max,
                                                apply_absolute_value=True).then_inc(g_max, 1)

                    for i in range(NI):
                        gate_value(i)
                        if i >= 1:
                            gated(i - 1)
                    gated(NI - 1)
                    dve.wait_ge(g_max, it * NI + NI)
                    keep_max(NI, it + 2 * NS + 1)
                whole_max(3, ((3, 0, NI),))
                small(nc.vector.tensor_scalar(col(GATED_STEP), whole(3), 1.0 / SIG_STEPS, 1.0 / QMAX, ALU.mult, ALU.mult))
                small(nc.vector.tensor_scalar(col(GATED_STEP), col(GATED_STEP), TINY, None, ALU.max))
                small(nc.vector.reciprocal(col(GATED_BY), col(GATED_STEP)))
                small(nc.vector.tensor_scalar(col(GATED_BY), col(GATED_BY), 1.0 / SIG_STEPS, None, ALU.mult))
                dve.sem_inc(scaled, 1)
                dve.sem_inc(u_prod, 2)
                with dve.Fori(0, NS // 2, 1) as it:
                    def product_up(i):
                        s, pr = it * 2 + i // NP, i % NP
                        dst = t["p"][:, 2 * pr:2 * pr + 2, bass.ds(s * SC, SC)]
                        dve.wait_ge(p_round, it * NI + i + 1)
                        wait_apart(dve, u_int, it * NI + i + 1)
                        nc.vector.scalar_tensor_tensor(dst, t["b"][i % 2][:, :].rearrange("p (e n) -> p e n", e=2), MAGIC,
                                                       t["a"][i % 2][:, :].rearrange("p (e n) -> p e n", e=2),
                                                       ALU.subtract, ALU.mult).then_inc(u_prod, 1)
                        wait_apart(dve, u_prod, it * NI + i + 3)
                        nc.vector.tensor_reduce(t["am"][:, i:i + 1], dst, mybir.AxisListType.XY, ALU.max,
                                                apply_absolute_value=True).then_inc(u_max, 1)

                    for i in range(NI):
                        product_up(i)
                    dve.wait_ge(u_max, it * NI + NI)
                    keep_max(NI, it + 2 * NS + NS // 2 + 1)
                whole_max(4, ((4, 0, NI),))
                small(nc.vector.tensor_scalar(col(PROD_STEP), col(GATED_STEP), col(UP_STEP), None, ALU.mult))
                small(nc.vector.tensor_scalar(col(OUT_STEP), whole(4), col(PROD_STEP), 1.0 / QMAX, ALU.mult, ALU.mult))
                small(nc.vector.tensor_scalar(col(OUT_STEP), col(OUT_STEP), TINY, None, ALU.max))
                small(nc.vector.reciprocal(col(OUT_BY), col(OUT_STEP)))
                small(nc.vector.tensor_scalar(col(OUT_BY), col(OUT_BY), col(PROD_STEP), None, ALU.mult))
                small(nc.vector.tensor_scalar(col(OUT_STEP), col(OUT_STEP), 1.0 / W_UP, None, ALU.mult))
                dve.sem_inc(scaled, 1)
                dve.sem_inc(d_added, 2)
                dve.sem_inc(o_int, 2)
                with dve.Fori(0, NS // 2, 1) as it:
                    for i in range(NI):
                        j, pr = i // NP, i % NP
                        if pr == 0:
                            dve.wait_ge(d_ps, it * 2 + j + 1)
                        a = t["a"][i % 2][:, :].rearrange("p (e n) -> p e n", e=2)
                        hi, lo = (o[:, 2 * pr:2 * pr + 2, :] for o in t["os"][j])
                        dve.wait_ge(o_round, it * NI + i + 1)
                        nc.vector.tensor_scalar(hi, a, MAGIC, None, ALU.subtract).then_inc(o_hi, 1)
                        dve.wait_ge(o_hi, it * NI + i + 1)
                        nc.vector.scalar_tensor_tensor(lo, a, MAGIC, hi, ALU.subtract, ALU.subtract).then_inc(o_int, 1)
                    for j in range(2):
                        wait_apart(dve, d_ps, it * 2 + j + 3)
                        for e in range(2):
                            xs = x_sb[:, bass.ds((it * 2 + j) * TS + 2 * e, 2), :]
                            o = psum[:, 2 * j + e, :].rearrange("p (m d) -> p m d", m=2)
                            ins = nc.vector.scalar_tensor_tensor(xs, o, col(OUT_STEP), xs, ALU.mult, ALU.add)
                        ins.then_inc(d_added, 1)

            return alloc, sync, gpsimd, tensor, scalar, vector

        def experts():
            NE, NX, FI = 8, 10, 352
            FTS = [(0, 128), (128, 128), (256, 96)]
            raw_loaded = [sem(f"xw_raw{i}") for i in range(2)]
            xw_ps, w_hi, w_lo, r_loaded, r_ps, r_sb = (sem("w_ps"), sem("w_hi"), sem("xw_lo"), sem("xr_loaded"),
                                                          sem("xr_ps"), sem("xr_sb"))
            xn_ready, xt_ps, xt_sb, xt_kept, l_ps, l_sb = (sem("xn_ready"), sem("xt_ps"), sem("xt_sb"), sem("xxt_kept"),
                                                          sem("xl_ps"), sem("xl_sb"))
            step, exp_done, tri_set = sem("router_step"), sem("exp_done"), sem("tri_set")
            h_hi, h_lo = sem("h_hi"), sem("h_lo")
            gu_ps, silu_done, h_done, dn_ps, x_done = sem("gu_ps"), sem("silu_done"), sem("xh_done"), sem("dn_ps"), sem("x_done")

            def alloc(stack):
                t = {"wg": [sb(f"xwg{i}", [P, NX, KT, FI], F16, stack=stack) for i in (HI, LO)],
                     "wu": [sb(f"xwu{i}", [P, NX, KT, FI], F16, stack=stack) for i in (HI, LO)],
                     "wd": [sb(f"xwd{i}", [P, NX, 3, D], F16, stack=stack) for i in (HI, LO)],
                     "xt": [sb(f"xx_t{i}", [P, KT, B * S], F16, stack=stack) for i in (HI, LO)],
                     "wts": sb("expert_weights", [P, NT, NX], stack=stack)}
                with ExitStack() as inner:
                    t["raw_g"] = [sb(f"raw_g{i}", [P, 3, D], stack=inner) for i in range(2)]
                    t["raw_u"] = [sb(f"raw_u{i}", [P, 3, D], stack=inner) for i in range(2)]
                    t["raw_d"] = [sb(f"raw_d{i}", [P, 2, FI], stack=inner) for i in range(2)]
                    t["raw_r"] = sb("raw_r", [NE + 1, D], stack=inner)
                    t["wr"] = sb("router_w", [P, KT, NE + 1], stack=inner)
                    t["xn"] = sb("xxn", [P, TS, D], stack=inner)
                    t["xs"] = sb("xxt_step", [P, KT, SC], stack=inner)
                    for name, shape in (("lg", [P, NT, NE + 1]), ("mx", [P, NT]), ("ex", [P, NT, NE]), ("sg", [P, NT]),
                                        ("sum", [P, NT]), ("gt", [P, NT, NE, NE]), ("eq", [P, NT, NE, NE]),
                                        ("rank", [P, NT, NE]), ("tri", [P, NE, NE])):
                        t[name] = sb(f"router_{name}_", shape, stack=inner)
                with ExitStack() as inner:
                    t["s"] = [sb(f"silu{i}", [P, SC], stack=inner) for i in range(3)]
                    t["h"] = [sb(f"xh{i}", [P, SC], stack=inner) for i in range(3)]
                    t["hs"] = [[sb(f"xh_{i}_{part}", [P, 3, SC], F16, stack=inner) for part in (HI, LO)]
                               for i in range(2)]
                return t

            def sources(e):
                if e < NE:
                    gu = a["L1_ffn_experts_gate_up"][e]
                    return gu[0:FI, :], gu[FI:2 * FI, :], a["L1_ffn_experts_down"][e]
                lo = (e - NE) * FI
                return (a["L1_ffn_shared_gate_w"][lo:lo + FI, :], a["L1_ffn_shared_up_w"][lo:lo + FI, :],
                        a["L1_ffn_shared_down_w"][:, lo:lo + FI])

            def sync(sp, t):
                sp.dma_start(t["raw_r"][0:NE, :], a["L1_ffn_gate_w"]).then_inc(r_loaded, 16)
                sp.dma_start(t["raw_r"][NE:NE + 1, :], a["L1_ffn_shared_expert_gate_w"]).then_inc(r_loaded, 16)
                for e in range(NX):
                    if e >= 2:
                        sp.wait_ge(xw_ps, e - 1)
                    g, u, d = sources(e)
                    for raw, w in ((t["raw_g"], g), (t["raw_u"], u)):
                        sp.dma_start(raw[e % 2][:, 0:2, :], w[0:2 * P, :].rearrange("(t p) n -> p t n", p=P)
                                     ).then_inc(raw_loaded[e % 2], 16)
                        sp.dma_start(raw[e % 2][0:FI - 2 * P, 2, :], w[2 * P:FI, :]).then_inc(raw_loaded[e % 2], 16)
                    sp.dma_start(t["raw_d"][e % 2][:, :, :], d.rearrange("(t p) f -> p t f", p=P)
                                 ).then_inc(raw_loaded[e % 2], 16)
                out_t = tokens(out)
                with sp.Fori(0, NS, 1) as s:
                    sp.wait_ge(x_done, (s + 1) * NX + 1)
                    sp.dma_start(out_t[:, bass.ds(s * TS, TS), :], x_sb[:, bass.ds(s * TS, TS), :]).then_inc(out_stored, 16)
                sp.wait_ge(out_stored, 16 * NS)

            def gpsimd(pool, t):
                nc.gpsimd.memset(t["tri"][:, :, :], 1.0).then_inc(tri_set, 1)
                pool.wait_ge(tri_set, 1)
                nc.gpsimd.affine_select(out=t["tri"][:, :, :], in_=t["tri"][:, :, :], compare_op=ALU.is_ge, fill=0.0,
                                        base=-1, pattern=[[1, NE], [-1, NE]], channel_multiplier=0).then_inc(tri_set, 1)
                pool.sem_inc(h_lo, 3)
                with pool.Fori(0, NS, 1) as s:
                    for m in range(3 * NX):
                        e, f = m // 3, m % 3
                        n = FTS[f][1]
                        hs = t["hs"][e % 2]
                        pool.wait_ge(h_hi, s * 3 * NX + m + 1)
                        nc.gpsimd.tensor_tensor(hs[LO][0:n, f, :], t["h"][m % 3][0:n, :], hs[HI][0:n, f, :],
                                                ALU.subtract).then_inc(h_lo, 1)

            def tensor(pe, t):
                pe.wait_ge(r_loaded, 32)
                for kt in range(KT):
                    ins = nc.tensor.transpose(psum[:, 7, kt * 16:kt * 16 + NE + 1], t["raw_r"][:, kt * P:(kt + 1) * P],
                                              ident[0:NE + 1, 0:NE + 1])
                ins.then_inc(r_ps, 1)
                for e in range(NX):
                    pe.wait_ge(raw_loaded[e % 2], 80 * (e // 2 + 1))
                    if e >= 1:
                        pe.wait_ge(w_lo, e)
                    for b0, raw in ((0, t["raw_g"]), (2, t["raw_u"])):
                        for kt in range(KT):
                            for f, (lo, n) in enumerate(FTS):
                                nc.tensor.transpose(psum[:, b0 + kt, lo:lo + n], raw[e % 2][0:n, f, kt * P:(kt + 1) * P],
                                                    ident[0:n, 0:n])
                    for f, (lo, n) in enumerate(FTS):
                        for ot in range(2):
                            ins = nc.tensor.transpose(psum[0:n, 4 + f // 2, (f % 2) * D + ot * P:(f % 2) * D + (ot + 1) * P],
                                                      t["raw_d"][e % 2][:, ot, lo:lo + n], ident[:, :])
                    ins.then_inc(xw_ps, 1)
                pe.wait_ge(w_lo, NX)
                pe.wait_ge(r_sb, 1)
                pe.sem_inc(l_ps, 1)
                pe.sem_inc(xt_ps, 1)
                with pe.Fori(0, NS, 1) as s:
                    pe.wait_ge(xn_ready, s + 1)
                    pe.wait_ge(xt_sb, s + 1)
                    for kt in range(KT):
                        for j in range(TS):
                            ins = nc.tensor.transpose(psum[:, kt, j * P:(j + 1) * P],
                                                      t["xn"][:, j, kt * P:(kt + 1) * P], ident[:, :])
                    ins.then_inc(xt_ps, 1)
                    pe.wait_ge(xt_sb, s + 2)
                    pe.wait_ge(l_sb, s + 1)
                    for j in range(TS):
                        for kt in range(KT):
                            ins = nc.tensor.matmul(psum[:, 2, j * 16:j * 16 + NE + 1], t["xs"][:, kt, j * P:(j + 1) * P],
                                                   t["wr"][:, kt, :], start=(kt == 0), stop=(kt == KT - 1))
                    ins.then_inc(l_ps, 1)
                pe.wait_ge(l_sb, NS + 1)
                pe.wait_ge(xt_kept, NS + 1)
                pe.sem_inc(dn_ps, 2)
                with pe.Fori(0, NS, 1) as s:
                    def gate_up(e):
                        for f, (lo, n) in enumerate(FTS):
                            m = e * 3 + f
                            pe.wait_ge(h_done, s * 3 * NX + m + 1)
                            for i, w in enumerate((t["wg"], t["wu"])):
                                for kt in range(KT):
                                    for k, (pw, px) in enumerate(SPLIT):
                                        ins = nc.tensor.matmul(psum[0:n, 2 * (m % 3) + i, :], w[pw][:, e, kt, lo:lo + n],
                                                               t["xt"][px][:, kt, bass.ds(s * SC, SC)],
                                                               start=(kt == 0 and k == 0), stop=(kt == KT - 1 and k == 2))
                            ins.then_inc(gu_ps, 1)

                    def down(e):
                        pe.wait_ge(h_lo, s * 3 * NX + e * 3 + 3 + 3)
                        pe.wait_ge(x_done, s * NX + e + 1)
                        for j in range(TS):
                            for f, (lo, n) in enumerate(FTS):
                                for k, (ph, pw) in enumerate(SPLIT):
                                    ins = nc.tensor.matmul(psum[:, 6 + j // 2, (j % 2) * D:(j % 2 + 1) * D],
                                                           t["hs"][e % 2][ph][0:n, f, j * P:(j + 1) * P],
                                                           t["wd"][pw][0:n, e, f, :],
                                                           start=(f == 0 and k == 0), stop=(f == 2 and k == 2))
                        ins.then_inc(dn_ps, 1)

                    for e in range(NX):
                        gate_up(e)
                        if e >= 1:
                            down(e - 1)
                    down(NX - 1)

            def scalar(act, t):
                for e in range(NX):
                    act.wait_ge(xw_ps, e + 1)
                    nc.scalar.mul(t["wd"][HI][:, e, 0:2, :].rearrange("p f n -> p (f n)"), psum[:, 4, :], W_UP)
                    nc.scalar.mul(t["wd"][HI][0:FI - 2 * P, e, 2, :], psum[0:FI - 2 * P, 5, 0:D], W_UP)
                    nc.scalar.mul(t["wg"][HI][:, e, :, :], psum[:, 0:2, 0:FI], W_UP)
                    nc.scalar.mul(t["wu"][HI][:, e, :, :], psum[:, 2:4, 0:FI], W_UP).then_inc(w_hi, 1)
                act.sem_inc(xt_sb, 1)
                with act.Fori(0, NS, 1) as s:
                    act.wait_ge(xt_ps, s + 2)
                    act.wait_ge(xt_kept, s + 1)
                    act.wait_ge(l_ps, s + 1)
                    nc.scalar.copy(t["xs"][:, :, :], psum[:, 0:2, :])
                    nc.scalar.copy(t["xt"][HI][:, :, bass.ds(s * SC, SC)], psum[:, 0:2, :]).then_inc(xt_sb, 1)
                act.wait_ge(step, 2)
                nc.scalar.activation(t["ex"][:, :, :], t["ex"][:, :, :], ACT.Exp)
                nc.scalar.activation(t["sg"][:, :], t["lg"][:, :, NE], ACT.Exp, scale=-1.0).then_inc(exp_done, 1)

                def high_part(s, m):
                    e, f = m // 3, m % 3
                    n = FTS[f][1]
                    act.wait_ge(h_done, s * 3 * NX + m + 4)
                    if f == 0:
                        act.wait_ge(dn_ps, s * NX + e + 1)
                    nc.scalar.copy(t["hs"][e % 2][HI][0:n, f, :], t["h"][m % 3][0:n, :]).then_inc(h_hi, 1)

                with act.Fori(0, NS, 1) as s:
                    for m in range(3 * NX):
                        n = FTS[m % 3][1]
                        act.wait_ge(gu_ps, s * 3 * NX + m + 1)
                        act.wait_ge(h_done, s * 3 * NX + m + 1)
                        nc.scalar.activation(t["s"][m % 3][0:n, :], psum[0:n, 2 * (m % 3), :], ACT.Silu,
                                             scale=1.0 / W_UP).then_inc(silu_done, 1)
                        if m >= 1:
                            high_part(s, m - 1)
                    high_part(s, 3 * NX - 1)

            def vector(dve, t):
                dve.wait_ge(r_ps, 1)
                nc.vector.tensor_copy(t["wr"][:, :, :], psum[:, 7, 0:32].rearrange("p (k n) -> p k n", k=2)[:, :, 0:NE + 1]
                                      ).then_inc(r_sb, 1)
                for e in range(NX):
                    dve.wait_ge(w_hi, e + 1)
                    n = FI - 2 * P
                    for dst, part, src in (
                            (t["wd"][LO][:, e, 0:2, :].rearrange("p f n -> p (f n)"),
                             t["wd"][HI][:, e, 0:2, :].rearrange("p f n -> p (f n)"), psum[:, 4, :]),
                            (t["wd"][LO][0:n, e, 2, :], t["wd"][HI][0:n, e, 2, :], psum[0:n, 5, 0:D]),
                            (t["wg"][LO][:, e, :, :], t["wg"][HI][:, e, :, :], psum[:, 0:2, 0:FI]),
                            (t["wu"][LO][:, e, :, :], t["wu"][HI][:, e, :, :], psum[:, 2:4, 0:FI])):
                        ins = nc.vector.scalar_tensor_tensor(dst, src, W_UP, part, ALU.mult, ALU.subtract)
                    ins.then_inc(w_lo, 1)
                dve.sem_inc(l_sb, 1)
                dve.sem_inc(xt_kept, 1)
                with dve.Fori(0, NS, 1) as s:
                    dve.wait_ge(xt_ps, s + 1)
                    for j in range(TS):
                        ins = nc.vector.tensor_scalar(t["xn"][:, j, :], x_sb[:, s * TS + j, :],
                                                      mv[:, s * TS + j, 0:1], rstd[:, bass.ds(s * TS + j, 1)],
                                                      ALU.subtract, ALU.mult)
                    ins.then_inc(xn_ready, 1)
                    dve.wait_ge(xt_sb, s + 2)
                    rows = bass.ds(s * SC, SC)
                    nc.vector.tensor_tensor(t["xt"][LO][:, :, rows], t["xs"][:, :, :], t["xt"][HI][:, :, rows],
                                            ALU.subtract).then_inc(xt_kept, 1)
                    wait_apart(dve, l_ps, s + 2)
                    nc.vector.tensor_copy(t["lg"][:, bass.ds(s * TS, TS), :],
                                          psum[:, 2, 0:64].rearrange("p (j n) -> p j n", j=TS)[:, :, 0:NE + 1]
                                          ).then_inc(l_sb, 1)
                dve.wait_ge(l_sb, NS + 1)
                lg = t["lg"][:, :, 0:NE]
                steps = [0]

                def small(ins):
                    steps[0] += 1
                    ins.then_inc(step, 1)
                    dve.wait_ge(step, steps[0])

                small(nc.vector.tensor_reduce(t["mx"][:, :], lg, X, ALU.max))
                small(nc.vector.tensor_tensor(t["ex"][:, :, :], lg, t["mx"][:, :].unsqueeze(2).broadcast_to((P, NT, NE)),
                                              ALU.subtract))
                dve.wait_ge(exp_done, 1)
                small(nc.vector.tensor_reduce(t["sum"][:, :], t["ex"][:, :, :], X, ALU.add))
                small(nc.vector.reciprocal(t["mx"][:, :], t["sum"][:, :]))
                small(nc.vector.tensor_tensor(t["ex"][:, :, :], t["ex"][:, :, :],
                                              t["mx"][:, :].unsqueeze(2).broadcast_to((P, NT, NE)), ALU.mult))
                pair = (P, NT, NE, NE)
                of_j = t["ex"][:, :, :].unsqueeze(2).broadcast_to(pair)
                of_i = t["ex"][:, :, :].unsqueeze(3).broadcast_to(pair)
                small(nc.vector.tensor_tensor(t["gt"][:, :, :, :], of_j, of_i, ALU.is_gt))
                small(nc.vector.tensor_tensor(t["eq"][:, :, :, :], of_j, of_i, ALU.is_equal))
                dve.wait_ge(tri_set, 2)
                eq = t["eq"][:, :, :, :].rearrange("p t i j -> p t (i j)")
                small(nc.vector.tensor_tensor(eq, eq, t["tri"][:, :, :].rearrange("p i j -> p (i j)").unsqueeze(1)
                                              .broadcast_to((P, NT, NE * NE)), ALU.mult))
                small(nc.vector.tensor_tensor(t["gt"][:, :, :, :], t["gt"][:, :, :, :], t["eq"][:, :, :, :], ALU.add))
                small(nc.vector.tensor_reduce(t["rank"][:, :, :], t["gt"][:, :, :, :], X, ALU.add))
                small(nc.vector.tensor_scalar(t["rank"][:, :, :], t["rank"][:, :, :], 1.5, None, ALU.is_lt))
                small(nc.vector.tensor_tensor(t["wts"][:, :, 0:NE], t["ex"][:, :, :], t["rank"][:, :, :], ALU.mult))
                small(nc.vector.tensor_scalar(t["sum"][:, :], t["sg"][:, :], 1.0, None, ALU.add))
                small(nc.vector.reciprocal(t["mx"][:, :], t["sum"][:, :]))
                small(nc.vector.tensor_copy(t["wts"][:, :, NE:NX], t["mx"][:, :].unsqueeze(2).broadcast_to((P, NT, 2))))
                small(nc.vector.tensor_scalar(t["wts"][:, :, :], t["wts"][:, :, :], 1.0 / W_UP, None, ALU.mult))
                dve.sem_inc(h_done, 3)
                dve.sem_inc(x_done, 1)
                with dve.Fori(0, NS, 1) as s:
                    def gated(e):
                        for f, (lo, n) in enumerate(FTS):
                            m = e * 3 + f
                            dve.wait_ge(silu_done, s * 3 * NX + m + 1)
                            dve.wait_ge(h_lo, s * 3 * NX + m + 1)
                            nc.vector.scalar_tensor_tensor(t["h"][m % 3][0:n, :], psum[0:n, 2 * (m % 3) + 1, :],
                                                           1.0 / W_UP, t["s"][m % 3][0:n, :], ALU.mult, ALU.mult
                                                           ).then_inc(h_done, 1)

                    def add(e):
                        wait_apart(dve, dn_ps, s * NX + e + 3)
                        for j in range(TS):
                            xs = x_sb[:, s * TS + j, :]
                            ins = nc.vector.scalar_tensor_tensor(xs, psum[:, 6 + j // 2, (j % 2) * D:(j % 2 + 1) * D],
                                                                 t["wts"][:, s * TS + j, e:e + 1], xs, ALU.mult, ALU.add)
                        ins.then_inc(x_done, 1)

                    for e in range(NX):
                        gated(e)
                        if e >= 1:
                            add(e - 1)
                    add(NX - 1)

            return alloc, sync, gpsimd, tensor, scalar, vector

        stats0_v, stats0_s = norm_stats(0)
        proj0 = projections(0, a["L0_xattn_Wq"], a["L0_xattn_Wk"], a["L0_xattn_Wv"],
                            a["L0_xattn_bq"], a["L0_xattn_bk"], a["L0_xattn_bv"])
        rel_alloc, rel_alloc_raw, rel_sync, rel_pool, rel_pe, rel_dve, rel_ready = relative_tables()
        with ExitStack() as rel_stack:
            rel_t = rel_alloc(rel_stack)
            with ExitStack() as stack:
                rel_alloc_raw(stack, rel_t)
                proj0_t = proj0[0](stack)
            att0 = attention(0, True, rel_t, rel_ready)
            with ExitStack() as stack:
                att0_t = att0[0](stack)
        fc0 = merge_heads(0, a["L0_xattn_W_fc"], False, (h_dr, r_dr), a["L0_xattn_b_fc"])
        with ExitStack() as stack:
            fc0_t = fc0[0](stack)
        stats1_v, stats1_s = norm_stats(1)
        ffn0 = quantised_ffn()
        with ExitStack() as stack:
            ffn0_t = ffn0[0](stack)
        stats2_v, stats2_s = norm_stats(2)
        proj1 = projections(1, a["L1_xattn_Wq"], a["L1_xattn_Wk"], a["L1_xattn_Wv"])
        with ExitStack() as stack:
            proj1_t = proj1[0](stack)
        att1 = attention(1, False)
        with ExitStack() as stack:
            att1_t = att1[0](stack)
        fc1 = merge_heads(1, a["L1_xattn_Wout"], True, (h_dr,))
        with ExitStack() as stack:
            fc1_t = fc1[0](stack)
        stats3_v, stats3_s = norm_stats(3)
        moe = experts()
        with ExitStack() as stack:
            moe_t = moe[0](stack)

        kept = {"phase_end", "phase_begun", "out_stored", "x_loaded", "consts_set"}

        def clear(pool):
            for name, used in semaphores.items():
                if name not in kept:
                    pool.sem_clear(used)

        blk = ctx.enter_context(nc.Block())

        @blk.sync
        def _(sp):
            x_t = tokens(a["x"])
            for i in range(4):
                sp.dma_start(x_sb[:, i * 8:(i + 1) * 8, :], x_t[:, i * 8:(i + 1) * 8, :]).then_inc(x_loaded, 16)
            rel_sync(sp, rel_t)
            proj0[1](sp, proj0_t)
            phase_barrier(sp, 0)
            att0[1](sp, att0_t)
            phase_barrier(sp, 1)
            fc0[1](sp, fc0_t)
            phase_barrier(sp, 2)
            phase_barrier(sp, 3)
            ffn0[1](sp, ffn0_t)
            phase_barrier(sp, 4)
            phase_barrier(sp, 5)
            proj1[1](sp, proj1_t)
            phase_barrier(sp, 6)
            att1[1](sp, att1_t)
            phase_barrier(sp, 7)
            fc1[1](sp, fc1_t)
            phase_barrier(sp, 8)
            phase_barrier(sp, 9)
            moe[1](sp, moe_t)

        @blk.gpsimd
        def _(pool):
            nc.gpsimd.memset(ident[:, :], 0.0)
            nc.gpsimd.memset(block[:, :], 1.0)
            nc.gpsimd.memset(block_rev[:, :], 1.0)
            nc.gpsimd.memset(eps[:, :], EPS).then_inc(consts_set, 1)
            pool.wait_ge(consts_set, 1)
            nc.gpsimd.affine_select(out=ident[:, :], in_=ident[:, :], compare_op=ALU.not_equal, fill=1.0, base=0,
                                    pattern=[[-1, P]], channel_multiplier=1)
            nc.gpsimd.affine_select(out=block[:, :], in_=block[:, :], compare_op=ALU.is_ge, fill=0.0, base=0,
                                    pattern=[[-16, 8]], channel_multiplier=1)
            nc.gpsimd.affine_select(out=block_rev[:, :], in_=block_rev[:, :], compare_op=ALU.is_ge, fill=0.0,
                                    base=-112, pattern=[[16, 8]], channel_multiplier=1).then_inc(consts_set, 1)
            pool.wait_ge(consts_set, 2)
            nc.gpsimd.affine_select(out=block[:, :], in_=block[:, :], compare_op=ALU.is_ge, fill=0.0, base=15,
                                    pattern=[[16, 8]], channel_multiplier=-1)
            nc.gpsimd.affine_select(out=block_rev[:, :], in_=block_rev[:, :], compare_op=ALU.is_ge, fill=0.0,
                                    base=127, pattern=[[-16, 8]], channel_multiplier=-1).then_inc(consts_set, 1)
            rel_pool(pool, rel_t)
            phase_barrier(pool, 0)
            att0[2](pool, att0_t)
            phase_barrier(pool, 1)
            fc0[2](pool, fc0_t)
            phase_barrier(pool, 2)
            clear(pool)
            phase_barrier(pool, 3)
            ffn0[2](pool, ffn0_t)
            phase_barrier(pool, 4)
            clear(pool)
            phase_barrier(pool, 5)
            phase_barrier(pool, 6)
            att1[2](pool, att1_t)
            phase_barrier(pool, 7)
            fc1[2](pool, fc1_t)
            phase_barrier(pool, 8)
            clear(pool)
            phase_barrier(pool, 9)
            moe[2](pool, moe_t)

        @blk.scalar
        def _(act):
            act.wait_ge(consts_set, 3)
            stats0_s(act)
            proj0[3](act, proj0_t)
            phase_barrier(act, 0)
            att0[4](act, att0_t)
            phase_barrier(act, 1)
            fc0[4](act, fc0_t)
            phase_barrier(act, 2)
            phase_barrier(act, 3)
            stats1_s(act)
            ffn0[4](act, ffn0_t)
            phase_barrier(act, 4)
            phase_barrier(act, 5)
            stats2_s(act)
            proj1[3](act, proj1_t)
            phase_barrier(act, 6)
            att1[4](act, att1_t)
            phase_barrier(act, 7)
            fc1[4](act, fc1_t)
            phase_barrier(act, 8)
            phase_barrier(act, 9)
            stats3_s(act)
            moe[4](act, moe_t)

        @blk.vector
        def _(dve):
            dve.wait_ge(x_loaded, 64)
            dve.wait_ge(consts_set, 3)
            rel_dve(dve, rel_t)
            stats0_v(dve)
            proj0[4](dve, proj0_t)
            phase_barrier(dve, 0)
            att0[5](dve, att0_t)
            phase_barrier(dve, 1)
            fc0[5](dve, fc0_t)
            phase_barrier(dve, 2)
            phase_barrier(dve, 3)
            stats1_v(dve)
            ffn0[5](dve, ffn0_t)
            phase_barrier(dve, 4)
            phase_barrier(dve, 5)
            stats2_v(dve)
            proj1[4](dve, proj1_t)
            phase_barrier(dve, 6)
            att1[5](dve, att1_t)
            phase_barrier(dve, 7)
            fc1[5](dve, fc1_t)
            phase_barrier(dve, 8)
            phase_barrier(dve, 9)
            stats3_v(dve)
            moe[5](dve, moe_t)

        @blk.tensor
        def _(pe):
            pe.wait_ge(consts_set, 3)
            rel_pe(pe, rel_t)
            proj0[2](pe, proj0_t)
            phase_barrier(pe, 0)
            att0[3](pe, att0_t)
            phase_barrier(pe, 1)
            fc0[3](pe, fc0_t)
            phase_barrier(pe, 2)
            phase_barrier(pe, 3)
            ffn0[3](pe, ffn0_t)
            phase_barrier(pe, 4)
            phase_barrier(pe, 5)
            proj1[2](pe, proj1_t)
            phase_barrier(pe, 6)
            att1[3](pe, att1_t)
            phase_barrier(pe, 7)
            fc1[3](pe, fc1_t)
            phase_barrier(pe, 8)
            phase_barrier(pe, 9)
            moe[3](pe, moe_t)


_INS = ['x', 'ctx_1024', 'mask_SxS2_ik1', 'L0_xattn_Wq', 'L0_xattn_bq', 'L0_xattn_Wk', 'L0_xattn_bk', 'L0_xattn_Wv',
        'L0_xattn_bv', 'L0_xattn_pos_k', 'L0_xattn_pos_v', 'L0_xattn_W_fc', 'L0_xattn_b_fc', 'L0_ffn_w_gate',
        'L0_ffn_w_up', 'L0_ffn_w_down', 'L1_xattn_Wv', 'L1_xattn_Wk', 'L1_xattn_Wq', 'L1_xattn_Wout',
        'L1_ffn_gate_w', 'L1_ffn_experts_gate_up', 'L1_ffn_experts_down', 'L1_ffn_shared_gate_w',
        'L1_ffn_shared_up_w', 'L1_ffn_shared_down_w', 'L1_ffn_shared_expert_gate_w']


def kernel(**inputs):
    import numpy as _np
    import concourse.bacc as _bacc
    from concourse import mybir as _mybir
    from concourse.bass_utils import run_bass_kernel_spmd as _run

    nc = _bacc.Bacc("TRN2", target_bir_lowering=False, num_devices=1)
    arrays, aps = {}, {}
    for name in _INS:
        arr = _np.ascontiguousarray(inputs[name])
        arrays[f"in_{name}"] = arr
        aps[name] = nc.dram_tensor(f"in_{name}", arr.shape, _mybir.dt.from_np(arr.dtype), kind="ExternalInput").ap()
    out = nc.dram_tensor("out_0", (16, 256, 256), _mybir.dt.float32, kind="ExternalOutput").ap()
    build(nc, aps, out)
    r = _run(nc, [arrays], core_ids=[0])
    return r.results[0]["out_0"]
```

```python
from contextlib import ExitStack

import concourse.bass as bass
from concourse import mybir

ALU = mybir.AluOpType
ACT = mybir.ActivationFunctionType
F32 = mybir.dt.float32
F16 = mybir.dt.float16
I32 = mybir.dt.int32
X = mybir.AxisListType.X
ABSMAX = bass.bass_isa.ReduceOp.absmax

P = 128
B, S, D = 16, 256, 256
H, DH = 16, 16
K = 64
KT = D // P
NT = B * S // P
SC = 512
NS = B * S // SC
TS = SC // P
EPS = 1e-5
SCALE = DH ** -0.5
MASKED = 1e-20
IN = 8
GN = S // IN
GC = 4
NC = GN // GC
NB2 = 2 * NC
QBLOCK = 32
W_QMAX = 7.0
QMAX = 32767.0
SIG_STEPS = 65536.0
TINY = 1e-12
MAGIC = 1.5 * 2.0 ** 23
X_STEP, X_BY, GATE_STEP, GATE_BY, UP_STEP, UP_BY, GATED_STEP, GATED_BY, PROD_STEP, OUT_STEP, OUT_BY = range(11)
ENGINES = 5
HI, LO = 0, 1
SPLIT = ((HI, HI), (HI, LO), (LO, HI))
W_UP = 64.0
A_UP = 1024.0


def tokens(ap):
    return ap.rearrange("b s d -> (b s) d").rearrange("(t p) d -> p t d", p=P)


def build(nc, a, out):
    with ExitStack() as ctx:
        def sb(name, shape, dt=F32, stack=ctx):
            return stack.enter_context(nc.sbuf_tensor(name, shape, dt))

        semaphores = {}

        def sem(name):
            if name not in semaphores:
                semaphores[name] = ctx.enter_context(nc.semaphore(name))
            return semaphores[name]

        def dram(name, shape, dt=F32):
            return nc.dram_tensor(name, shape, dt, kind="Internal").ap()

        x_sb = sb("x_sb", [P, NT, D])
        ident = sb("ident", [P, P])
        block = sb("block16", [P, 8])
        block_rev = sb("block16_rev", [P, 8])
        stats = sb("stats", [P, NT, 6])
        mv = sb("mv", [P, NT, 2])
        sd = sb("sd", [P, NT])
        rstd = sb("rstd", [P, NT])
        eps = sb("eps", [P, 1])
        psum = ctx.enter_context(nc.psum_tensor("psum", [P, 8, 512], F32))

        q0_dr = dram("q0_dr", [B, H * DH, S, 2], F16)
        q1_dr = [dram(f"q1_dr{i}", [B, H * DH, S], F16) for i in (HI, LO)]
        k_dr = [dram(f"k_dr{i}", [B, H * DH, S], F16) for i in (HI, LO)]
        v_dr = dram("v_dr", [B * S, H * DH])
        h_dr = dram("h_dr", [B, H * DH, S])
        r_dr = dram("r_dr", [B, H * DH, S])
        extv_dr = dram("extv_dr", [2 * S, DH])

        phase_end, phase_begun = sem("phase_end"), sem("phase_begun")
        x_loaded = sem("x_loaded")
        consts_set = sem("consts_set")
        out_stored = sem("out_stored")

        def phase_barrier(eng, k):
            eng.drain().then_inc(phase_end, 1)
            eng.wait_ge(phase_end, ENGINES * (k + 1))
            eng.sem_inc(phase_begun, 1)

        apart = {}

        def wait_apart(eng, semaphore, value):
            if eng not in apart:
                apart[eng] = sem(f"apart_{len(apart)}")
            eng.wait_ge(semaphore, value)
            eng.sem_inc(apart[eng], 1)

        def norm_stats(n):
            stats_done, mv_done = sem("stats_done"), sem("mv_done")
            sd_done, rstd_done = sem("sd_done"), sem("rstd_done")

            def vector(dve):
                with dve.Fori(0, NT // 4, 1) as t:
                    for j in range(4):
                        ins = nc.vector.bn_stats(stats[:, t * 4 + j, :], x_sb[:, t * 4 + j, :])
                    ins.then_inc(stats_done, 1)
                dve.wait_ge(stats_done, NT // 4)
                for t in range(NT):
                    ins = nc.vector.bn_aggr(mv[:, t, :], stats[:, t, :])
                ins.then_inc(mv_done, 1)
                dve.wait_ge(sd_done, 1)
                nc.vector.reciprocal(rstd[:, :], sd[:, :]).then_inc(rstd_done, 1)
                dve.wait_ge(rstd_done, 1)

            def scalar(act):
                act.wait_ge(mv_done, 1)
                nc.scalar.activation(sd[:, :], mv[:, :, 1], ACT.Sqrt, bias=eps[:, 0:1]).then_inc(sd_done, 1)

            return vector, scalar

        def projections(n, wq_ap, wk_ap, wv_ap, bq_ap=None, bk_ap=None, bv_ap=None):
            biased = bq_ap is not None
            xn_ready, ctx_loaded, w_loaded = sem("xn_ready"), sem("ctx_loaded"), sem("w_loaded")
            xt_ps, ct_ps, xt_sb, ct_sb = sem("xt_ps"), sem("ct_ps"), sem("xt_sb"), sem("ct_sb")
            q_ps, k_ps, v_ps = sem("q_ps"), sem("k_ps"), sem("v_ps")
            q_out, k_out, v_out = sem("q_out"), sem("k_out"), sem("v_out")
            q_stored, k_stored, v_stored = sem("q_stored"), sem("k_stored"), sem("v_stored")
            w_ps, w_sb_done, bq_scaled = sem("w_ps"), sem("w_sb_done"), sem("bq_scaled")
            q_hi, k_hi = sem("q_hi"), sem("k_hi")
            w_hi, xt_hi, ct_hi = sem("w_hi"), sem("xt_hi"), sem("ct_hi")
            n_w = 9 if biased else 3
            q_dmas = 2 if biased else 4

            def alloc(stack):
                t = {}
                for name, shape in (("w_raw", [P, 3, KT, D]), ("bqk", [P, 2, 2]),
                                    ("bv", [P, D]), ("xn", [P, TS, D]), ("cin", [P, TS, D]),
                                    ("qo", [P, 2, SC]), ("ko", [P, 2, SC]), ("vo", [P, TS, D])):
                    t[name] = sb(f"{name}{n}", shape, stack=stack)
                for name, shape in (("w", [P, 3, KT, D]), ("xt", [P, KT, SC]), ("ct", [P, KT, SC])):
                    t[name] = [sb(f"{name}{n}_{i}", shape, F16, stack=stack) for i in (HI, LO)]
                if biased:
                    t["q_both"] = sb(f"q_both{n}", [P, 2, SC, 2], F16, stack=stack)
                    t["qs"] = [t["q_both"][:, :, :, i] for i in (HI, LO)]
                else:
                    t["qs"] = [sb(f"q_part{n}_{i}", [P, 2, SC], F16, stack=stack)[:, :, :] for i in (HI, LO)]
                t["ks"] = [sb(f"k_part{n}_{i}", [P, 2, SC], F16, stack=stack)[:, :, :] for i in (HI, LO)]
                return t

            def sync_first(sp, t):
                if biased:
                    for i, w in enumerate((wq_ap, wk_ap, wv_ap)):
                        for kt in range(KT):
                            sp.dma_start(t["w_raw"][:, i, kt, :].rearrange("p (h d) -> p h d", h=H),
                                         w[:, kt * P:(kt + 1) * P, :].rearrange("h p d -> p h d")
                                         ).then_inc(w_loaded, 16)
                    for i, v in enumerate((bq_ap, bk_ap)):
                        sp.dma_start(t["bqk"][:, i, :], v.rearrange("(t h) d -> (h d) t", t=2),
                                     allow_slow_non_contiguous=True).then_inc(w_loaded, 16)
                    sp.dma_start(t["bv"][:, :], bv_ap.rearrange("h d -> (h d)").partition_broadcast(P)
                                 ).then_inc(w_loaded, 16)
                else:
                    for i, w in enumerate((wq_ap, wk_ap, wv_ap)):
                        sp.dma_start(t["w_raw"][:, i, :, :],
                                     w.rearrange("(t p) n -> p t n", p=P)).then_inc(w_loaded, 16)
                sp.dma_start(t["cin"][:, :, :], tokens(a["ctx_1024"])[:, 0:TS, :]).then_inc(ctx_loaded, 16)

            def sync(sp, t):
                ctx_t = tokens(a["ctx_1024"])
                for granted in (q_stored, k_stored, v_stored):
                    sp.sem_inc(granted, 16)
                q0_t = q0_dr.rearrange("b (t p) s e -> p t b (s e)", p=P)
                q1_t = [q.rearrange("b (t p) s -> p t b s", p=P) for q in q1_dr]
                k_t = [k.rearrange("b (t p) s -> p t b s", p=P) for k in k_dr]
                v_t = v_dr.rearrange("(t p) d -> p t d", p=P)
                with sp.Fori(0, NS, 1) as s:
                    sp.wait_ge(ct_ps, s + 1)
                    nxt = (s + 1) % NS
                    sp.dma_start(t["cin"][:, :, :], ctx_t[:, bass.ds(nxt * TS, TS), :]).then_inc(ctx_loaded, 16)
                    sp.wait_ge(q_out, s + 1)
                    for hh in range(2):
                        if biased:
                            sp.dma_start(q0_t[:, hh, bass.ds(2 * s, 2), :],
                                         t["q_both"][:, hh, :, :].rearrange("p (b s) e -> p b (s e)", b=2)
                                         ).then_inc(q_stored, 16)
                        else:
                            for i in (HI, LO):
                                sp.dma_start(q1_t[i][:, hh, bass.ds(2 * s, 2), :],
                                             t["qs"][i][:, hh, :].rearrange("p (b s) -> p b s", b=2)
                                             ).then_inc(q_stored, 16)
                    sp.wait_ge(v_out, s + 2)
                    sp.dma_start(v_t[:, bass.ds(s * TS, TS), :], t["vo"][:, :, :]).then_inc(v_stored, 16)
                    sp.wait_ge(k_out, s + 2)
                    for hh in range(2):
                        for i in (HI, LO):
                            sp.dma_start(k_t[i][:, hh, bass.ds(2 * s, 2), :],
                                         t["ks"][i][:, hh, :].rearrange("p (b s) -> p b s", b=2)
                                         ).then_inc(k_stored, 16)
                sp.wait_ge(q_stored, 16 * q_dmas * NS + 16)
                sp.wait_ge(k_stored, 64 * NS + 16)
                sp.wait_ge(v_stored, 16 * NS + 16)
                sp.wait_ge(ctx_loaded, 16 * (NS + 1))

            def tensor(pe, t):
                def feature_major(which, src):
                    for hh in range(2):
                        for kt in range(KT):
                            for k, (pw, px) in enumerate(SPLIT):
                                ins = nc.tensor.matmul(psum[:, 4 + hh, :], t["w"][pw][:, which, kt, hh * P:(hh + 1) * P],
                                                       src[px][:, kt, :], start=(kt == 0 and k == 0),
                                                       stop=(kt == KT - 1 and k == 2))
                    return ins

                pe.wait_ge(w_loaded, 16 * n_w)
                if not biased:
                    for i in range(3):
                        for ot in range(2):
                            for kt in range(KT):
                                ins = nc.tensor.transpose(psum[:, i * 2 + kt, ot * P:(ot + 1) * P],
                                                          t["w_raw"][:, i, ot, kt * P:(kt + 1) * P], ident[:, :])
                    ins.then_inc(w_ps, 1)
                pe.wait_ge(w_sb_done, 1)

                def transposes(n):
                    pe.wait_ge(xn_ready, n)
                    for kt in range(KT):
                        for j in range(TS):
                            ins = nc.tensor.transpose(psum[:, kt, j * P:(j + 1) * P],
                                                      t["xn"][:, j, kt * P:(kt + 1) * P], ident[:, :])
                    ins.then_inc(xt_ps, 1)
                    pe.wait_ge(ctx_loaded, 16 * n)
                    for kt in range(KT):
                        for j in range(TS):
                            ins = nc.tensor.transpose(psum[:, 2 + kt, j * P:(j + 1) * P],
                                                      t["cin"][:, j, kt * P:(kt + 1) * P], ident[:, :])
                    ins.then_inc(ct_ps, 1)

                transposes(1)
                with pe.Fori(0, NS, 1) as s:
                    pe.wait_ge(xt_sb, s + 1)
                    pe.wait_ge(k_hi, s + 1)
                    feature_major(0, t["xt"]).then_inc(q_ps, 1)
                    pe.wait_ge(ct_sb, s + 1)
                    pe.wait_ge(v_out, s + 1)
                    for j in range(TS):
                        for kt in range(KT):
                            for k, (pc, pw) in enumerate(SPLIT):
                                ins = nc.tensor.matmul(psum[:, 6 + j // 2, (j % 2) * D:(j % 2 + 1) * D],
                                                       t["ct"][pc][:, kt, j * P:(j + 1) * P], t["w"][pw][:, 2, kt, :],
                                                       start=(kt == 0 and k == 0), stop=(kt == KT - 1 and k == 2))
                    ins.then_inc(v_ps, 1)
                    transposes(s + 2)
                    pe.wait_ge(q_hi, s + 1)
                    feature_major(1, t["ct"]).then_inc(k_ps, 1)

            def scalar(act, t):
                if biased:
                    act.wait_ge(w_loaded, 16 * n_w)
                    nc.scalar.mul(t["bqk"][:, 0, :], t["bqk"][:, 0, :], SCALE).then_inc(bq_scaled, 1)
                    act.wait_ge(bq_scaled, 1)
                    ins = nc.scalar.mul(t["w"][HI][:, :, :, :], t["w_raw"][:, :, :, :], W_UP)
                else:
                    act.wait_ge(w_ps, 1)
                    ins = nc.scalar.mul(t["w"][HI][:, :, :, :].rearrange("p i k n -> p (i k) n"), psum[:, 0:6, 0:D], W_UP)
                ins.then_inc(w_hi, 1)
                act.sem_inc(k_hi, 1)

                def evacuate(whole, high, which, scale, done):
                    for dst in (whole, high):
                        for hh in range(2):
                            src = psum[:, 4 + hh, :]
                            if biased:
                                ins = nc.scalar.activation(dst[:, hh, :], src, ACT.Identity,
                                                           bias=t["bqk"][:, which, hh:hh + 1], scale=scale)
                            else:
                                ins = nc.scalar.mul(dst[:, hh, :], src, scale)
                    ins.then_inc(done, 1)

                act.wait_ge(xt_ps, 1)
                nc.scalar.copy(t["xt"][HI][:, :, :], psum[:, 0:2, :]).then_inc(xt_hi, 1)
                act.wait_ge(ct_ps, 1)
                nc.scalar.copy(t["ct"][HI][:, :, :], psum[:, 2:4, :]).then_inc(ct_hi, 1)
                with act.Fori(0, NS, 1) as s:
                    act.wait_ge(q_ps, s + 1)
                    act.wait_ge(q_stored, 16 * q_dmas * s + 16)
                    evacuate(t["qo"], t["qs"][HI], 0, SCALE / W_UP, q_hi)
                    act.wait_ge(xt_ps, s + 2)
                    nc.scalar.copy(t["xt"][HI][:, :, :], psum[:, 0:2, :]).then_inc(xt_hi, 1)
                    act.wait_ge(k_ps, s + 1)
                    act.wait_ge(k_stored, 64 * s + 16)
                    evacuate(t["ko"], t["ks"][HI], 1, 1.0 / W_UP, k_hi)
                    act.wait_ge(ct_ps, s + 2)
                    nc.scalar.copy(t["ct"][HI][:, :, :], psum[:, 2:4, :]).then_inc(ct_hi, 1)

            def vector(dve, t):
                dve.wait_ge(w_hi, 1)
                raw = t["w_raw"][:, :, :, :].rearrange("p i k n -> p (i k) n") if biased else psum[:, 0:6, 0:D]
                hi, lo = (w[:, :, :, :].rearrange("p i k n -> p (i k) n") for w in t["w"])
                nc.vector.scalar_tensor_tensor(lo, raw, W_UP, hi, ALU.mult, ALU.subtract).then_inc(w_sb_done, 1)
                if biased:
                    dve.wait_ge(w_loaded, 16 * n_w)
                dve.sem_inc(k_out, 1)
                dve.sem_inc(v_out, 1)

                def norm(i):
                    for j in range(TS):
                        ins = nc.vector.tensor_scalar(t["xn"][:, j, :], x_sb[:, i * TS + j, :],
                                                      mv[:, i * TS + j, 0:1], rstd[:, bass.ds(i * TS + j, 1)],
                                                      ALU.subtract, ALU.mult)
                    ins.then_inc(xn_ready, 1)

                def low_part(name, b0, high, n, done):
                    dve.wait_ge(high, n)
                    nc.vector.tensor_tensor(t[name][LO][:, :, :], psum[:, b0:b0 + 2, :], t[name][HI][:, :, :],
                                            ALU.subtract).then_inc(done, 1)

                norm(0)
                low_part("xt", 0, xt_hi, 1, xt_sb)
                norm(1)
                low_part("ct", 2, ct_hi, 1, ct_sb)
                with dve.Fori(0, NS, 1) as s:
                    dve.wait_ge(q_hi, s + 1)
                    nc.vector.tensor_tensor(t["qs"][LO], t["qo"][:, :, :], t["qs"][HI], ALU.subtract
                                            ).then_inc(q_out, 1)
                    dve.wait_ge(v_ps, s + 1)
                    dve.wait_ge(v_stored, 16 * s + 16)
                    v_in = psum[:, 6:8, :].rearrange("p a (j d) -> p (a j) d", j=2)
                    if biased:
                        ins = nc.vector.scalar_tensor_tensor(t["vo"][:, :, :], v_in, 1.0 / W_UP,
                                                             t["bv"][:, :].unsqueeze(1).broadcast_to((P, TS, D)),
                                                             ALU.mult, ALU.add)
                    else:
                        ins = nc.vector.tensor_scalar(t["vo"][:, :, :], v_in, 1.0 / W_UP, None, ALU.mult)
                    ins.then_inc(v_out, 1)
                    low_part("xt", 0, xt_hi, s + 2, xt_sb)
                    norm((s + 2) % NS)
                    dve.wait_ge(k_hi, s + 2)
                    nc.vector.tensor_tensor(t["ks"][LO], t["ko"][:, :, :], t["ks"][HI], ALU.subtract
                                            ).then_inc(k_out, 1)
                    low_part("ct", 2, ct_hi, s + 2, ct_sb)

            return alloc, sync, tensor, scalar, vector, sync_first

        def relative_tables():
            ext_written, tables_loaded = sem("ext_written"), sem("tables_loaded")
            regrouped, pk_loaded, pk_ps, pk_t, ext_filled = (
                sem("regrouped"), sem("pk_loaded"), sem("pk_ps"), sem("pk_t"), sem("ext_filled"))
            up_set, raw_up, pk_parts = sem("up_set"), sem("raw_up"), sem("pk_parts")
            lo = S - 1 - K
            hi = S - 1 + K

            def alloc(stack):
                return {"kw": [sb(f"pos_k_skewed{i}", [P, S + GN - 1], F16, stack=stack) for i in (HI, LO)],
                        "vw": [sb(f"pos_v_by_key{i}", [P, 2, GN, P], F16, stack=stack) for i in (HI, LO)]}

            def alloc_raw(stack, t):
                t["raw"] = sb("pos_v_by_query", [P, 2, S * DH], stack=stack)
                t["pk"] = sb("pos_k_rows", [2 * K, DH], stack=stack)
                t["pk_last"] = sb("pos_k_last", [1, DH], stack=stack)
                t["pkt"] = sb("pos_k_t", [DH, 2 * K + 1], stack=stack)
                t["pkp"] = [sb(f"pos_k_t{i}", [DH, 2 * K + 1], F16, stack=stack) for i in (HI, LO)]
                t["extk"] = [sb(f"pos_k_ext{i}", [DH, 2 * S], F16, stack=stack) for i in (HI, LO)]
                t["up"] = sb("w_up", [P, 1], stack=stack)

            def gpsimd(pool, t):
                nc.gpsimd.memset(t["up"][:, :], W_UP).then_inc(up_set, 1)
                pool.wait_ge(up_set, 1)
                pool.wait_ge(tables_loaded, 16 * (2 * IN + 2))
                raw = t["raw"][:, :, :]
                shape = (P, 2, S * DH)
                nc.gpsimd.tensor_tensor(raw, raw, t["up"][:, :].unsqueeze(2).broadcast_to(shape), ALU.mult
                                        ).then_inc(raw_up, 1)
                pool.wait_ge(raw_up, 1)
                by_key = [[v[:, kt, :, :].rearrange("p g (r d) -> p g r d", r=IN) for kt in range(2)] for v in t["vw"]]
                by_query = [t["raw"][:, kt, :].rearrange("p (r g d) -> p g r d", r=IN, g=GN) for kt in range(2)]
                for kt in range(2):
                    ins = nc.gpsimd.tensor_copy(by_key[HI][kt], by_query[kt])
                ins.then_inc(raw_up, 1)
                pool.wait_ge(raw_up, 2)
                for kt in range(2):
                    for i in range(IN):
                        ins = nc.gpsimd.tensor_tensor(by_key[LO][kt][:, :, i, :], by_query[kt][:, :, i, :],
                                                      by_key[HI][kt][:, :, i, :], ALU.subtract)
                ins.then_inc(regrouped, 1)

            def sync(sp, t):
                pk, pv = a["L0_xattn_pos_k"], a["L0_xattn_pos_v"]
                sp.dma_start(t["pk"][:, :], pk[0:2 * K, :]).then_inc(pk_loaded, 16)
                sp.dma_start(t["pk_last"][0:1, :], pk[2 * K:2 * K + 1, :]).then_inc(pk_loaded, 16)
                sp.dma_start(extv_dr[lo:hi + 1, :], pv).then_inc(ext_written, 16)
                sp.dma_start(extv_dr[0:lo, :], pv[0:1, :].broadcast_to((lo, DH))).then_inc(ext_written, 16)
                sp.dma_start(extv_dr[hi + 1:2 * S, :],
                             pv[2 * K:2 * K + 1, :].broadcast_to((2 * S - hi - 1, DH))).then_inc(ext_written, 16)
                sp.wait_ge(ext_written, 16 * 3)
                sp.wait_ge(ext_filled, 1)
                for i in range(IN):
                    off = S - GN - GN * i
                    for part in (HI, LO):
                        sp.dma_start(t["kw"][part][i * DH:(i + 1) * DH, :], t["extk"][part][:, off:off + S + GN - 1]
                                     ).then_inc(tables_loaded, 16)
                for kt in range(2):
                    rows = bass.AP(extv_dr.tensor, kt * P * DH, [[DH, P], [1, S * DH]])
                    sp.dma_start(t["raw"][:, kt, :], rows).then_inc(tables_loaded, 16)

            def tensor(pe, t):
                pe.wait_ge(pk_loaded, 32)
                nc.tensor.transpose(psum[0:DH, 0, 0:2 * K], t["pk"][:, :], ident[:, :])
                nc.tensor.transpose(psum[0:DH, 0, 2 * K:2 * K + 1], t["pk_last"][0:1, :], ident[0:1, 0:1]
                                    ).then_inc(pk_ps, 1)
                pe.wait_ge(ext_filled, 1)

            def vector(dve, t):
                dve.wait_ge(pk_ps, 1)
                nc.vector.tensor_copy(t["pkt"][:, :], psum[0:DH, 0, 0:2 * K + 1]).then_inc(pk_t, 1)
                dve.wait_ge(pk_t, 1)
                nc.vector.tensor_copy(t["pkp"][HI][:, :], t["pkt"][:, :]).then_inc(pk_parts, 1)
                dve.wait_ge(pk_parts, 1)
                nc.vector.tensor_tensor(t["pkp"][LO][:, :], t["pkt"][:, :], t["pkp"][HI][:, :], ALU.subtract
                                        ).then_inc(pk_parts, 1)
                dve.wait_ge(pk_parts, 2)
                for part in (HI, LO):
                    ext, src = t["extk"][part], t["pkp"][part]
                    nc.vector.tensor_copy(ext[:, lo:hi + 1], src[:, :])
                    nc.vector.tensor_copy(ext[:, 0:lo], src[:, 0:1].broadcast_to((DH, lo)))
                    ins = nc.vector.tensor_copy(ext[:, hi + 1:2 * S],
                                                src[:, 2 * K:2 * K + 1].broadcast_to((DH, 2 * S - hi - 1)))
                ins.then_inc(ext_filled, 1)

            return alloc, alloc_raw, sync, gpsimd, tensor, vector, regrouped

        def attention(n_, relative, tables=None, tables_ready=None, w_out_ap=None):
            wo_loaded, wo_ps, wo_hi, wo_done = sem("wo_loaded"), sem("wo_ps"), sem("wo_hi"), sem("wo_done")
            h_hi, h_lo, fc_ps, fc_added = sem("h_hi"), sem("h_lo"), sem("fc_ps"), sem("fc_added")
            in_loaded = [sem(f"qkv_loaded_{i}") for i in range(2)]
            in_dmas = 4 + IN if relative else 1 + 4 * len(SPLIT)
            NW = 4
            KR = len(SPLIT) * 2 * DH
            mask_loaded = sem("mask_loaded")
            qd_ready, v_padded, s_ps = sem("qd_ready"), sem("v_padded"), sem("s_ps")
            masked, max_done, exp_done = sem("masked"), sem("max_done"), sem("exp_done")
            recip_done, w_ready, t_ps = sem("recip_done"), sem("w_ready"), sem("t_ps")
            wt_hi, wt_lo, v_done = sem("wt_hi"), sem("wt_lo"), sem("v_done")
            v_hi, q_zeroed, parity_set = sem("v_hi"), sem("q_zeroed"), sem("parity_set")
            NIT = B // 2
            LAG = 3 if relative else 6

            def rounds(eng, stages):
                def round_(it, n):
                    for lag, f in stages:
                        if not isinstance(it, int) or 0 <= it * NB2 + n - lag < NIT * NB2:
                            f(it, n - lag)

                for n in range(LAG):
                    round_(0, n)
                with eng.Fori(0, NIT - 1, 1) as it:
                    for n in range(LAG, LAG + NB2):
                        round_(it, n)
                for n in range(LAG, LAG + NB2):
                    round_(NIT - 1, n)
            x_out, x_masked, zeroed = sem("x_out"), sem("x_masked"), sem("zeroed")
            h_stored = [sem(f"h_stored_{i}") for i in range(2)]
            out_dmas = 1 + IN

            def alloc(stack):
                def parts(name, shape):
                    return [[sb(f"{name}{n_}_{i}_{part}", shape, F16, stack=stack) for part in (HI, LO)]
                            for i in range(2)]

                t = {"v": [sb(f"v_b{n_}_{i}", [P, 2, D], stack=stack) for i in range(2)],
                     "vz": parts("v_parts_b", [P, 2, D] if relative else [P, 2, H, 32]),
                     "negmax": sb(f"negmax{n_}", [P, 2, GC], stack=stack),
                     "sums": sb(f"sums{n_}", [P, 2, GC], stack=stack),
                     "recip": sb(f"recip{n_}", [P, 2, GC], stack=stack),
                     "w": [sb(f"weights{n_}_{i}", [P, GC, S], stack=stack) for i in range(NW)],
                     "wt": parts("weights_t", [P, 2, 512]),
                     }
                if relative:
                    t["q"] = [sb(f"q_b{n_}_{i}", [P, 2, S, 2], F16, stack=stack) for i in range(2)]
                    t["k"] = parts("k_b", [P, 2, S])
                    t["q2"] = [sb(f"q_by_i{n_}_{i}", [P, H, GN, 2], F16, stack=stack) for i in range(2)]
                    t["qd"] = parts("q_blocks", [P, 512])
                    t["qd2"] = parts("q_blocks_rel", [P, 512])
                    t["h"] = [sb(f"heads{n_}_{i}", [P, 2, S], stack=stack) for i in range(2)]
                    t["parity"] = sb(f"parity{n_}", [P, 2], stack=stack)
                    t["xv"] = sb(f"x_odd{n_}", [P, 64], stack=stack)
                    t["xm"] = sb(f"x_masked_t{n_}", [P, 512], stack=stack)
                    t["r"] = [sb(f"rel_heads{n_}_{i}", [P, H, GN], stack=stack) for i in range(2)]
                else:
                    t["q"] = [sb(f"q_b{n_}_{i}", [KR, NC, 2, S], F16, stack=stack) for i in range(2)]
                    t["k"] = [sb(f"k_b{n_}_{i}", [KR, NC, S], F16, stack=stack) for i in range(2)]
                    t["h"] = sb(f"heads{n_}", [P, 2, S], stack=stack)
                    t["hs"] = [sb(f"head_part{n_}_{i}", [P, 2, S], F16, stack=stack) for i in (HI, LO)]
                    t["wo"] = [sb(f"w_out{n_}_{i}", [P, KT, D], F16, stack=stack) for i in (HI, LO)]
                    t["wo_raw"] = sb(f"w_out_raw{n_}", [P, KT, D], stack=stack)
                    t["mask"] = sb(f"mask{n_}", [P, 2, S], I32, stack=stack)
                    t["ms"] = [sb(f"masked_scores{n_}_{i}", [P, 2, 2 * S], stack=stack) for i in range(2)]
                return t

            def sync(sp, t):
                v_t = v_dr.rearrange("(b t p) d -> p b t d", p=P, t=2)
                h_t = h_dr.rearrange("b (t p) s -> p b t s", p=P)
                r_t = r_dr.rearrange("b (h d) (i g) -> d b h i g", h=H, i=IN)
                if relative:
                    q_t = q0_dr.rearrange("b (t p) s e -> p b t (s e)", p=P)
                    q2_t = q0_dr.rearrange("b (h d) (i g) e -> d b h i (g e)", h=H, i=IN)
                    k_t = [k.rearrange("b (t p) s -> p b t s", p=P) for k in k_dr]
                else:
                    by_pair = "b (e c d) s -> d b e c s"
                    q_t = [q.rearrange(by_pair, e=2, c=NC) for q in q1_dr]
                    k_t = [k.rearrange(by_pair, e=2, c=NC) for k in k_dr]

                def load(b, bb):
                    done = in_loaded[bb]
                    sp.dma_start(t["v"][bb][:, :, :], v_t[:, b]).then_inc(done, 16)
                    if relative:
                        sp.dma_start(t["q"][bb][:, :, :, :].rearrange("p t s e -> p t (s e)"), q_t[:, b]
                                     ).then_inc(done, 16)
                        for i in (HI, LO):
                            sp.dma_start(t["k"][bb][i][:, :, :], k_t[i][:, b]).then_inc(done, 16)
                        for i in range(IN):
                            sp.dma_start(t["q2"][bb][i * DH:(i + 1) * DH, :, :, :].rearrange("d h g e -> d h (g e)"),
                                         q2_t[:, b, :, i, :]).then_inc(done, 16)
                    else:
                        for k, (pq, pk) in enumerate(SPLIT):
                            for e in range(2):
                                rows = slice((2 * k + e) * DH, (2 * k + e + 1) * DH)
                                sp.dma_start(t["q"][bb][rows, :, e, :], q_t[pq][:, b, e]).then_inc(done, 16)
                                sp.dma_start(t["k"][bb][rows, :, :], k_t[pk][:, b, e]).then_inc(done, 16)

                if not relative:
                    sp.dma_start(t["mask"][:, :, :], a["mask_SxS2_ik1"].rearrange("(t p) k -> p t k", p=P)
                                 ).then_inc(mask_loaded, 16)
                if not relative:
                    w = w_out_ap.rearrange("(t p) n -> p t n", p=P)
                    for dst, src, n in ((0, 0, P), (P, P + 64, 64), (P + 64, P, 64)):
                        sp.dma_start(t["wo_raw"][:, :, dst:dst + n], w[:, :, src:src + n]).then_inc(wo_loaded, 16)
                    sp.wait_ge(q_zeroed, 1)
                for bb in range(2):
                    load(bb, bb)
                    if relative:
                        sp.sem_inc(h_stored[bb], 16)
                with sp.Fori(0, B // 2, 1) as it:
                    for bb in range(2):
                        sp.wait_ge(x_out, it * NB2 + NC * (bb + 1) + 1)
                        if relative:
                            sp.dma_start(h_t[:, it * 2 + bb], t["h"][bb][:, :, :]).then_inc(h_stored[bb], 16)
                            for r in range(IN):
                                sp.dma_start(r_t[:, it * 2 + bb, :, IN - 1 - r, :],
                                             t["r"][bb][r * DH:(r + 1) * DH, :, :]).then_inc(h_stored[bb], 16)
                        load((it * 2 + bb + 2) % B, bb)
                for bb in range(2):
                    if relative:
                        sp.wait_ge(h_stored[bb], 16 + 16 * out_dmas * (B // 2))
                    sp.wait_ge(in_loaded[bb], 16 * in_dmas * (B // 2 + 1))

            def gpsimd(pool, t):
                if not relative:
                    for vz in t["vz"]:
                        for i in (HI, LO):
                            nc.gpsimd.memset(vz[i][:, :, :, :], 0.0)
                    for i in range(2):
                        ins = nc.gpsimd.memset(t["ms"][i][:, :, :], MASKED)
                    ins.then_inc(zeroed, 1)
                    pool.wait_ge(zeroed, 1)
                pool.sem_inc(v_done, NB2)

                def q_blocks(it, n):
                    bb, c, buf = n // NC % 2, n % NC, n % 2
                    if c == 0:
                        pool.wait_ge(in_loaded[bb], 16 * in_dmas * (it + n // NB2 + 1))
                    pool.wait_ge(s_ps, it * NB2 + n + 1)
                    for i in (HI, LO):
                        for hh in range(2):
                            out_ = t["qd"][buf][i][:, hh * 256:(hh + 1) * 256].rearrange("p (g h i) -> p g h i", g=GC, h=8)
                            src = t["q"][bb][:, hh, :, i].rearrange("p (i g) -> p g i", g=GN)[:, GC * c:GC * (c + 1), :]
                            nc.gpsimd.tensor_tensor(
                                out_, src.unsqueeze(2).broadcast_to((P, GC, 8, IN)),
                                block[:, :].unsqueeze(1).unsqueeze(3).broadcast_to((P, GC, 8, IN)), ALU.mult)
                        out_ = t["qd2"][buf][i][:, :].rearrange("p (g h i) -> p g h i", g=GC, h=H)
                        src = t["q2"][bb][:, :, GC * c:GC * (c + 1), i].rearrange("p h g -> p g h")
                        ins = nc.gpsimd.tensor_tensor(
                            out_, src.unsqueeze(3).broadcast_to((P, GC, H, IN)),
                            block[:, :].unsqueeze(1).unsqueeze(1).broadcast_to((P, GC, H, IN)), ALU.mult)
                    ins.then_inc(qd_ready, 1)

                def scale(it, n):
                    pool.wait_ge(recip_done, it * NB2 + n + 1)
                    nc.gpsimd.tensor_tensor(
                        t["w"][n % NW][:, :, :], t["w"][n % NW][:, :, :],
                        t["recip"][:, n % 2, :].unsqueeze(2).broadcast_to((P, GC, S)), ALU.mult).then_inc(w_ready, 1)

                def low_v(it, n):
                    if n % NC != 0:
                        return
                    bb = n // NC % 2
                    pool.wait_ge(v_hi, it * 2 + n // NC + 1)
                    if relative:
                        ins = nc.gpsimd.tensor_tensor(t["vz"][bb][LO][:, :, :], t["v"][bb][:, :, :],
                                                      t["vz"][bb][HI][:, :, :], ALU.subtract)
                    else:
                        for kt in range(2):
                            for h2 in range(2):
                                (hi, lo) = (z[:, kt, :, :].rearrange("p (j e) c -> p j e c", e=2)
                                            [:, :, h2, h2 * DH:(h2 + 1) * DH] for z in t["vz"][bb])
                                src = t["v"][bb][:, kt, :].rearrange("p (j e d) -> p j e d", e=2, d=DH)[:, :, h2, :]
                                ins = nc.gpsimd.tensor_tensor(lo, src, hi, ALU.subtract)
                    ins.then_inc(v_padded, 1)

                def low_heads(it, n):
                    if n % NC != NC - 1:
                        return
                    pool.wait_ge(h_hi, it * 2 + n // NC + 1)
                    nc.gpsimd.tensor_tensor(t["hs"][LO][:, :, :], t["h"][:, :, :], t["hs"][HI][:, :, :], ALU.subtract
                                            ).then_inc(h_lo, 1)

                rounds(pool, [(0, q_blocks), (2, low_v)] if relative else [(1, scale), (1, low_v), (4, low_heads)])

            def tensor(pe, t):
                pe.sem_inc(s_ps, 2)
                if not relative:
                    pe.wait_ge(wo_loaded, 48)
                    for ot in range(2):
                        for kt in range(KT):
                            ins = nc.tensor.transpose(psum[:, 6 + kt, ot * P:(ot + 1) * P],
                                                      t["wo_raw"][:, ot, kt * P:(kt + 1) * P], ident[:, :])
                    ins.then_inc(wo_ps, 1)
                    pe.wait_ge(wo_done, 1)
                if relative:
                    pe.wait_ge(tables_ready, 1)
                def scores(it, n):
                    bb, c, buf = n // NC % 2, n % NC, n % 2
                    if c == 0:
                        pe.wait_ge(in_loaded[bb], 16 * in_dmas * (it + n // NB2 + 1))
                    if relative:
                        pe.wait_ge(qd_ready, it * NB2 + n + 1)
                    if n >= 2:
                        pe.wait_ge(exp_done if relative else masked, it * NB2 + n - 1)
                    for g in range(GC):
                        s_g = psum[:, buf * 2 + g // 2, (g % 2) * S:(g % 2 + 1) * S]
                        if relative:
                            off = GN - 1 - (GC * c + g)
                            for k, (pq, pk) in enumerate(SPLIT):
                                nc.tensor.matmul(s_g, t["qd2"][buf][pq][:, g * P:(g + 1) * P],
                                                 tables["kw"][pk][:, off:off + S], start=(k == 0), stop=False,
                                                 skip_group_check=True)
                            for pq, pk in SPLIT:
                                for hh in range(2):
                                    ins = nc.tensor.matmul(
                                        psum[hh * 64:(hh + 1) * 64, buf * 2 + g // 2, (g % 2) * S:(g % 2 + 1) * S],
                                        t["qd"][buf][pq][:, hh * 256 + g * 64:hh * 256 + (g + 1) * 64],
                                        t["k"][bb][pk][:, hh, :], start=False, stop=True, skip_group_check=True)
                        else:
                            ins = nc.tensor.matmul(s_g, t["q"][bb][:, c, g // 2, (g % 2) * P:(g % 2 + 1) * P],
                                                   t["k"][bb][:, c, :], start=True, stop=True)
                    ins.then_inc(s_ps, 1)

                def transposes(it, n):
                    pe.wait_ge(w_ready, it * NB2 + n + 1)
                    for kt in range(2):
                        pe.wait_ge(wt_lo, 2 * (it * NB2 + n) + kt + 1)
                        for g in range(GC):
                            ins = nc.tensor.transpose(psum[:, 4 + kt, g * P:(g + 1) * P],
                                                      t["w"][n % NW][:, g, kt * P:(kt + 1) * P], ident[:, :])
                        ins.then_inc(t_ps, 1)

                def values(it, n):
                    bb, c = n // NC % 2, n % NC
                    if c == 0:
                        pe.wait_ge(v_padded, it * 2 + n // NC + 1)
                    pe.wait_ge(wt_lo, 2 * (it * NB2 + n) + 4)
                    pe.wait_ge(x_out, it * NB2 + n + 1)
                    if not relative and c >= 2:
                        pe.wait_ge(fc_added, it * 2 + n // NC + 1)
                    wt = t["wt"][n % 2]
                    if relative:
                        for hh in range(2):
                            for kt in range(2):
                                for k, (pv, pw) in enumerate(SPLIT):
                                    for j in range(4):
                                        pair = hh * 4 + j
                                        rhs = wt[pw][:, kt, :].rearrange("p (g c) -> p g c", g=GC)[
                                            :, :, pair * 2 * IN:(pair + 1) * 2 * IN]
                                        nc.tensor.matmul(psum[32 * j:32 * j + 32, 6, hh * 64:(hh + 1) * 64],
                                                         t["vz"][bb][pv][:, kt, pair * 32:(pair + 1) * 32], rhs,
                                                         start=(kt == 0 and k == 0), stop=(kt == 1 and k == 2),
                                                         tile_position=(0, 32 * j), skip_group_check=True)
                        for g in range(GC):
                            for kt in range(2):
                                for k, (pv, pw) in enumerate(SPLIT):
                                    ins = nc.tensor.matmul(psum[:, 7, g * P:(g + 1) * P],
                                                           tables["vw"][pv][:, kt, GN - 1 - (GC * c + g), :],
                                                           wt[pw][:, kt, g * P:(g + 1) * P],
                                                           start=(kt == 0 and k == 0), stop=(kt == 1 and k == 2))
                    else:
                        for kt in range(2):
                            for k, (pv, pw) in enumerate(SPLIT):
                                for e in range(2):
                                    j = (c // 2 + 2 * e) % 4
                                    ins = nc.tensor.matmul(psum[32 * j:32 * j + 32, 6 + e, 0:S],
                                                           t["vz"][bb][pv][:, kt, NC * e + c, :],
                                                           wt[pw][:, kt, e * S:(e + 1) * S],
                                                           start=(c % 2 == 0 and kt == 0 and k == 0),
                                                           stop=(c % 2 == 1 and kt == 1 and k == 2),
                                                           tile_position=(0, 32 * j), skip_group_check=True)
                    ins.then_inc(v_done, 1)

                def output(it, n):
                    if n % NC != NC - 1:
                        return
                    pe.wait_ge(h_lo, it * 2 + n // NC + 1)
                    for m in range(2):
                        for kt in range(KT):
                            for k, (ph, pw) in enumerate(SPLIT):
                                ins = nc.tensor.matmul(psum[:, 6 + m, S:S + D], t["hs"][ph][:, kt, m * P:(m + 1) * P],
                                                       t["wo"][pw][:, kt, :], start=(kt == 0 and k == 0),
                                                       stop=(kt == KT - 1 and k == 2), skip_group_check=True)
                    ins.then_inc(fc_ps, 1)

                rounds(pe, [(0, scores), (2, transposes), (3, values)] + ([] if relative else [(5, output)]))

            def scalar(act, t):
                if not relative:
                    act.wait_ge(zeroed, 1)
                    act.wait_ge(wo_ps, 1)
                    nc.scalar.mul(t["wo"][HI][:, :, :], psum[:, 6:8, 0:D], W_UP).then_inc(wo_hi, 1)

                def high_v(it, n):
                    if n % NC != 0:
                        return
                    bb = n // NC % 2
                    act.wait_ge(in_loaded[bb], 16 * in_dmas * (it + n // NB2 + 1))
                    act.wait_ge(v_done, it * NB2 + NC * (n // NC + 1))
                    if relative:
                        ins = nc.scalar.copy(t["vz"][bb][HI][:, :, :], t["v"][bb][:, :, :])
                    else:
                        for kt in range(2):
                            for h2 in range(2):
                                dst = t["vz"][bb][HI][:, kt, :, :].rearrange("p (j e) c -> p j e c", e=2)
                                src = t["v"][bb][:, kt, :].rearrange("p (j e d) -> p j e d", e=2, d=DH)
                                ins = nc.scalar.copy(dst[:, :, h2, h2 * DH:(h2 + 1) * DH], src[:, :, h2, :])
                    ins.then_inc(v_hi, 1)

                def exps(it, n):
                    act.wait_ge(max_done, it * NB2 + n + 1)
                    for g in range(GC):
                        if relative:
                            src = psum[:, (n % 2) * 2 + g // 2, (g % 2) * S:(g % 2 + 1) * S]
                        else:
                            src = t["ms"][n % 2][:, g // 2, (g % 2) * S:(g % 2 + 1) * S]
                        ins = nc.scalar.activation(t["w"][n % NW][:, g, :], src, ACT.Exp,
                                                   bias=t["negmax"][:, n % 2, g:g + 1],
                                                   accum_out=t["sums"][:, n % 2, g:g + 1])
                    ins.then_inc(exp_done, 1)

                def scale(it, n):
                    act.wait_ge(recip_done, it * NB2 + n + 1)
                    for g in range(GC):
                        w = t["w"][n % NW][:, g, :]
                        ins = nc.scalar.mul(w, w, t["recip"][:, n % 2, g:g + 1])
                    ins.then_inc(w_ready, 1)

                def evacuate(it, n):
                    act.wait_ge(v_done, it * NB2 + NB2 + n - 1)
                    for kt in range(2):
                        act.wait_ge(t_ps, 2 * (it * NB2 + n) + kt + 1)
                        nc.scalar.mul(t["wt"][n % 2][HI][:, kt, :], psum[:, 4 + kt, :], A_UP).then_inc(wt_hi, 1)

                def high_heads(it, n):
                    if n % NC != NC - 1:
                        return
                    act.wait_ge(x_out, it * NB2 + n + 2)
                    nc.scalar.copy(t["hs"][HI][:, :, :], t["h"][:, :, :]).then_inc(h_hi, 1)

                rounds(act, [(0, high_v), (2, evacuate), (0, exps), (1, scale) if relative else (4, high_heads)])

            def vector(dve, t):
                dve.sem_inc(x_out, 1)
                dve.sem_inc(wt_lo, 2)
                if not relative:
                    for q in t["q"]:
                        ins = nc.vector.memset(q[:, :, :, :], 0.0)
                    ins.then_inc(q_zeroed, 1)
                    dve.wait_ge(wo_hi, 1)
                    nc.vector.scalar_tensor_tensor(t["wo"][LO][:, :, :], psum[:, 6:8, 0:D], W_UP, t["wo"][HI][:, :, :],
                                                   ALU.mult, ALU.subtract).then_inc(wo_done, 1)
                    dve.sem_inc(fc_added, 1)
                    dve.wait_ge(mask_loaded, 16)
                    dve.wait_ge(zeroed, 1)
                else:
                    nc.vector.tensor_reduce(t["parity"][:, :], block[:, :].rearrange("p (j e) -> p e j", e=2), X, ALU.add
                                            ).then_inc(parity_set, 1)
                    dve.wait_ge(parity_set, 1)
                    nc.vector.tensor_scalar(t["parity"][:, :], t["parity"][:, :], 1.0 / A_UP, None, ALU.mult
                                            ).then_inc(parity_set, 1)
                    dve.wait_ge(parity_set, 2)
                def maxima(it, n):
                    if relative:
                        dve.wait_ge(s_ps, it * NB2 + n + 3)
                    else:
                        if n >= 2:
                            dve.wait_ge(exp_done, it * NB2 + n - 1)
                        wait_apart(dve, s_ps, it * NB2 + n + 3)
                    src = psum[:, (n % 2) * 2:(n % 2) * 2 + 2, :]
                    if not relative:
                        nc.vector.copy_predicated(t["ms"][n % 2][:, :, :],
                                                  t["mask"][:, :, :].rearrange("p t k -> p (t k)").unsqueeze(1)
                                                  .broadcast_to((P, 2, 2 * S)), src).then_inc(masked, 1)
                        dve.wait_ge(masked, it * NB2 + n + 1)
                        src = t["ms"][n % 2][:, :, :]
                    nc.vector.tensor_reduce(t["negmax"][:, n % 2, :],
                                            src.rearrange("p a (g k) -> p (a g) k", g=2), X, ALU.max,
                                            negate=True).then_inc(max_done, 1)

                def reciprocals(it, n):
                    dve.wait_ge(exp_done, it * NB2 + n + 1)
                    nc.vector.reciprocal(t["recip"][:, n % 2, :], t["sums"][:, n % 2, :]).then_inc(recip_done, 1)

                def evacuate(it, n):
                    for kt in range(2):
                        dve.wait_ge(wt_hi, 2 * (it * NB2 + n) + kt + 1)
                        nc.vector.scalar_tensor_tensor(t["wt"][n % 2][LO][:, kt, :], psum[:, 4 + kt, :], A_UP,
                                                       t["wt"][n % 2][HI][:, kt, :], ALU.mult, ALU.subtract
                                                       ).then_inc(wt_lo, 1)

                def heads(it, n):
                    bb, c = n // NC % 2, n % NC
                    if not relative and c != NC - 1:
                        dve.sem_inc(x_out, 1)
                        return
                    dve.wait_ge(v_done, it * NB2 + NB2 + n + 1)
                    if c == 0 and relative:
                        dve.wait_ge(h_stored[bb], (it + n // NB2) * 16 * out_dmas + 16)
                    if relative:
                        dst = t["h"][bb][:, :, :].rearrange("p t (i g) -> p t g i", g=GN)[:, :, GC * c:GC * (c + 1), :]
                        even, odd = (psum[:, 6, 0:128].rearrange("p (t g e i) -> p t g e i", t=2, g=GC, e=2)[:, :, :, e, :]
                                     for e in range(2))
                        xv = t["xv"][:, :].rearrange("p (t g i) -> p t g i", t=2, g=GC)
                        nc.vector.tensor_scalar(xv, odd, t["parity"][:, 1:2], None, ALU.mult)
                        nc.vector.scalar_tensor_tensor(
                            t["xm"][:, :].rearrange("p (m i) -> p m i", i=IN),
                            psum[:, 7, :].rearrange("p (m i) -> p m i", i=IN), 1.0 / (A_UP * W_UP),
                            block_rev[:, :].unsqueeze(1).broadcast_to((P, GC * H, IN)), ALU.mult, ALU.mult
                        ).then_inc(x_masked, 1)
                        dve.wait_ge(x_masked, it * NB2 + n + 1)
                        for half in range(2):
                            nc.vector.scalar_tensor_tensor(dst[:, half], even[:, half], t["parity"][:, 0:1], xv[:, half],
                                                           ALU.mult, ALU.add)
                        nc.vector.tensor_reduce(
                            t["r"][bb][:, :, GC * c:GC * (c + 1)].rearrange("p h g -> p g h"),
                            t["xm"][:, :].rearrange("p (g h i) -> p g h i", g=GC, h=H), X, ALU.add
                        ).then_inc(x_out, 1)
                    else:
                        nc.vector.tensor_scalar(t["h"][:, :, :], psum[:, 6:8, 0:S], 1.0 / A_UP, None, ALU.mult
                                                ).then_inc(x_out, 1)

                def add(it, n):
                    if n % NC != NC - 1:
                        return
                    wait_apart(dve, fc_ps, it * 2 + n // NC + 1)
                    for m in range(2):
                        xs = x_sb[:, (it * 2 + n // NC) * 2 + m, :]
                        ins = nc.vector.scalar_tensor_tensor(xs, psum[:, 6 + m, S:S + D], 1.0 / W_UP, xs, ALU.mult, ALU.add)
                    ins.then_inc(fc_added, 1)

                rounds(dve, ([] if relative else [(6, add)]) + [(0, maxima), (1, reciprocals), (2, evacuate), (3, heads)])

            return alloc, sync, gpsimd, tensor, scalar, vector

        def merge_heads(n_, w_ap, parts, bias_ap):
            h_loaded = [sem(f"h_loaded_{i}") for i in range(2)]
            w_loaded, o_ps, x_added = sem("fc_loaded"), sem("o_ps"), sem("x_added")
            w_hi, w_done, ones_set = sem("fc_hi"), sem("fc_done"), sem("ones_set")
            h_sum, h_hi, h_lo = sem("h_sum"), sem("h_hi"), sem("h_lo")
            np_ = len(parts)

            def alloc(stack):
                return {"w": [sb(f"w_fc{n_}_{i}", [P, KT, D], F16, stack=stack) for i in (HI, LO)],
                        "raw": sb(f"w_fc_raw{n_}", [P, KT, D], stack=stack),
                        "bias": sb(f"b_fc{n_}", [1, D], stack=stack), "ones": sb(f"ones{n_}", [1, P], F16, stack=stack),
                        "bias_parts": [sb(f"b_fc{n_}_{i}", [1, D], F16, stack=stack) for i in (HI, LO)],
                        "h": [sb(f"h_in{n_}_{i}", [P, np_, 2, SC], stack=stack) for i in range(2)],
                        "hs": [[sb(f"h_part{n_}_{i}_{part}", [P, 2, SC], F16, stack=stack) for part in (HI, LO)]
                               for i in range(2)]}

            def sync(sp, t):
                sp.dma_start(t["raw"][:, :, :], w_ap.rearrange("(t p) n -> p t n", p=P)).then_inc(w_loaded, 16)
                sp.dma_start(t["bias"][0:1, :], bias_ap.unsqueeze(0)).then_inc(w_loaded, 16)
                sp.sem_inc(h_lo, 2)
                with sp.Fori(0, NS // 2, 1) as it:
                    for j in range(2):
                        sp.wait_ge(h_lo, it * 2 + j + 1)
                        for i, part in enumerate(parts):
                            src = part.rearrange("b (t p) s -> p t b s", p=P)
                            for hh in range(2):
                                sp.dma_start(t["h"][j][:, i, hh, :].rearrange("p (b s) -> p b s", b=2),
                                             src[:, hh, bass.ds((it * 2 + j) * 2, 2), :]).then_inc(h_loaded[j], 16)

            def gpsimd(pool, t):
                with pool.Fori(0, NS // 2, 1) as it:
                    for j in range(2):
                        h = t["h"][j]
                        pool.wait_ge(h_loaded[j], 32 * np_ * (it + 1))
                        nc.gpsimd.tensor_tensor(h[:, 0], h[:, 0], h[:, 1], ALU.add).then_inc(h_sum, 1)
                        pool.wait_ge(h_hi, it * 2 + j + 1)
                        nc.gpsimd.tensor_tensor(t["hs"][j][LO][:, :, :], h[:, 0], t["hs"][j][HI][:, :, :], ALU.subtract
                                                ).then_inc(h_lo, 1)

            def scalar(act, t):
                act.wait_ge(w_loaded, 32)
                nc.scalar.mul(t["bias_parts"][HI][0:1, :], t["bias"][0:1, :], W_UP)
                nc.scalar.mul(t["w"][HI][:, :, :], t["raw"][:, :, :], W_UP).then_inc(w_hi, 1)
                act.sem_inc(o_ps, 2)
                with act.Fori(0, NS // 2, 1) as it:
                    for j in range(2):
                        act.wait_ge(h_sum, it * 2 + j + 1)
                        act.wait_ge(o_ps, it * 2 + j + 1)
                        nc.scalar.copy(t["hs"][j][HI][:, :, :], t["h"][j][:, 0]).then_inc(h_hi, 1)

            def tensor(pe, t):
                pe.wait_ge(w_done, 1)
                pe.wait_ge(ones_set, 1)
                with pe.Fori(0, NS // 2, 1) as it:
                    for j in range(2):
                        pe.wait_ge(h_lo, it * 2 + j + 3)
                        pe.wait_ge(x_added, it * 2 + j + 1)
                        for m in range(TS):
                            o = psum[:, 2 + 2 * j + m // 2, (m % 2) * D:(m % 2 + 1) * D]
                            for i in (HI, LO):
                                nc.tensor.matmul(o, t["ones"][0:1, :], t["bias_parts"][i][0:1, :], start=(i == HI),
                                                 stop=False)
                            for kt in range(KT):
                                for k, (ph, pw) in enumerate(SPLIT):
                                    ins = nc.tensor.matmul(o, t["hs"][j][ph][:, kt, m * P:(m + 1) * P],
                                                           t["w"][pw][:, kt, :],
                                                           start=False, stop=(kt == KT - 1 and k == 2))
                        ins.then_inc(o_ps, 1)

            def vector(dve, t):
                dve.wait_ge(w_hi, 1)
                nc.vector.scalar_tensor_tensor(t["bias_parts"][LO][0:1, :], t["bias"][0:1, :], W_UP,
                                               t["bias_parts"][HI][0:1, :], ALU.mult, ALU.subtract)
                nc.vector.scalar_tensor_tensor(t["w"][LO][:, :, :], t["raw"][:, :, :], W_UP, t["w"][HI][:, :, :],
                                               ALU.mult, ALU.subtract).then_inc(w_done, 1)
                nc.vector.memset(t["ones"][0:1, :], 1.0).then_inc(ones_set, 1)
                dve.sem_inc(x_added, 2)
                with dve.Fori(0, NS // 2, 1) as it:
                    for j in range(2):
                        wait_apart(dve, o_ps, it * 2 + j + 3)
                        for e in range(2):
                            xs = x_sb[:, bass.ds((it * 2 + j) * TS + 2 * e, 2), :]
                            o = psum[:, 2 + 2 * j + e, :].rearrange("p (m d) -> p m d", m=2)
                            ins = nc.vector.scalar_tensor_tensor(xs, o, 1.0 / W_UP, xs, ALU.mult, ALU.add)
                        ins.then_inc(x_added, 1)

            return alloc, sync, gpsimd, tensor, scalar, vector

        def quantised_ffn():
            w_loaded, w_amax, w_step_done, w_recip = sem("fw_loaded"), sem("fw_amax"), sem("fw_step"), sem("fw_recip")
            w_round, w_quant, w_ps, w_sb_done = sem("fw_round"), sem("fw_quant"), sem("w_ps"), sem("fw_sb")
            xn_ready, xt_ps, xt_sb, x_max = sem("xn_ready"), sem("xt_ps"), sem("xt_sb"), sem("fx_max")
            fold, amax_part, amax_all, sc_step, scaled = (sem("amax_fold"), sem("amax_part"), sem("amax_all"),
                                                          sem("scale_step"), sem("scaled"))
            x_round, x_quant, magic_set, acc_set = sem("x_round"), sem("x_quant"), sem("magic_set"), sem("acc_set")
            m_ps, m_used = sem("m_ps"), sem("m_used")
            g_ps, g_round, g_val, g_sig, g_y, g_clip, g_prod = (sem("g_ps"), sem("g_round"), sem("g_val"), sem("g_sig"),
                                                                sem("g_y"), sem("g_clip"), sem("g_prod"))
            g_max = sem("g_max")
            u_ps, u_round, p_round, u_int, u_prod, u_max = (sem("u_ps"), sem("u_round"), sem("p_round"), sem("u_int"),
                                                            sem("u_prod"), sem("u_max"))
            o_round, o_hi, o_int, d_ps, d_added = sem("o_round"), sem("o_hi"), sem("o_int"), sem("d_ps"), sem("d_added")
            x_hi, w_hi = sem("fx_hi"), sem("w_hi")
            F = 768
            FT = F // P
            NP = FT // 2
            NI = 2 * NP

            def alloc(stack):
                t = {"wg": [sb(f"wg_t{i}", [P, KT, F], F16, stack=stack) for i in (HI, LO)],
                     "wu": [sb(f"wu_t{i}", [P, KT, F], F16, stack=stack) for i in (HI, LO)],
                     "wd": [sb(f"wd_t{i}", [P, FT, D], F16, stack=stack) for i in (HI, LO)],
                     "am": sb("amax_new", [P, 12], stack=stack), "acc": sb("amax_sofar", [P, 12], stack=stack),
                     "ar": sb("amax_row", [P, 8], stack=stack), "aa": sb("amax_whole", [P, 8], stack=stack),
                     "sc": sb("scales", [P, 16], stack=stack),
                     "magic": sb("magic", [P, 1], stack=stack)}
                with ExitStack() as inner:
                    t["os"] = [[sb(f"ff_o_part{i}_{part}", [P, FT, SC], F16, stack=inner) for part in (HI, LO)]
                               for i in range(2)]
                t["xq"] = [sb(f"xq_t{i}", [P, KT, B * S], F16, stack=stack) for i in (HI, LO)]
                with ExitStack() as inner:
                    t["xt"] = sb("x_t", [P, KT, B * S], stack=inner)
                    t["raw"] = sb("fw_raw", [P, 3, F * D // P], stack=inner)
                    t["wq"] = sb("fw_q", [P, 3, F * D // P], stack=inner)
                    t["wam"] = sb("fw_amax_t", [P, 3, F * D // P // QBLOCK], stack=inner)
                    t["wsc"] = sb("fw_scale_t", [P, 3, F * D // P // QBLOCK], stack=inner)
                    t["xn"] = sb("fxn", [P, TS, D], stack=inner)
                t["p"] = sb("gated", [P, FT, B * S], stack=stack)
                with ExitStack() as inner:
                    t["a"] = [sb(f"ff_a{i}", [P, 2 * SC], stack=inner) for i in range(2)]
                    t["b"] = [sb(f"ff_b{i}", [P, 2 * SC], stack=inner) for i in range(2)]
                    t["c"] = [sb(f"ff_c{i}", [P, 2 * SC], stack=inner) for i in range(2)]
                return t

            def sync(sp, t):
                for i, nm in enumerate(("L0_ffn_w_gate", "L0_ffn_w_up", "L0_ffn_w_down")):
                    w = a[nm]
                    sp.dma_start(t["raw"][:, i, :].rearrange("p (t n) -> p t n", n=w.shape[1]),
                                 w.rearrange("(t p) n -> p t n", p=P)).then_inc(w_loaded, 16)

            def gpsimd(pool, t):
                nc.gpsimd.memset(t["magic"][:, :], MAGIC).then_inc(magic_set, 1)
                pool.wait_ge(magic_set, 1)
                raw, wq, flat = weight_blocks(t)
                shape = (P, 3 * F * D // P // QBLOCK, QBLOCK)
                wam, wsc = (t[n_][:, :, :].rearrange("p i b -> p (i b)").unsqueeze(2).broadcast_to(shape)
                            for n_ in ("wam", "wsc"))
                magic = t["magic"][:, :].broadcast_to((P, 3 * F * D // P))
                pool.wait_ge(w_recip, 1)
                nc.gpsimd.tensor_tensor(wq, raw, wam, ALU.mult).then_inc(w_round, 1)
                pool.wait_ge(w_round, 1)
                nc.gpsimd.tensor_tensor(flat, flat, magic, ALU.add).then_inc(w_round, 1)
                pool.wait_ge(w_round, 2)
                nc.gpsimd.tensor_tensor(flat, flat, magic, ALU.subtract).then_inc(w_round, 1)
                pool.wait_ge(w_round, 3)
                nc.gpsimd.tensor_tensor(wq, wq, wsc, ALU.mult).then_inc(w_quant, 1)
                for k, (c0, n) in enumerate(((0, 1), (1, 2), (3, 1), (4, 1))):
                    pool.wait_ge(amax_part, k + 1)
                    nc.gpsimd.partition_all_reduce(t["aa"][:, c0:c0 + n], t["ar"][:, c0:c0 + n], P, ABSMAX
                                                   ).then_inc(amax_all, 1)
                    if k == 2:
                        with pool.Fori(0, NS // 2, 1) as it:
                            for i in range(NI):
                                pool.wait_ge(u_round, it * NI + i + 4)
                                nc.gpsimd.tensor_tensor(t["a"][i % 2][:, :], t["a"][i % 2][:, :],
                                                        t["magic"][:, :].broadcast_to((P, 2 * SC)), ALU.subtract
                                                        ).then_inc(u_int, 1)

            def weight_blocks(t):
                raw, wq = (t[n_][:, :, :].rearrange("p i (b q) -> p (i b) q", q=QBLOCK) for n_ in ("raw", "wq"))
                return raw, wq, t["wq"][:, :, :].rearrange("p i n -> p (i n)")

            def gate_up_weights(t):
                for w, b0 in ((t["wg"], 0), (t["wu"], 3)):
                    for kt in range(KT):
                        src = psum[:, b0:b0 + 3, :].rearrange("p a (f k m) -> p (a f) k m", f=2, k=KT)
                        hi, lo = (w[i][:, kt, :].rearrange("p (f m) -> p f m", f=FT) for i in (HI, LO))
                        yield hi, lo, src[:, :, kt, :]

            def bank_pair(i):
                return psum[:, 2 * (i % 3):2 * (i % 3) + 2, :]

            def product(w, xq, s, pr, i, done):
                for e in range(2):
                    f = pr * 2 + e
                    for kt in range(KT):
                        for k, (pw, px) in enumerate(SPLIT):
                            ins = nc.tensor.matmul(psum[:, 2 * (i % 3) + e, :], w[pw][:, kt, f * P:(f + 1) * P],
                                                   xq[px][:, kt, bass.ds(s * SC, SC)],
                                                   start=(kt == 0 and k == 0), stop=(kt == KT - 1 and k == 2))
                ins.then_inc(done, 1)

            def tensor(pe, t):
                pe.sem_inc(xt_ps, 1)
                with pe.Fori(0, NS, 1) as s:
                    pe.wait_ge(xn_ready, s + 1)
                    pe.wait_ge(xt_sb, s + 1)
                    for kt in range(KT):
                        for j in range(TS):
                            ins = nc.tensor.transpose(psum[:, kt, j * P:(j + 1) * P],
                                                      t["xn"][:, j, kt * P:(kt + 1) * P], ident[:, :])
                    ins.then_inc(xt_ps, 1)
                pe.wait_ge(xt_sb, NS + 1)
                pe.wait_ge(w_quant, 1)
                for i in range(2):
                    for f in range(FT):
                        for kt in range(KT):
                            idx = (i * FT + f) * KT + kt
                            ins = nc.tensor.transpose(psum[:, idx // 4, (idx % 4) * P:(idx % 4 + 1) * P],
                                                      t["wq"][:, i, f * D + kt * P:f * D + (kt + 1) * P], ident[:, :])
                ins.then_inc(w_ps, 1)
                pe.wait_ge(w_sb_done, 1)
                for ot in range(KT):
                    for f in range(FT):
                        idx = f * KT + ot
                        ins = nc.tensor.transpose(psum[:, idx // 4, (idx % 4) * P:(idx % 4 + 1) * P],
                                                  t["wq"][:, 2, ot * F + f * P:ot * F + (f + 1) * P], ident[:, :])
                ins.then_inc(w_ps, 1)
                pe.wait_ge(w_sb_done, 2)
                with pe.Fori(0, NS, 1) as s:
                    pe.wait_ge(x_quant, s + 1)
                    for i in range(NI):
                        pe.wait_ge(m_used, s * NI + i + 1)
                        product((t["wg"], t["wu"])[i // NP], t["xq"], s, i % NP, i, m_ps)
                pe.wait_ge(m_used, NS * NI + 3)
                with pe.Fori(0, NS // 2, 1) as it:
                    for i in range(NI):
                        pe.wait_ge(g_round, it * NI + i + 1)
                        product(t["wg"], t["xq"], it * 2 + i // NP, i % NP, i, g_ps)
                pe.wait_ge(g_round, NS // 2 * NI + 3)
                with pe.Fori(0, NS // 2, 1) as it:
                    for i in range(NI):
                        pe.wait_ge(u_round, it * NI + i + 1)
                        product(t["wu"], t["xq"], it * 2 + i // NP, i % NP, i, u_ps)
                pe.wait_ge(u_round, NS // 2 * NI + 3)
                pe.sem_inc(d_ps, 2)
                with pe.Fori(0, NS // 2, 1) as it:
                    for j in range(2):
                        pe.wait_ge(o_int, NP * (it * 2 + j) + NP + 2)
                        pe.wait_ge(d_added, it * 2 + j + 1)
                        for m in range(TS):
                            for f in range(FT):
                                for k, (po, pw) in enumerate(SPLIT):
                                    ins = nc.tensor.matmul(psum[:, 2 * j + m // 2, (m % 2) * D:(m % 2 + 1) * D],
                                                           t["os"][j][po][:, f, m * P:(m + 1) * P], t["wd"][pw][:, f, :],
                                                           start=(f == 0 and k == 0), stop=(f == FT - 1 and k == 2))
                        ins.then_inc(d_ps, 1)

            def scalar(act, t):
                act.wait_ge(magic_set, 1)
                act.sem_inc(xt_sb, 1)
                act.sem_inc(g_round, 3)
                act.sem_inc(u_round, 3)
                with act.Fori(0, NS, 1) as s:
                    wait_apart(act, xt_ps, s + 2)
                    nc.scalar.copy(t["xt"][:, :, bass.ds(s * SC, SC)], psum[:, 0:2, :]).then_inc(xt_sb, 1)
                act.wait_ge(w_ps, 1)
                for hi, lo, src in gate_up_weights(t):
                    ins = nc.scalar.mul(hi, src, W_UP)
                ins.then_inc(w_hi, 1)
                act.wait_ge(w_ps, 2)
                nc.scalar.mul(t["wd"][HI][:, :, :], psum[:, 0:3, :].rearrange("p a (f n) -> p (a f) n", f=2), W_UP
                              ).then_inc(w_hi, 1)
                magic = t["magic"][:, 0:1]
                act.wait_ge(scaled, 2)
                with act.Fori(0, NS // 2, 1) as it:
                    def round_gate(i):
                        act.wait_ge(g_ps, it * NI + i + 1)
                        if i >= 2:
                            act.wait_ge(g_val, it * NI + i - 1)
                        nc.scalar.activation(t["a"][i % 2][:, :].rearrange("p (a n) -> p a n", a=2), bank_pair(i),
                                             ACT.Identity, bias=magic, scale=t["sc"][:, GATE_BY:GATE_BY + 1]
                                             ).then_inc(g_round, 1)

                    def sigmoid(i):
                        act.wait_ge(g_val, it * NI + i + 1)
                        act.wait_ge(g_prod, it * NI + i + 1)
                        nc.scalar.activation(t["c"][i % 2][:, :], t["b"][i % 2][:, :], ACT.Sigmoid).then_inc(g_sig, 1)
                        act.wait_ge(g_sig, it * NI + i + 1)
                        nc.scalar.activation(t["c"][i % 2][:, :], t["c"][i % 2][:, :], ACT.Identity,
                                             bias=magic, scale=SIG_STEPS).then_inc(g_y, 1)

                    for i in range(NI):
                        round_gate(i)
                        if i >= 1:
                            sigmoid(i - 1)
                    sigmoid(NI - 1)
                act.wait_ge(scaled, 3)
                with act.Fori(0, NS // 2, 1) as it:
                    for i in range(NI):
                        s, pr = it * 2 + i // NP, i % NP
                        wait_apart(act, u_prod, it * NI + i + 1)
                        nc.scalar.activation(t["b"][i % 2][:, :].rearrange("p (e n) -> p e n", e=2),
                                             t["p"][:, 2 * pr:2 * pr + 2, bass.ds(s * SC, SC)], ACT.Identity,
                                             bias=magic, scale=t["sc"][:, GATED_BY:GATED_BY + 1]).then_inc(p_round, 1)
                        act.wait_ge(u_ps, it * NI + i + 1)
                        nc.scalar.activation(t["a"][i % 2][:, :].rearrange("p (a n) -> p a n", a=2), bank_pair(i),
                                             ACT.Identity, bias=magic, scale=t["sc"][:, UP_BY:UP_BY + 1]
                                             ).then_inc(u_round, 1)
                act.wait_ge(scaled, 4)

                def round_output(s, pr, count, buf):
                    wait_apart(act, o_int, count + 1)
                    nc.scalar.activation(t["a"][buf][:, :].rearrange("p (e n) -> p e n", e=2),
                                         t["p"][:, 2 * pr:2 * pr + 2, bass.ds(s * SC, SC)],
                                         ACT.Identity, bias=magic, scale=t["sc"][:, OUT_BY:OUT_BY + 1]
                                         ).then_inc(o_round, 1)

                for pr in range(NP):
                    round_output(0, pr, pr, pr % 2)
                with act.Fori(0, NS // 2, 1) as it:
                    for i in range(NI):
                        round_output((it * 2 + 1 + i // NP) % NS, i % NP, it * NI + i + NP, (i + NP) % 2)

            def scales(dve, t):
                wam, wsc = (t[n_][:, :, :].rearrange("p i b -> p (i b)") for n_ in ("wam", "wsc"))
                dve.wait_ge(w_loaded, 48)
                nc.vector.tensor_reduce(wam, weight_blocks(t)[0], X, ALU.max, apply_absolute_value=True).then_inc(w_amax, 1)
                dve.wait_ge(w_amax, 1)
                nc.vector.tensor_scalar(wsc, wam, 1.0 / W_QMAX, TINY, ALU.mult, ALU.max).then_inc(w_step_done, 1)
                dve.wait_ge(w_step_done, 1)
                nc.vector.reciprocal(wam, wsc).then_inc(w_recip, 1)

            def vector(dve, t, stats):
                stats(dve)
                nc.vector.memset(t["acc"][:, :], 0.0).then_inc(acc_set, 1)
                dve.wait_ge(acc_set, 1)

                def keep_max(n, count):
                    nc.vector.tensor_tensor(t["acc"][:, 0:n], t["acc"][:, 0:n], t["am"][:, 0:n], ALU.max
                                            ).then_inc(fold, 1)
                    dve.wait_ge(fold, count)

                def whole_max(k, groups):
                    for c, lo, hi in groups:
                        ins = nc.vector.tensor_reduce(t["ar"][:, c:c + 1], t["acc"][:, lo:hi], X, ALU.max)
                    ins.then_inc(amax_part, 1)
                    dve.wait_ge(amax_all, k)
                    nc.vector.memset(t["acc"][:, :], 0.0)

                steps = [0]

                def small(ins):
                    steps[0] += 1
                    ins.then_inc(sc_step, 1)
                    dve.wait_ge(sc_step, steps[0])

                def col(i):
                    return t["sc"][:, i:i + 1]

                def whole(i):
                    return t["aa"][:, i:i + 1]

                with dve.Fori(0, NS, 1) as s:
                    dve.wait_ge(xt_ps, s + 1)
                    for j in range(TS):
                        ins = nc.vector.tensor_scalar(t["xn"][:, j, :], x_sb[:, s * TS + j, :],
                                                      mv[:, s * TS + j, 0:1], rstd[:, bass.ds(s * TS + j, 1)],
                                                      ALU.subtract, ALU.mult)
                    ins.then_inc(xn_ready, 1)
                    dve.wait_ge(xn_ready, s + 1)
                    nc.vector.tensor_reduce(t["am"][:, 0:1], t["xn"][:, :, :].rearrange("p t n -> p (t n)"), X,
                                            ALU.max, apply_absolute_value=True).then_inc(x_max, 1)
                    dve.wait_ge(x_max, s + 1)
                    keep_max(1, s + 1)
                whole_max(1, ((0, 0, 1),))
                small(nc.vector.tensor_scalar(col(X_STEP), whole(0), 1.0 / QMAX, TINY, ALU.mult, ALU.max))
                small(nc.vector.reciprocal(col(X_BY), col(X_STEP)))
                small(nc.vector.tensor_scalar(col(X_STEP), col(X_STEP), 1.0 / W_UP, None, ALU.mult))
                dve.wait_ge(xt_sb, NS + 1)
                for s in range(NS):
                    if s == 1:
                        dve.wait_ge(w_hi, 1)
                        for hi, lo, src in gate_up_weights(t):
                            ins = nc.vector.scalar_tensor_tensor(lo, src, W_UP, hi, ALU.mult, ALU.subtract)
                        ins.then_inc(w_sb_done, 1)
                    if s == 3:
                        dve.wait_ge(w_hi, 2)
                        nc.vector.scalar_tensor_tensor(t["wd"][LO][:, :, :], psum[:, 0:3, :].rearrange("p a (f n) -> p (a f) n", f=2),
                                                       W_UP, t["wd"][HI][:, :, :], ALU.mult, ALU.subtract).then_inc(w_sb_done, 1)
                    xt = t["xt"][:, :, s * SC:(s + 1) * SC]
                    hi, lo = (x[:, :, s * SC:(s + 1) * SC] for x in t["xq"])
                    nc.vector.tensor_scalar(xt, xt, col(X_BY), MAGIC, ALU.mult, ALU.add).then_inc(x_round, 1)
                    dve.wait_ge(x_round, s + 1)
                    nc.vector.tensor_scalar(hi, xt, MAGIC, None, ALU.subtract).then_inc(x_hi, 1)
                    dve.wait_ge(x_hi, s + 1)
                    nc.vector.scalar_tensor_tensor(lo, xt, MAGIC, hi, ALU.subtract, ALU.subtract).then_inc(x_quant, 1)
                dve.sem_inc(m_used, 3)
                with dve.Fori(0, NS, 1) as s:
                    for i in range(NI):
                        dve.wait_ge(m_ps, s * NI + i + 1)
                        nc.vector.tensor_reduce(t["am"][:, i:i + 1], bank_pair(i), mybir.AxisListType.XY, ALU.max,
                                                apply_absolute_value=True).then_inc(m_used, 1)
                    dve.wait_ge(m_used, s * NI + NI + 3)
                    keep_max(NI, s + NS + 1)
                whole_max(2, ((1, 0, NP), (2, NP, NI)))
                for c, step, by in ((1, GATE_STEP, GATE_BY), (2, UP_STEP, UP_BY)):
                    small(nc.vector.tensor_scalar(col(step), whole(c), col(X_STEP), 1.0 / QMAX, ALU.mult, ALU.mult))
                    small(nc.vector.tensor_scalar(col(step), col(step), TINY, None, ALU.max))
                    small(nc.vector.reciprocal(col(by), col(step)))
                    small(nc.vector.tensor_scalar(col(by), col(by), col(X_STEP), None, ALU.mult))
                dve.sem_inc(scaled, 2)
                dve.sem_inc(g_prod, 2)
                with dve.Fori(0, NS // 2, 1) as it:
                    def gate_value(i):
                        dve.wait_ge(g_round, it * NI + i + 4)
                        nc.vector.tensor_scalar(t["b"][i % 2][:, :], t["a"][i % 2][:, :], MAGIC, col(GATE_STEP),
                                                ALU.subtract, ALU.mult).then_inc(g_val, 1)

                    def gated(i):
                        s, pr = it * 2 + i // NP, i % NP
                        c = t["c"][i % 2][:, :]
                        dve.wait_ge(g_y, it * NI + i + 1)
                        nc.vector.tensor_scalar(c, c, MAGIC + SIG_STEPS - 1, MAGIC, ALU.min, ALU.subtract
                                                ).then_inc(g_clip, 1)
                        dve.wait_ge(g_clip, it * NI + i + 1)
                        dst = t["p"][:, 2 * pr:2 * pr + 2, bass.ds(s * SC, SC)]
                        nc.vector.tensor_tensor(dst, c.rearrange("p (e n) -> p e n", e=2),
                                                t["b"][i % 2][:, :].rearrange("p (e n) -> p e n", e=2), ALU.mult
                                                ).then_inc(g_prod, 1)
                        wait_apart(dve, g_prod, it * NI + i + 3)
                        nc.vector.tensor_reduce(t["am"][:, i:i + 1], dst, mybir.AxisListType.XY, ALU.max,
                                                apply_absolute_value=True).then_inc(g_max, 1)

                    for i in range(NI):
                        gate_value(i)
                        if i >= 1:
                            gated(i - 1)
                    gated(NI - 1)
                    dve.wait_ge(g_max, it * NI + NI)
                    keep_max(NI, it + 2 * NS + 1)
                whole_max(3, ((3, 0, NI),))
                small(nc.vector.tensor_scalar(col(GATED_STEP), whole(3), 1.0 / SIG_STEPS, 1.0 / QMAX, ALU.mult, ALU.mult))
                small(nc.vector.tensor_scalar(col(GATED_STEP), col(GATED_STEP), TINY, None, ALU.max))
                small(nc.vector.reciprocal(col(GATED_BY), col(GATED_STEP)))
                small(nc.vector.tensor_scalar(col(GATED_BY), col(GATED_BY), 1.0 / SIG_STEPS, None, ALU.mult))
                dve.sem_inc(scaled, 1)
                dve.sem_inc(u_prod, 2)
                with dve.Fori(0, NS // 2, 1) as it:
                    def product_up(i):
                        s, pr = it * 2 + i // NP, i % NP
                        dst = t["p"][:, 2 * pr:2 * pr + 2, bass.ds(s * SC, SC)]
                        dve.wait_ge(p_round, it * NI + i + 1)
                        wait_apart(dve, u_int, it * NI + i + 1)
                        nc.vector.scalar_tensor_tensor(dst, t["b"][i % 2][:, :].rearrange("p (e n) -> p e n", e=2), MAGIC,
                                                       t["a"][i % 2][:, :].rearrange("p (e n) -> p e n", e=2),
                                                       ALU.subtract, ALU.mult).then_inc(u_prod, 1)
                        wait_apart(dve, u_prod, it * NI + i + 3)
                        nc.vector.tensor_reduce(t["am"][:, i:i + 1], dst, mybir.AxisListType.XY, ALU.max,
                                                apply_absolute_value=True).then_inc(u_max, 1)

                    for i in range(NI):
                        product_up(i)
                    dve.wait_ge(u_max, it * NI + NI)
                    keep_max(NI, it + 2 * NS + NS // 2 + 1)
                whole_max(4, ((4, 0, NI),))
                small(nc.vector.tensor_scalar(col(PROD_STEP), col(GATED_STEP), col(UP_STEP), None, ALU.mult))
                small(nc.vector.tensor_scalar(col(OUT_STEP), whole(4), col(PROD_STEP), 1.0 / QMAX, ALU.mult, ALU.mult))
                small(nc.vector.tensor_scalar(col(OUT_STEP), col(OUT_STEP), TINY, None, ALU.max))
                small(nc.vector.reciprocal(col(OUT_BY), col(OUT_STEP)))
                small(nc.vector.tensor_scalar(col(OUT_BY), col(OUT_BY), col(PROD_STEP), None, ALU.mult))
                small(nc.vector.tensor_scalar(col(OUT_STEP), col(OUT_STEP), 1.0 / W_UP, None, ALU.mult))
                dve.sem_inc(scaled, 1)
                dve.sem_inc(d_added, 2)
                dve.sem_inc(o_int, 2)

                def output_parts(j, base, n):
                    dve.wait_ge(d_ps, n + 1)
                    for pr in range(NP):
                        a = t["a"][(j * NP + pr) % 2][:, :].rearrange("p (e n) -> p e n", e=2)
                        hi, lo = (o[:, 2 * pr:2 * pr + 2, :] for o in t["os"][j])
                        dve.wait_ge(o_round, base + pr + 1)
                        nc.vector.tensor_scalar(hi, a, MAGIC, None, ALU.subtract).then_inc(o_hi, 1)
                        dve.wait_ge(o_hi, base + pr + 1)
                        nc.vector.scalar_tensor_tensor(lo, a, MAGIC, hi, ALU.subtract, ALU.subtract).then_inc(o_int, 1)

                def add(j, n):
                    wait_apart(dve, d_ps, n + 3)
                    for e in range(2):
                        xs = x_sb[:, bass.ds(n * TS + 2 * e, 2), :]
                        o = psum[:, 2 * j + e, :].rearrange("p (m d) -> p m d", m=2)
                        ins = nc.vector.scalar_tensor_tensor(xs, o, col(OUT_STEP), xs, ALU.mult, ALU.add)
                    ins.then_inc(d_added, 1)

                output_parts(0, 0, 0)
                with dve.Fori(0, NS // 2, 1) as it:
                    output_parts(1, it * NI + NP, it * 2 + 1)
                    add(0, it * 2)
                    output_parts(0, it * NI + NI, it * 2 + 2)
                    add(1, it * 2 + 1)

            return alloc, sync, gpsimd, tensor, scalar, vector, scales

        def experts():
            NE, NX, FI = 8, 10, 352
            FTS = [(0, 128), (128, 128), (256, 96)]
            raw_loaded = [sem(f"xw_raw{i}") for i in range(2)]
            xw_ps, w_hi, w_lo, r_loaded, r_ps, r_sb = (sem("w_ps"), sem("w_hi"), sem("xw_lo"), sem("xr_loaded"),
                                                          sem("xr_ps"), sem("xr_sb"))
            xn_ready, xt_ps, xt_sb, xt_kept, l_ps, l_sb = (sem("xn_ready"), sem("xt_ps"), sem("xt_sb"), sem("xxt_kept"),
                                                          sem("xl_ps"), sem("xl_sb"))
            step, exp_done, tri_set = sem("router_step"), sem("exp_done"), sem("tri_set")
            h_hi, h_lo = sem("h_hi"), sem("h_lo")
            gu_ps, silu_done, h_done, dn_ps, x_done = sem("gu_ps"), sem("silu_done"), sem("xh_done"), sem("dn_ps"), sem("x_done")

            def alloc(stack):
                t = {"wg": [sb(f"xwg{i}", [P, NX, KT, FI], F16, stack=stack) for i in (HI, LO)],
                     "wu": [sb(f"xwu{i}", [P, NX, KT, FI], F16, stack=stack) for i in (HI, LO)],
                     "wd": [sb(f"xwd{i}", [P, NX, 3, D], F16, stack=stack) for i in (HI, LO)],
                     "xt": [sb(f"xx_t{i}", [P, KT, B * S], F16, stack=stack) for i in (HI, LO)],
                     "wts": sb("expert_weights", [P, NT, NX], stack=stack)}
                with ExitStack() as inner:
                    t["raw_g"] = [sb(f"raw_g{i}", [P, 3, D], stack=inner) for i in range(2)]
                    t["raw_u"] = [sb(f"raw_u{i}", [P, 3, D], stack=inner) for i in range(2)]
                    t["raw_d"] = [sb(f"raw_d{i}", [P, 2, FI], stack=inner) for i in range(2)]
                    t["raw_r"] = sb("raw_r", [NE + 1, D], stack=inner)
                    t["wr"] = sb("router_w", [P, KT, NE + 1], stack=inner)
                    t["xn"] = sb("xxn", [P, TS, D], stack=inner)
                    t["xs"] = sb("xxt_step", [P, KT, SC], stack=inner)
                    for name, shape in (("lg", [P, NT, NE + 1]), ("mx", [P, NT]), ("ex", [P, NT, NE]), ("sg", [P, NT]),
                                        ("sum", [P, NT]), ("gt", [P, NT, NE, NE]), ("eq", [P, NT, NE, NE]),
                                        ("rank", [P, NT, NE]), ("tri", [P, NE, NE])):
                        t[name] = sb(f"router_{name}_", shape, stack=inner)
                with ExitStack() as inner:
                    t["s"] = [sb(f"silu{i}", [P, SC], stack=inner) for i in range(3)]
                    t["h"] = [sb(f"xh{i}", [P, SC], stack=inner) for i in range(3)]
                    t["hs"] = [[sb(f"xh_{i}_{part}", [P, 3, SC], F16, stack=inner) for part in (HI, LO)]
                               for i in range(2)]
                return t

            def sources(e):
                if e < NE:
                    gu = a["L1_ffn_experts_gate_up"][e]
                    return gu[0:FI, :], gu[FI:2 * FI, :], a["L1_ffn_experts_down"][e]
                lo = (e - NE) * FI
                return (a["L1_ffn_shared_gate_w"][lo:lo + FI, :], a["L1_ffn_shared_up_w"][lo:lo + FI, :],
                        a["L1_ffn_shared_down_w"][:, lo:lo + FI])

            def sync(sp, t):
                sp.dma_start(t["raw_r"][0:NE, :], a["L1_ffn_gate_w"]).then_inc(r_loaded, 16)
                sp.dma_start(t["raw_r"][NE:NE + 1, :], a["L1_ffn_shared_expert_gate_w"]).then_inc(r_loaded, 16)
                for e in range(NX):
                    if e >= 2:
                        sp.wait_ge(xw_ps, e - 1)
                    g, u, d = sources(e)
                    for raw, w in ((t["raw_g"], g), (t["raw_u"], u)):
                        sp.dma_start(raw[e % 2][:, 0:2, :], w[0:2 * P, :].rearrange("(t p) n -> p t n", p=P)
                                     ).then_inc(raw_loaded[e % 2], 16)
                        sp.dma_start(raw[e % 2][0:FI - 2 * P, 2, :], w[2 * P:FI, :]).then_inc(raw_loaded[e % 2], 16)
                    sp.dma_start(t["raw_d"][e % 2][:, :, :], d.rearrange("(t p) f -> p t f", p=P)
                                 ).then_inc(raw_loaded[e % 2], 16)
                out_t = tokens(out)
                with sp.Fori(0, NS, 1) as s:
                    sp.wait_ge(x_done, (s + 1) * NX + 1)
                    sp.dma_start(out_t[:, bass.ds(s * TS, TS), :], x_sb[:, bass.ds(s * TS, TS), :]).then_inc(out_stored, 16)
                sp.wait_ge(out_stored, 16 * NS)

            def gpsimd(pool, t):
                nc.gpsimd.memset(t["tri"][:, :, :], 1.0).then_inc(tri_set, 1)
                pool.wait_ge(tri_set, 1)
                nc.gpsimd.affine_select(out=t["tri"][:, :, :], in_=t["tri"][:, :, :], compare_op=ALU.is_ge, fill=0.0,
                                        base=-1, pattern=[[1, NE], [-1, NE]], channel_multiplier=0).then_inc(tri_set, 1)
                pool.sem_inc(h_lo, 3)
                with pool.Fori(0, NS, 1) as s:
                    for m in range(3 * NX):
                        e, f = m // 3, m % 3
                        n = FTS[f][1]
                        hs = t["hs"][e % 2]
                        pool.wait_ge(h_hi, s * 3 * NX + m + 1)
                        nc.gpsimd.tensor_tensor(hs[LO][0:n, f, :], t["h"][m % 3][0:n, :], hs[HI][0:n, f, :],
                                                ALU.subtract).then_inc(h_lo, 1)

            def down_weights(f, ot):
                if f < 2:
                    return psum[:, 4, f * D + ot * P:f * D + (ot + 1) * P]
                return psum[:, ot, FI:FI + P]

            def tensor(pe, t):
                pe.wait_ge(r_loaded, 32)
                for kt in range(KT):
                    ins = nc.tensor.transpose(psum[:, 7, kt * 16:kt * 16 + NE + 1], t["raw_r"][:, kt * P:(kt + 1) * P],
                                              ident[0:NE + 1, 0:NE + 1])
                ins.then_inc(r_ps, 1)
                for e in range(NX):
                    pe.wait_ge(raw_loaded[e % 2], 80 * (e // 2 + 1))
                    if e >= 1:
                        pe.wait_ge(w_lo, e)
                    for b0, raw in ((0, t["raw_g"]), (2, t["raw_u"])):
                        for kt in range(KT):
                            for f, (lo, n) in enumerate(FTS):
                                nc.tensor.transpose(psum[:, b0 + kt, lo:lo + n], raw[e % 2][0:n, f, kt * P:(kt + 1) * P],
                                                    ident[0:n, 0:n])
                    for f, (lo, n) in enumerate(FTS):
                        for ot in range(2):
                            ins = nc.tensor.transpose(down_weights(f, ot)[0:n], t["raw_d"][e % 2][:, ot, lo:lo + n],
                                                      ident[:, :])
                    ins.then_inc(xw_ps, 1)
                    if 1 <= e <= NS:
                        pe.wait_ge(xt_sb, e)
                        if e >= 2:
                            pe.wait_ge(l_sb, e - 1)
                        for j in range(TS):
                            for kt in range(KT):
                                ins = nc.tensor.matmul(psum[:, 5, j * 16:j * 16 + NE + 1], t["xs"][:, kt, j * P:(j + 1) * P],
                                                       t["wr"][:, kt, :], start=(kt == 0), stop=(kt == KT - 1))
                        ins.then_inc(l_ps, 1)
                    if e < NS:
                        pe.wait_ge(xn_ready, e + 1)
                        if e == 0:
                            pe.wait_ge(r_sb, 1)
                        if e >= 1:
                            pe.wait_ge(xt_kept, e)
                        for kt in range(KT):
                            for j in range(TS):
                                ins = nc.tensor.transpose(psum[:, 6 + kt, j * P:(j + 1) * P],
                                                          t["xn"][:, j, kt * P:(kt + 1) * P], ident[:, :])
                        ins.then_inc(xt_ps, 1)
                pe.wait_ge(w_lo, NX)
                pe.wait_ge(l_sb, NS)
                pe.wait_ge(xt_kept, NS)
                pe.sem_inc(dn_ps, 2)
                with pe.Fori(0, NS, 1) as s:
                    def gate_up(e):
                        for f, (lo, n) in enumerate(FTS):
                            m = e * 3 + f
                            pe.wait_ge(h_done, s * 3 * NX + m + 1)
                            for i, w in enumerate((t["wg"], t["wu"])):
                                for kt in range(KT):
                                    for k, (pw, px) in enumerate(SPLIT):
                                        ins = nc.tensor.matmul(psum[0:n, 2 * (m % 3) + i, :], w[pw][:, e, kt, lo:lo + n],
                                                               t["xt"][px][:, kt, bass.ds(s * SC, SC)],
                                                               start=(kt == 0 and k == 0), stop=(kt == KT - 1 and k == 2))
                            ins.then_inc(gu_ps, 1)

                    def down(e):
                        pe.wait_ge(h_lo, s * 3 * NX + e * 3 + 3 + 3)
                        pe.wait_ge(x_done, s * NX + e + 1)
                        for j in range(TS):
                            for f, (lo, n) in enumerate(FTS):
                                for k, (ph, pw) in enumerate(SPLIT):
                                    ins = nc.tensor.matmul(psum[:, 6 + j // 2, (j % 2) * D:(j % 2 + 1) * D],
                                                           t["hs"][e % 2][ph][0:n, f, j * P:(j + 1) * P],
                                                           t["wd"][pw][0:n, e, f, :],
                                                           start=(f == 0 and k == 0), stop=(f == 2 and k == 2))
                        ins.then_inc(dn_ps, 1)

                    for e in range(NX):
                        gate_up(e)
                        if e >= 1:
                            down(e - 1)
                    down(NX - 1)

            def scalar(act, t):
                for e in range(NX):
                    act.wait_ge(xw_ps, e + 1)
                    nc.scalar.mul(t["wd"][HI][:, e, 0:2, :].rearrange("p f n -> p (f n)"), psum[:, 4, :], W_UP)
                    n = FI - 2 * P
                    nc.scalar.mul(t["wd"][HI][0:n, e, 2, :].rearrange("p (o m) -> p o m", o=2), psum[0:n, 0:2, FI:FI + P],
                                  W_UP)
                    nc.scalar.mul(t["wg"][HI][:, e, :, :], psum[:, 0:2, 0:FI], W_UP)
                    nc.scalar.mul(t["wu"][HI][:, e, :, :], psum[:, 2:4, 0:FI], W_UP).then_inc(w_hi, 1)
                    if e < NS:
                        act.wait_ge(xt_ps, e + 1)
                        if e >= 1:
                            act.wait_ge(xt_kept, e)
                        nc.scalar.copy(t["xs"][:, :, :], psum[:, 6:8, :])
                        nc.scalar.copy(t["xt"][HI][:, :, e * SC:(e + 1) * SC], psum[:, 6:8, :]).then_inc(xt_sb, 1)
                act.wait_ge(step, 2)
                nc.scalar.activation(t["ex"][:, :, :], t["ex"][:, :, :], ACT.Exp)
                nc.scalar.activation(t["sg"][:, :], t["lg"][:, :, NE], ACT.Exp, scale=-1.0).then_inc(exp_done, 1)

                def high_part(s, m):
                    e, f = m // 3, m % 3
                    n = FTS[f][1]
                    act.wait_ge(h_done, s * 3 * NX + m + 4)
                    if f == 0:
                        act.wait_ge(dn_ps, s * NX + e + 1)
                    nc.scalar.copy(t["hs"][e % 2][HI][0:n, f, :], t["h"][m % 3][0:n, :]).then_inc(h_hi, 1)

                with act.Fori(0, NS, 1) as s:
                    for m in range(3 * NX):
                        n = FTS[m % 3][1]
                        act.wait_ge(gu_ps, s * 3 * NX + m + 1)
                        act.wait_ge(h_done, s * 3 * NX + m + 1)
                        nc.scalar.activation(t["s"][m % 3][0:n, :], psum[0:n, 2 * (m % 3), :], ACT.Silu,
                                             scale=1.0 / W_UP).then_inc(silu_done, 1)
                        if m >= 1:
                            high_part(s, m - 1)
                    high_part(s, 3 * NX - 1)

            def vector(dve, t):
                dve.wait_ge(r_ps, 1)
                nc.vector.tensor_copy(t["wr"][:, :, :], psum[:, 7, 0:32].rearrange("p (k n) -> p k n", k=2)[:, :, 0:NE + 1]
                                      ).then_inc(r_sb, 1)

                def norm(s):
                    for j in range(TS):
                        ins = nc.vector.tensor_scalar(t["xn"][:, j, :], x_sb[:, s * TS + j, :],
                                                      mv[:, s * TS + j, 0:1], rstd[:, s * TS + j:s * TS + j + 1],
                                                      ALU.subtract, ALU.mult)
                    ins.then_inc(xn_ready, 1)

                norm(0)
                for e in range(NX):
                    dve.wait_ge(w_hi, e + 1)
                    n = FI - 2 * P
                    for dst, part, src in (
                            (t["wd"][LO][:, e, 0:2, :].rearrange("p f n -> p (f n)"),
                             t["wd"][HI][:, e, 0:2, :].rearrange("p f n -> p (f n)"), psum[:, 4, :]),
                            (t["wd"][LO][0:n, e, 2, :].rearrange("p (o m) -> p o m", o=2),
                             t["wd"][HI][0:n, e, 2, :].rearrange("p (o m) -> p o m", o=2), psum[0:n, 0:2, FI:FI + P]),
                            (t["wg"][LO][:, e, :, :], t["wg"][HI][:, e, :, :], psum[:, 0:2, 0:FI]),
                            (t["wu"][LO][:, e, :, :], t["wu"][HI][:, e, :, :], psum[:, 2:4, 0:FI])):
                        ins = nc.vector.scalar_tensor_tensor(dst, src, W_UP, part, ALU.mult, ALU.subtract)
                    ins.then_inc(w_lo, 1)
                    if 1 <= e <= NS:
                        dve.wait_ge(l_ps, e)
                        nc.vector.tensor_copy(t["lg"][:, (e - 1) * TS:e * TS, :],
                                              psum[:, 5, 0:64].rearrange("p (j n) -> p j n", j=TS)[:, :, 0:NE + 1]
                                              ).then_inc(l_sb, 1)
                    if e < NS:
                        dve.wait_ge(xt_sb, e + 1)
                        nc.vector.tensor_tensor(t["xt"][LO][:, :, e * SC:(e + 1) * SC], t["xs"][:, :, :],
                                                t["xt"][HI][:, :, e * SC:(e + 1) * SC], ALU.subtract
                                                ).then_inc(xt_kept, 1)
                    if e + 1 < NS:
                        norm(e + 1)
                dve.wait_ge(l_sb, NS)
                lg = t["lg"][:, :, 0:NE]
                steps = [0]

                def small(ins):
                    steps[0] += 1
                    ins.then_inc(step, 1)
                    dve.wait_ge(step, steps[0])

                small(nc.vector.tensor_reduce(t["mx"][:, :], lg, X, ALU.max))
                small(nc.vector.tensor_tensor(t["ex"][:, :, :], lg, t["mx"][:, :].unsqueeze(2).broadcast_to((P, NT, NE)),
                                              ALU.subtract))
                dve.wait_ge(exp_done, 1)
                small(nc.vector.tensor_reduce(t["sum"][:, :], t["ex"][:, :, :], X, ALU.add))
                small(nc.vector.reciprocal(t["mx"][:, :], t["sum"][:, :]))
                small(nc.vector.tensor_tensor(t["ex"][:, :, :], t["ex"][:, :, :],
                                              t["mx"][:, :].unsqueeze(2).broadcast_to((P, NT, NE)), ALU.mult))
                pair = (P, NT, NE, NE)
                of_j = t["ex"][:, :, :].unsqueeze(2).broadcast_to(pair)
                of_i = t["ex"][:, :, :].unsqueeze(3).broadcast_to(pair)
                small(nc.vector.tensor_tensor(t["gt"][:, :, :, :], of_j, of_i, ALU.is_gt))
                small(nc.vector.tensor_tensor(t["eq"][:, :, :, :], of_j, of_i, ALU.is_equal))
                dve.wait_ge(tri_set, 2)
                eq = t["eq"][:, :, :, :].rearrange("p t i j -> p t (i j)")
                small(nc.vector.tensor_tensor(eq, eq, t["tri"][:, :, :].rearrange("p i j -> p (i j)").unsqueeze(1)
                                              .broadcast_to((P, NT, NE * NE)), ALU.mult))
                small(nc.vector.tensor_tensor(t["gt"][:, :, :, :], t["gt"][:, :, :, :], t["eq"][:, :, :, :], ALU.add))
                small(nc.vector.tensor_reduce(t["rank"][:, :, :], t["gt"][:, :, :, :], X, ALU.add))
                small(nc.vector.tensor_scalar(t["rank"][:, :, :], t["rank"][:, :, :], 1.5, None, ALU.is_lt))
                small(nc.vector.tensor_tensor(t["wts"][:, :, 0:NE], t["ex"][:, :, :], t["rank"][:, :, :], ALU.mult))
                small(nc.vector.tensor_scalar(t["sum"][:, :], t["sg"][:, :], 1.0, None, ALU.add))
                small(nc.vector.reciprocal(t["mx"][:, :], t["sum"][:, :]))
                small(nc.vector.tensor_copy(t["wts"][:, :, NE:NX], t["mx"][:, :].unsqueeze(2).broadcast_to((P, NT, 2))))
                small(nc.vector.tensor_scalar(t["wts"][:, :, :], t["wts"][:, :, :], 1.0 / W_UP, None, ALU.mult))
                dve.sem_inc(h_done, 3)
                dve.sem_inc(x_done, 1)
                with dve.Fori(0, NS, 1) as s:
                    def gated(e):
                        for f, (lo, n) in enumerate(FTS):
                            m = e * 3 + f
                            dve.wait_ge(silu_done, s * 3 * NX + m + 1)
                            dve.wait_ge(h_lo, s * 3 * NX + m + 1)
                            nc.vector.scalar_tensor_tensor(t["h"][m % 3][0:n, :], psum[0:n, 2 * (m % 3) + 1, :],
                                                           1.0 / W_UP, t["s"][m % 3][0:n, :], ALU.mult, ALU.mult
                                                           ).then_inc(h_done, 1)

                    def add(e):
                        wait_apart(dve, dn_ps, s * NX + e + 3)
                        for j in range(TS):
                            xs = x_sb[:, s * TS + j, :]
                            ins = nc.vector.scalar_tensor_tensor(xs, psum[:, 6 + j // 2, (j % 2) * D:(j % 2 + 1) * D],
                                                                 t["wts"][:, s * TS + j, e:e + 1], xs, ALU.mult, ALU.add)
                        ins.then_inc(x_done, 1)

                    for e in range(NX):
                        gated(e)
                        if e >= 1:
                            add(e - 1)
                    add(NX - 1)

            return alloc, sync, gpsimd, tensor, scalar, vector

        stats0_v, stats0_s = norm_stats(0)
        proj0 = projections(0, a["L0_xattn_Wq"], a["L0_xattn_Wk"], a["L0_xattn_Wv"],
                            a["L0_xattn_bq"], a["L0_xattn_bk"], a["L0_xattn_bv"])
        rel_alloc, rel_alloc_raw, rel_sync, rel_pool, rel_pe, rel_dve, rel_ready = relative_tables()
        with ExitStack() as rel_stack:
            rel_t = rel_alloc(rel_stack)
            with ExitStack() as stack:
                rel_alloc_raw(stack, rel_t)
                proj0_t = proj0[0](stack)
            att0 = attention(0, True, rel_t, rel_ready)
            with ExitStack() as stack:
                att0_t = att0[0](stack)
        fc0 = merge_heads(0, a["L0_xattn_W_fc"], (h_dr, r_dr), a["L0_xattn_b_fc"])
        with ExitStack() as stack:
            fc0_t = fc0[0](stack)
        stats1_v, stats1_s = norm_stats(1)
        ffn0 = quantised_ffn()
        with ExitStack() as stack:
            ffn0_t = ffn0[0](stack)
        stats2_v, stats2_s = norm_stats(2)
        proj1 = projections(1, a["L1_xattn_Wq"], a["L1_xattn_Wk"], a["L1_xattn_Wv"])
        with ExitStack() as stack:
            proj1_t = proj1[0](stack)
        att1 = attention(1, False, w_out_ap=a["L1_xattn_Wout"])
        with ExitStack() as stack:
            att1_t = att1[0](stack)
        stats3_v, stats3_s = norm_stats(3)
        moe = experts()
        with ExitStack() as stack:
            moe_t = moe[0](stack)

        kept = {"fw_loaded", "fw_recip", "phase_end", "phase_begun", "out_stored", "x_loaded", "consts_set"}

        def clear(pool):
            for name, used in semaphores.items():
                if name not in kept:
                    pool.sem_clear(used)

        blk = ctx.enter_context(nc.Block())

        @blk.sync
        def _(sp):
            x_t = tokens(a["x"])
            for i in range(4):
                sp.dma_start(x_sb[:, i * 8:(i + 1) * 8, :], x_t[:, i * 8:(i + 1) * 8, :]).then_inc(x_loaded, 16)
            proj0[5](sp, proj0_t)
            rel_sync(sp, rel_t)
            proj0[1](sp, proj0_t)
            phase_barrier(sp, 0)
            att0[1](sp, att0_t)
            phase_barrier(sp, 1)
            fc0[1](sp, fc0_t)
            ffn0[1](sp, ffn0_t)
            phase_barrier(sp, 2)
            phase_barrier(sp, 3)
            phase_barrier(sp, 4)
            phase_barrier(sp, 5)
            proj1[5](sp, proj1_t)
            proj1[1](sp, proj1_t)
            phase_barrier(sp, 6)
            att1[1](sp, att1_t)
            phase_barrier(sp, 7)
            phase_barrier(sp, 8)
            moe[1](sp, moe_t)

        @blk.gpsimd
        def _(pool):
            nc.gpsimd.memset(ident[:, :], 0.0)
            nc.gpsimd.memset(block[:, :], 1.0)
            nc.gpsimd.memset(block_rev[:, :], 1.0)
            nc.gpsimd.memset(eps[:, :], EPS).then_inc(consts_set, 1)
            pool.wait_ge(consts_set, 1)
            nc.gpsimd.affine_select(out=ident[:, :], in_=ident[:, :], compare_op=ALU.not_equal, fill=1.0, base=0,
                                    pattern=[[-1, P]], channel_multiplier=1)
            nc.gpsimd.affine_select(out=block[:, :], in_=block[:, :], compare_op=ALU.is_ge, fill=0.0, base=0,
                                    pattern=[[-16, 8]], channel_multiplier=1)
            nc.gpsimd.affine_select(out=block_rev[:, :], in_=block_rev[:, :], compare_op=ALU.is_ge, fill=0.0,
                                    base=-112, pattern=[[16, 8]], channel_multiplier=1).then_inc(consts_set, 1)
            pool.wait_ge(consts_set, 2)
            nc.gpsimd.affine_select(out=block[:, :], in_=block[:, :], compare_op=ALU.is_ge, fill=0.0, base=15,
                                    pattern=[[16, 8]], channel_multiplier=-1)
            nc.gpsimd.affine_select(out=block_rev[:, :], in_=block_rev[:, :], compare_op=ALU.is_ge, fill=0.0,
                                    base=127, pattern=[[-16, 8]], channel_multiplier=-1).then_inc(consts_set, 1)
            rel_pool(pool, rel_t)
            phase_barrier(pool, 0)
            att0[2](pool, att0_t)
            phase_barrier(pool, 1)
            fc0[2](pool, fc0_t)
            phase_barrier(pool, 2)
            clear(pool)
            phase_barrier(pool, 3)
            ffn0[2](pool, ffn0_t)
            phase_barrier(pool, 4)
            clear(pool)
            phase_barrier(pool, 5)
            phase_barrier(pool, 6)
            att1[2](pool, att1_t)
            phase_barrier(pool, 7)
            clear(pool)
            phase_barrier(pool, 8)
            moe[2](pool, moe_t)

        @blk.scalar
        def _(act):
            act.wait_ge(consts_set, 3)
            stats0_s(act)
            proj0[3](act, proj0_t)
            phase_barrier(act, 0)
            att0[4](act, att0_t)
            phase_barrier(act, 1)
            fc0[4](act, fc0_t)
            phase_barrier(act, 2)
            phase_barrier(act, 3)
            stats1_s(act)
            ffn0[4](act, ffn0_t)
            phase_barrier(act, 4)
            phase_barrier(act, 5)
            stats2_s(act)
            proj1[3](act, proj1_t)
            phase_barrier(act, 6)
            att1[4](act, att1_t)
            phase_barrier(act, 7)
            phase_barrier(act, 8)
            stats3_s(act)
            moe[4](act, moe_t)

        @blk.vector
        def _(dve):
            dve.wait_ge(x_loaded, 64)
            dve.wait_ge(consts_set, 3)
            rel_dve(dve, rel_t)
            stats0_v(dve)
            proj0[4](dve, proj0_t)
            phase_barrier(dve, 0)
            att0[5](dve, att0_t)
            phase_barrier(dve, 1)
            fc0[5](dve, fc0_t)
            ffn0[6](dve, ffn0_t)
            phase_barrier(dve, 2)
            phase_barrier(dve, 3)
            ffn0[5](dve, ffn0_t, stats1_v)
            phase_barrier(dve, 4)
            phase_barrier(dve, 5)
            stats2_v(dve)
            proj1[4](dve, proj1_t)
            phase_barrier(dve, 6)
            att1[5](dve, att1_t)
            phase_barrier(dve, 7)
            phase_barrier(dve, 8)
            stats3_v(dve)
            moe[5](dve, moe_t)

        @blk.tensor
        def _(pe):
            pe.wait_ge(consts_set, 3)
            rel_pe(pe, rel_t)
            proj0[2](pe, proj0_t)
            phase_barrier(pe, 0)
            att0[3](pe, att0_t)
            phase_barrier(pe, 1)
            fc0[3](pe, fc0_t)
            phase_barrier(pe, 2)
            phase_barrier(pe, 3)
            ffn0[3](pe, ffn0_t)
            phase_barrier(pe, 4)
            phase_barrier(pe, 5)
            proj1[2](pe, proj1_t)
            phase_barrier(pe, 6)
            att1[3](pe, att1_t)
            phase_barrier(pe, 7)
            phase_barrier(pe, 8)
            moe[3](pe, moe_t)


_INS = ['x', 'ctx_1024', 'mask_SxS2_ik1', 'L0_xattn_Wq', 'L0_xattn_bq', 'L0_xattn_Wk', 'L0_xattn_bk', 'L0_xattn_Wv',
        'L0_xattn_bv', 'L0_xattn_pos_k', 'L0_xattn_pos_v', 'L0_xattn_W_fc', 'L0_xattn_b_fc', 'L0_ffn_w_gate',
        'L0_ffn_w_up', 'L0_ffn_w_down', 'L1_xattn_Wv', 'L1_xattn_Wk', 'L1_xattn_Wq', 'L1_xattn_Wout',
        'L1_ffn_gate_w', 'L1_ffn_experts_gate_up', 'L1_ffn_experts_down', 'L1_ffn_shared_gate_w',
        'L1_ffn_shared_up_w', 'L1_ffn_shared_down_w', 'L1_ffn_shared_expert_gate_w']


def kernel(**inputs):
    import numpy as _np
    import concourse.bacc as _bacc
    from concourse import mybir as _mybir
    from concourse.bass_utils import run_bass_kernel_spmd as _run

    nc = _bacc.Bacc("TRN2", target_bir_lowering=False, num_devices=1)
    arrays, aps = {}, {}
    for name in _INS:
        arr = _np.ascontiguousarray(inputs[name])
        arrays[f"in_{name}"] = arr
        aps[name] = nc.dram_tensor(f"in_{name}", arr.shape, _mybir.dt.from_np(arr.dtype), kind="ExternalInput").ap()
    out = nc.dram_tensor("out_0", (16, 256, 256), _mybir.dt.float32, kind="ExternalOutput").ap()
    build(nc, aps, out)
    r = _run(nc, [arrays], core_ids=[0])
    return r.results[0]["out_0"]
```
